# Optimizing a Trainium2 kernel written in Bass

```python
import numpy as np
import jax
import jax.numpy as jnp

def _softmax(x, axis=-1):
    return jax.nn.softmax(x, axis=axis)

def _gelu(x):
    return jax.nn.gelu(x, approximate=True)

def _silu(x):
    return jax.nn.silu(x)

def _sigmoid(x):
    return jax.nn.sigmoid(x)

def _layernorm(x, axis=-1, eps=1e-05):
    m = jnp.mean(x, axis=axis, keepdims=True)
    v = jnp.var(x, axis=axis, keepdims=True)
    return (x - m) / jnp.sqrt(v + eps)

def _scatter_add(tgt, idx, src, axis=0):
    return tgt.at[idx].add(src)

def _segment_sum(src, seg, n):
    return jax.ops.segment_sum(src, seg, n)
kernel_name = 'mk_xattn_ffn_d2_seqx_r4_9f22f0'

def setup_inputs(seed: int=0):
    np.random.seed(seed)
    _w = jnp.asarray

    def _rec_inputs():
        import jax
        import jax.numpy as jnp
        _rk = jax.random.key(seed)
        x = 7.22e-05 + 1 * jax.random.normal(jax.random.fold_in(_rk, 1), (8, 512, 256), jnp.float32)
        _lenS = 512 - jax.random.randint(jax.random.fold_in(_rk, 7), (8,), 0, max(1, 512 // 4) + 1, jnp.int32)
        _lenS2 = 512 - jax.random.randint(jax.random.fold_in(_rk, 8), (8,), 0, max(1, 512 // 4) + 1, jnp.int32)
        _ctx_1024P = jax.random.normal(jax.random.fold_in(_rk, 11), (8, 16, 256), jnp.float32)
        _ctx_1024c = jax.random.dirichlet(jax.random.fold_in(_rk, 511), 0.3 * jnp.ones((16,), jnp.float32), (8, 512))
        _ctx_1024t = jnp.einsum('bsk,bkd->bsd', _ctx_1024c, _ctx_1024P)
        _ctx_1024t = _ctx_1024t * jax.lax.rsqrt(jnp.mean(jnp.square(_ctx_1024t)) + 1e-12) * 0.953939
        ctx_1024 = 4.13588e-05 + 0.999923 * (_ctx_1024t + 0.3 * jax.random.normal(jax.random.fold_in(_rk, 611), (8, 512, 256), jnp.float32))
        _validS = jnp.arange(512)[None, :] < _lenS[:, None]
        _validS2 = jnp.arange(512)[None, :] < _lenS2[:, None]
        _causal = jnp.tril(jnp.ones((512, 512), dtype=bool))
        mask_BxS2_bf1 = jnp.ones((8, 512), dtype=bool)
        return (x, ctx_1024, mask_BxS2_bf1)
    x, ctx_1024, mask_BxS2_bf1 = _rec_inputs()

    def _L0_xattn_setup():
        import jax, jax.numpy as jnp
        import numpy as np
        D_MODEL = 256
        N_HEADS = 16
        HEAD_DIM = D_MODEL // N_HEADS
        key = jax.random.key(seed)
        ks = jax.random.split(key, 11)
        B, Q, K = (4, 512, 512)
        s = 1.0 / np.sqrt(D_MODEL)
        inp = {'q': jax.random.normal(ks[0], (B, Q, D_MODEL), jnp.float32), 'k': jax.random.normal(ks[1], (B, K, D_MODEL), jnp.float32), 'v': jax.random.normal(ks[2], (B, K, D_MODEL), jnp.float32), 'kv_mask': jnp.ones((B, K), dtype=bool), 'Wq': jax.random.normal(ks[3], (D_MODEL, D_MODEL), jnp.float32) * s, 'bq': jnp.zeros((D_MODEL,), jnp.float32), 'Wk': jax.random.normal(ks[4], (D_MODEL, D_MODEL), jnp.float32) * s, 'bk': jnp.zeros((D_MODEL,), jnp.float32), 'Wv': jax.random.normal(ks[5], (D_MODEL, D_MODEL), jnp.float32) * s, 'bv': jnp.zeros((D_MODEL,), jnp.float32), 'Wo': jax.random.normal(ks[6], (D_MODEL, D_MODEL), jnp.float32) * s, 'bo': jnp.zeros((D_MODEL,), jnp.float32)}
        return inp
    _L0_xattn_all = _L0_xattn_setup()
    _L0_xattn_in = {k: v for k, v in _L0_xattn_all.items() if k in ('Wq', 'bq', 'Wk', 'bk', 'Wv', 'bv', 'Wo', 'bo')}
    del _L0_xattn_all

    def _L0_ffn_setup():
        import jax, jax.numpy as jnp
        import numpy as np
        B, S, H = (8, 1024, 256)
        NAV = 128
        E = 8
        F = 2 * H
        key = jax.random.key(seed)
        ks = jax.random.split(key, 12)

        def w(k, shape, fan_in):
            return jax.random.normal(k, shape, dtype=jnp.float32) / np.sqrt(fan_in)
        return {'hidden_states': jax.random.normal(ks[0], (B, S, H), dtype=jnp.float32), 'Wp1': w(ks[1], (H, NAV), H), 'bp1': jnp.zeros((NAV,), jnp.float32), 'Wp2': w(ks[2], (NAV, E), NAV), 'bp2': jnp.zeros((E,), jnp.float32), 'W1': w(ks[3], (E, H, F), H), 'b1': jnp.zeros((E, F), jnp.float32), 'W2': w(ks[4], (E, F, H), F), 'b2': jnp.zeros((E, H), jnp.float32), 'Wo': w(ks[5], (H, H), H), 'bo': jnp.zeros((H,), jnp.float32)}
    _L0_ffn_all = _L0_ffn_setup()
    _L0_ffn_in = {k: v for k, v in _L0_ffn_all.items() if k in ('Wp1', 'bp1', 'Wp2', 'bp2', 'W1', 'b1', 'W2', 'b2', 'Wo', 'bo')}
    del _L0_ffn_all

    def _L1_xattn_setup():
        import jax, jax.numpy as jnp
        import numpy as np
        NUM_HEADS = 16
        EPS = 1e-05

        def _layernorm(x, gamma, beta):
            mu = jnp.mean(x, axis=-1, keepdims=True)
            var = jnp.var(x, axis=-1, keepdims=True)
            return (x - mu) * jax.lax.rsqrt(var + EPS) * gamma + beta
        key = jax.random.key(seed)
        ks = jax.random.split(key, 10)
        B, L, C = (1, 1024, 256)
        D = C // NUM_HEADS
        s = 0.02
        return {'q': jax.random.normal(ks[0], (B, L, C), dtype=jnp.float32), 'k': jax.random.normal(ks[1], (B, L, C), dtype=jnp.float32), 'v': jax.random.normal(ks[2], (B, L, C), dtype=jnp.float32), 'Wq': jax.random.normal(ks[3], (C, C), dtype=jnp.float32) * s, 'Wk': jax.random.normal(ks[4], (C, C), dtype=jnp.float32) * s, 'Wv': jax.random.normal(ks[5], (C, C), dtype=jnp.float32) * s, 'gq': jnp.ones((D,), jnp.float32), 'bq': jnp.zeros((D,), jnp.float32), 'gk': jnp.ones((D,), jnp.float32), 'bk': jnp.zeros((D,), jnp.float32), 'Wp': jax.random.normal(ks[6], (C, C), dtype=jnp.float32) * s, 'bp': jnp.zeros((C,), jnp.float32)}
    _L1_xattn_all = _L1_xattn_setup()
    _L1_xattn_in = {k: v for k, v in _L1_xattn_all.items() if k in ('Wq', 'Wk', 'Wv', 'gq', 'bq', 'gk', 'bk', 'Wp', 'bp')}
    del _L1_xattn_all

    def _L1_ffn_setup():
        import math
        import jax, jax.numpy as jnp
        import numpy as np
        E = 8
        TOPK = 2
        CF = 1.25
        EPS = 1e-05
        NEG = -1e+30

        def _layer_norm(x, gamma, beta):
            mu = jnp.mean(x, axis=-1, keepdims=True)
            var = jnp.mean((x - mu) ** 2, axis=-1, keepdims=True)
            return (x - mu) * jax.lax.rsqrt(var + EPS) * gamma + beta
        key = jax.random.key(seed)
        ks = jax.random.split(key, 8)
        B, S, H, F = (4, 512, 256, 1024)
        hidden_states = jax.random.normal(ks[0], (B, S, H), jnp.float32)
        token_mask = jnp.ones((B, S), jnp.int32)
        Wr = jax.random.normal(ks[1], (H, E), jnp.float32) * 0.001
        br = jnp.zeros((E,), jnp.float32)
        W1 = jax.random.normal(ks[2], (E, H, F), jnp.float32) * (1.0 / np.sqrt(H))
        b1 = jax.random.normal(ks[3], (E, F), jnp.float32) * 0.01
        W2 = jax.random.normal(ks[4], (E, F, H), jnp.float32) * (1.0 / np.sqrt(F))
        b2 = jax.random.normal(ks[5], (E, H), jnp.float32) * 0.01
        gamma = jnp.ones((H,), jnp.float32)
        beta = jnp.zeros((H,), jnp.float32)
        return {'hidden_states': hidden_states, 'Wr': Wr, 'br': br, 'W1': W1, 'b1': b1, 'W2': W2, 'b2': b2, 'gamma': gamma, 'beta': beta, 'token_mask': token_mask}
    _L1_ffn_all = _L1_ffn_setup()
    _L1_ffn_in = {k: v for k, v in _L1_ffn_all.items() if k in ('Wr', 'br', 'W1', 'b1', 'W2', 'b2', 'gamma', 'beta', 'token_mask')}
    del _L1_ffn_all
    return {'x': x, 'ctx_1024': ctx_1024, 'mask_BxS2_bf1': mask_BxS2_bf1, 'L0_xattn_Wq': _L0_xattn_in['Wq'], 'L0_xattn_bq': _L0_xattn_in['bq'], 'L0_xattn_Wk': _L0_xattn_in['Wk'], 'L0_xattn_bk': _L0_xattn_in['bk'], 'L0_xattn_Wv': _L0_xattn_in['Wv'], 'L0_xattn_bv': _L0_xattn_in['bv'], 'L0_xattn_Wo': _L0_xattn_in['Wo'], 'L0_xattn_bo': _L0_xattn_in['bo'], 'L0_ffn_Wp1': _L0_ffn_in['Wp1'], 'L0_ffn_bp1': _L0_ffn_in['bp1'], 'L0_ffn_Wp2': _L0_ffn_in['Wp2'], 'L0_ffn_bp2': _L0_ffn_in['bp2'], 'L0_ffn_W1': _L0_ffn_in['W1'], 'L0_ffn_b1': _L0_ffn_in['b1'], 'L0_ffn_W2': _L0_ffn_in['W2'], 'L0_ffn_b2': _L0_ffn_in['b2'], 'L0_ffn_Wo': _L0_ffn_in['Wo'], 'L0_ffn_bo': _L0_ffn_in['bo'], 'L1_xattn_Wq': _L1_xattn_in['Wq'], 'L1_xattn_Wk': _L1_xattn_in['Wk'], 'L1_xattn_Wv': _L1_xattn_in['Wv'], 'L1_xattn_gq': _L1_xattn_in['gq'], 'L1_xattn_bq': _L1_xattn_in['bq'], 'L1_xattn_gk': _L1_xattn_in['gk'], 'L1_xattn_bk': _L1_xattn_in['bk'], 'L1_xattn_Wp': _L1_xattn_in['Wp'], 'L1_xattn_bp': _L1_xattn_in['bp'], 'L1_ffn_Wr': _L1_ffn_in['Wr'], 'L1_ffn_br': _L1_ffn_in['br'], 'L1_ffn_W1': _L1_ffn_in['W1'], 'L1_ffn_b1': _L1_ffn_in['b1'], 'L1_ffn_W2': _L1_ffn_in['W2'], 'L1_ffn_b2': _L1_ffn_in['b2'], 'L1_ffn_gamma': _L1_ffn_in['gamma'], 'L1_ffn_beta': _L1_ffn_in['beta'], 'L1_ffn_token_mask': _L1_ffn_in['token_mask']}

def reference(x, ctx_1024, mask_BxS2_bf1, L0_xattn_Wq, L0_xattn_bq, L0_xattn_Wk, L0_xattn_bk, L0_xattn_Wv, L0_xattn_bv, L0_xattn_Wo, L0_xattn_bo, L0_ffn_Wp1, L0_ffn_bp1, L0_ffn_Wp2, L0_ffn_bp2, L0_ffn_W1, L0_ffn_b1, L0_ffn_W2, L0_ffn_b2, L0_ffn_Wo, L0_ffn_bo, L1_xattn_Wq, L1_xattn_Wk, L1_xattn_Wv, L1_xattn_gq, L1_xattn_bq, L1_xattn_gk, L1_xattn_bk, L1_xattn_Wp, L1_xattn_bp, L1_ffn_Wr, L1_ffn_br, L1_ffn_W1, L1_ffn_b1, L1_ffn_W2, L1_ffn_b2, L1_ffn_gamma, L1_ffn_beta, L1_ffn_token_mask):
    import jax
    import jax.numpy as jnp

    def _L0_xattn_ref(q, k, v, kv_mask, Wq, bq, Wk, bk, Wv, bv, Wo, bo):
        import jax, jax.numpy as jnp
        import numpy as np
        D_MODEL = 256
        N_HEADS = 16
        HEAD_DIM = D_MODEL // N_HEADS
        B, Qlen, _ = q.shape
        Klen = k.shape[1]
        qh = (q @ Wq.T + bq).reshape(B, Qlen, N_HEADS, HEAD_DIM).transpose(0, 2, 1, 3)
        kh = (k @ Wk.T + bk).reshape(B, Klen, N_HEADS, HEAD_DIM).transpose(0, 2, 1, 3)
        vh = (v @ Wv.T + bv).reshape(B, Klen, N_HEADS, HEAD_DIM).transpose(0, 2, 1, 3)
        score = jnp.einsum('bhqd,bhkd->bhqk', qh, kh) / np.sqrt(HEAD_DIM).astype(np.float32)
        score = jnp.where(kv_mask[:, None, None, :], score, jnp.float32(-10000.0))
        attn = jax.nn.softmax(score, axis=-1)
        out = jnp.einsum('bhqk,bhkd->bhqd', attn, vh)
        out = out.transpose(0, 2, 1, 3).reshape(B, Qlen, D_MODEL)
        return out @ Wo.T + bo

    def _L0_ffn_ref(hidden_states, Wp1, bp1, Wp2, bp2, W1, b1, W2, b2, Wo, bo):
        import jax, jax.numpy as jnp
        import numpy as np
        B, S, H = (8, 1024, 256)
        NAV = 128
        E = 8
        F = 2 * H
        last = hidden_states[:, -1, :]
        logits = jax.nn.gelu(last @ Wp1 + bp1, approximate=False) @ Wp2 + bp2
        action_probs = jax.nn.softmax(logits, axis=-1)
        sel = jnp.argmax(action_probs, axis=-1)
        w1 = W1[sel]
        w2 = W2[sel]
        h = jax.nn.gelu(jnp.einsum('bsh,bhf->bsf', hidden_states, w1) + b1[sel][:, None, :], approximate=False)
        reasoned = jnp.einsum('bsf,bfh->bsh', h, w2) + b2[sel][:, None, :]
        out = reasoned @ Wo + bo
        return hidden_states + 0.3 * out

    def _L1_xattn_ref(q, k, v, Wq, Wk, Wv, gq, bq, gk, bk, Wp, bp):
        import jax, jax.numpy as jnp
        import numpy as np
        NUM_HEADS = 16
        EPS = 1e-05

        def _layernorm(x, gamma, beta):
            mu = jnp.mean(x, axis=-1, keepdims=True)
            var = jnp.var(x, axis=-1, keepdims=True)
            return (x - mu) * jax.lax.rsqrt(var + EPS) * gamma + beta
        B, Lq, C = q.shape
        Lk = k.shape[1]
        H = NUM_HEADS
        D = C // H
        scale = D ** (-0.5)
        qh = (q @ Wq.T).reshape(B, Lq, H, D).transpose(0, 2, 1, 3)
        kh = (k @ Wk.T).reshape(B, Lk, H, D).transpose(0, 2, 1, 3)
        vh = (v @ Wv.T).reshape(B, Lk, H, D).transpose(0, 2, 1, 3)
        qh = _layernorm(qh, gq, bq) * scale
        kh = _layernorm(kh, gk, bk)
        attn = jax.nn.sigmoid(jnp.einsum('bhqd,bhkd->bhqk', qh, kh))
        x = jnp.einsum('bhqk,bhkd->bhqd', attn, vh)
        x = x.transpose(0, 2, 1, 3).reshape(B, Lq, C)
        return x @ Wp.T + bp

    def _L1_ffn_ref(hidden_states, Wr, br, W1, b1, W2, b2, gamma, beta, token_mask):
        import math
        import jax, jax.numpy as jnp
        import numpy as np
        E = 8
        TOPK = 2
        CF = 1.25
        EPS = 1e-05
        NEG = -1e+30

        def _layer_norm(x, gamma, beta):
            mu = jnp.mean(x, axis=-1, keepdims=True)
            var = jnp.mean((x - mu) ** 2, axis=-1, keepdims=True)
            return (x - mu) * jax.lax.rsqrt(var + EPS) * gamma + beta
        B, S, H = hidden_states.shape
        x = hidden_states.reshape(-1, H)
        N = x.shape[0]
        logits = x @ Wr + br
        top_vals, top_idx = jax.lax.top_k(logits, TOPK)
        w = jax.nn.softmax(top_vals, axis=-1)
        flat_idx = top_idx.reshape(-1)
        flat_tok = jnp.repeat(jnp.arange(N), TOPK)
        w_flat = w.reshape(-1)
        cap = max(int(math.ceil(N / E * CF)), 1)
        key_mat = jnp.where(flat_idx[None, :] == jnp.arange(E)[:, None], w_flat[None, :], NEG)
        kv, ki = jax.lax.top_k(key_mat, cap)
        valid = kv > NEG / 2
        tok = flat_tok[ki]
        gate = jnp.where(valid, w_flat[ki], 0.0)
        xe = x[tok]
        h1 = jnp.einsum('ech,ehf->ecf', xe, W1) + b1[:, None, :]
        h1 = jax.nn.gelu(h1, approximate=False)
        y = jnp.einsum('ecf,efh->ech', h1, W2) + b2[:, None, :]
        out = jnp.zeros_like(x).at[tok.reshape(-1)].add((y * gate[..., None]).reshape(-1, H))
        out = out.reshape(B, S, H) + hidden_states
        return _layer_norm(out, gamma, beta)
    x = x + _L0_xattn_ref(_layernorm(x, axis=-1), ctx_1024, ctx_1024, mask_BxS2_bf1, L0_xattn_Wq, L0_xattn_bq, L0_xattn_Wk, L0_xattn_bk, L0_xattn_Wv, L0_xattn_bv, L0_xattn_Wo, L0_xattn_bo)
    x = x + _L0_ffn_ref(_layernorm(x, axis=-1), L0_ffn_Wp1, L0_ffn_bp1, L0_ffn_Wp2, L0_ffn_bp2, L0_ffn_W1, L0_ffn_b1, L0_ffn_W2, L0_ffn_b2, L0_ffn_Wo, L0_ffn_bo)
    x = x + _L1_xattn_ref(_layernorm(x, axis=-1), ctx_1024, ctx_1024, L1_xattn_Wq, L1_xattn_Wk, L1_xattn_Wv, L1_xattn_gq, L1_xattn_bq, L1_xattn_gk, L1_xattn_bk, L1_xattn_Wp, L1_xattn_bp)
    x = x + _L1_ffn_ref(_layernorm(x, axis=-1), L1_ffn_Wr, L1_ffn_br, L1_ffn_W1, L1_ffn_b1, L1_ffn_W2, L1_ffn_b2, L1_ffn_gamma, L1_ffn_beta, L1_ffn_token_mask)
    return x

_drawn_inputs = setup_inputs


def setup_inputs(seed=0):
    import zlib

    import numpy as np

    out = dict(_drawn_inputs(seed))
    spreads = {'L0_xattn_bq': (0.0, 0.8),
     'L0_xattn_bk': (0.0, 2.0),
     'L0_xattn_bv': (0.0, 0.337),
     'L0_xattn_bo': (0.0, 0.281),
     'L0_ffn_bp1': (0.0, 0.1),
     'L0_ffn_bp2': (0.0, 0.608),
     'L0_ffn_b1': (0.0, 2.0),
     'L0_ffn_b2': (0.0, 0.8),
     'L0_ffn_bo': (0.0, 0.8),
     'L1_xattn_gq': (1.0, 0.2),
     'L1_xattn_bq': (0.0, 0.443),
     'L1_xattn_gk': (1.0, 0.2),
     'L1_xattn_bk': (0.0, 0.1),
     'L1_xattn_bp': (0.0, 0.8),
     'L1_ffn_br': (0.0, 0.399),
     'L1_ffn_gamma': (1.0, 0.6),
     'L1_ffn_beta': (0.0, 0.8)}
    factors = {'L1_ffn_Wr': 4.433,
     'L1_ffn_W1': 4.448,
     'L1_ffn_b1': 64.0,
     'L1_ffn_W2': 4.039,
     'L1_ffn_b2': 64.0}
    for name, (base, spread) in spreads.items():
        noise = np.random.default_rng([zlib.crc32(name.encode()), seed]).standard_normal(out[name].shape)
        drawn = base * np.exp(spread * noise) if base else spread * noise
        out[name] = jnp.asarray(drawn.astype(out[name].dtype))
    for name, factor in factors.items():
        out[name] = (out[name] * factor).astype(out[name].dtype)
    return out
```

```python
from contextlib import ExitStack

import numpy as np

import concourse.bass as bass
from concourse import mybir

F32 = mybir.dt.float32
BF16 = mybir.dt.bfloat16
I32 = mybir.dt.int32
U32 = mybir.dt.uint32
U8 = mybir.dt.uint8
ALU = mybir.AluOpType
ACT = mybir.ActivationFunctionType
AX = mybir.AxisListType

P = 128
B, S, D = 8, 512, 256
NT = S // P
KC = D // P
H, HD = 16, 16
HC = H // KC
HG = 4
NG = H // HG
EPS = 1e-5
PAIRS = 6
K_MASK = PAIRS * HD
K_MAX = K_MASK + 1
K_ALL = K_MASK + 4
Q_PARTS = (0, 0, 0, 1, 1, 2)
K_PARTS = (0, 1, 2, 0, 1, 0)
SCALE = 1.0 / np.sqrt(HD)
MASK_Q, MASK_K = 250.0, -160.0
assert MASK_Q * MASK_K * SCALE == -10000.0


class Tally:

    def __init__(self, sem, base=0):
        self.sem, self.base, self.n = sem, base, 0

    def inc(self, ins):
        ins.then_inc(self.sem, 1)
        self.n += 1
        return self.base + self.n


def softmax_attention(nc, io, x, ident, identb):
    QUADS = NG * NT
    MX_LEAD = 6
    PV_LAG = 2
    STACK_DMAS = 4 * PAIRS + 1
    ctx = ExitStack()
    with ctx:
        def sb(name, shape, dt=F32):
            return ctx.enter_context(nc.sbuf_tensor("a_" + name, shape, dt))

        def ps(name, shape, dt=F32):
            return ctx.enter_context(nc.psum_tensor("a_" + name, shape, dt))

        def sem(name):
            return ctx.enter_context(nc.semaphore("a_" + name))

        wq, wk, wv, wo = (sb(n, [P, KC, D]) for n in ("wq", "wk", "wv", "wo"))
        bq, bk, bv = (sb(n, [P, KC]) for n in ("bq", "bk", "bv"))
        bo = sb("bo", [P, D])
        head_rows = sb("head_rows", [H, KC, P])
        ctxT = sb("ctxT", [P, KC, S])
        mask8 = sb("mask8", [P, S], U8)
        maskf = sb("maskf", [P, S])
        mask_row = sb("mask_row", [P, S], BF16)
        stats = sb("stats", [P, NT, 6])
        moments = sb("moments", [P, NT, 2])
        var_eps = sb("var_eps", [P, NT])
        rstd = sb("rstd", [P, NT])
        minus_half = sb("minus_half", [P, NT])
        xn = sb("xn", [P, NT, D])
        xT = sb("xT", [P, KC, S])
        proj = sb("proj", [P, 2, S])
        rest = sb("rest", [P, 2, S])
        parts = sb("parts", [P, 2, 3, S], BF16)
        q_stack = [sb(f"q_stack{i}", [P, H, S], BF16) for i in range(2)]
        k_stack = [sb(f"k_stack{i}", [P, H, S], BF16) for i in range(2)]
        v_ones = [sb(f"v_ones{i}", [P, NT, H, 2 * HD]) for i in range(2)]
        probs = sb("probs", [P, NT, HG, S])
        neg_max = sb("neg_max", [P, 2, NT, HG])
        neg_rest = sb("neg_rest", [P, NT, HG])
        neg_parts = sb("neg_parts", [P, NT, 3, HG], BF16)
        neg_rows = sb("neg_rows", [3 * HG, S], BF16)
        sums = sb("sums", [P, 2, S])
        values = sb("values", [P, 2, KC, S])
        den = sb("den", [P, 64])
        rden = sb("rden", [P, 64])
        rden_h = sb("rden_h", [H, S])
        oT = sb("oT", [P, KC, S])

        ps_score = [ps(f"score{i}", [P, S]) for i in range(2)]
        ps_max = [ps(f"max{i}", [P, S]) for i in range(2)]
        ps_pv = [ps(f"pv{i}", [P, S]) for i in range(2)]
        ps_a = ps("act", [P, S])
        ps_d = ps("dve", [P, S])

        x_first_in, x_rest_in = sem("x_first_in"), sem("x_rest_in")
        w_in, ctx_in, mask_in = sem("w_in"), sem("ctx_in"), sem("mask_in")
        consts, v_consts = sem("consts"), sem("v_consts")
        stats_ready, moments_ready, var_ready = sem("stats_ready"), sem("moments_ready"), sem("var_ready")
        rstd_ready, xn_ready = sem("rstd_ready"), sem("xn_ready")
        a_ready, a_empty = sem("a_ready"), sem("a_empty")
        d_ready, d_empty = sem("d_ready"), sem("d_empty")
        maskf_ready, mask_row_ready, mask_landed = sem("maskf_ready"), sem("mask_row_ready"), sem("mask_landed")
        masked, part0, rest_ready, part1, part2 = (
            sem("masked"), sem("part0"), sem("rest_ready"), sem("part1"), sem("part2"))
        stacked = [sem(f"stacked{i}") for i in range(2)]
        score_ready, probs_ready, pv_ready, sums_ready = (
            sem("score_ready"), sem("probs_ready"), sem("pv_ready"), sem("sums_ready"))
        max_ready, max_read, neg_chain, neg_ready, neg_landed = (
            sem("max_ready"), sem("max_read"), sem("neg_chain"), sem("neg_ready"), sem("neg_landed"))
        values_landed = [sem(f"values_landed{i}") for i in range(2)]
        den_landed = [sem(f"den_landed{i}") for i in range(2)]
        rden_ready, rden_landed = sem("rden_ready"), sem("rden_landed")
        weighted, ot_ready, residual, x_done = sem("weighted"), sem("ot_ready"), sem("residual"), sem("x_done")

        def batches(eng, batch):
            batch(0, 0, True, False)
            with eng.Fori(0, (B - 2) // 2) as i:
                batch(i * 2 + 1, 1, False, False)
                batch(i * 2 + 2, 0, False, False)
            batch(B - 1, (B - 1) % 2, False, True)

        KEYS0, KEYS1, XT0, XT1, QUERIES0, QUERIES1, V0, V1 = range(8)
        A_ITEMS = 8
        PROJ = ((KEYS0, False, 0), (KEYS1, False, 1), (QUERIES0, True, 0), (QUERIES1, True, 1))

        D_FIRST = ("neg1", "neg2", "neg3", "neg4")
        D_LATER = ("neg1", "neg2", "rden0", "rden1", "out0", "neg3", "out1", "neg4")
        D_END = 1 + len(D_FIRST) + len(D_LATER) * (B - 1) - 1

        def d_item(b, first, name):
            if first:
                return 1 + D_FIRST.index(name)
            return (b - 1) * len(D_LATER) + (1 + len(D_FIRST) + D_LATER.index(name))

        block = ctx.enter_context(nc.Block())

        @block.sync
        def _(sp):
            def loads(bb):
                sp.dma_start(ctxT[:], io["ctxT"][bass.ds(bb, 1)].rearrange("a (c p) n -> p (a c) n", p=P)
                             ).then_inc(ctx_in, 16)
                sp.dma_start(mask8[:], io["mask"][bass.ds(bb, 1), :].to_broadcast([P, S])).then_inc(mask_in, 16)

            def mask_to_stack(bb, par, unused=True):
                if not unused:
                    sp.wait_ge(score_ready, (bb - 1) * 64)
                sp.wait_ge(mask_row_ready, bb * 2 + 2)
                row = mask_row[96:97, :]
                sp.dma_start(k_stack[par][K_MASK:K_MASK + 1, :, :],
                             bass.AP(row.tensor, row.offset, [[S, 1], [0, H], [1, S]])).then_inc(mask_landed, 16)

            def stack(bb, par, k):
                _, is_q, c = PROJ[k]
                dst = (q_stack if is_q else k_stack)[par]
                for part, ready in enumerate((part0, part1, part2)):
                    sp.wait_ge(ready, bb * 4 + (k + 1))
                    for j in range(PAIRS):
                        if (Q_PARTS if is_q else K_PARTS)[j] == part:
                            sp.dma_start(dst[HD * j:HD * (j + 1), HC * c:HC * (c + 1), :],
                                         parts[:, k % 2, part, :]).then_inc(stacked[k % 2], 16)

            def sums_out(b, par, g, first):
                if g == 0 and not first:
                    sp.wait_ge(ot_ready, (b - 1) * KC)
                    sp.wait_ge(rden_ready, b)
                sp.wait_ge(sums_ready, b * 4 + (g + 1))
                for hh in range(HG):
                    h = HG * g + hh
                    sp.dma_start(values[HD * (h % HC):HD * (h % HC + 1), par, h // HC, :],
                                 sums[32 * hh:32 * hh + HD, g % 2, :]).then_inc(values_landed[g % 2], 16)
                    sp.dma_start(den[8 * h:8 * h + 8, :],
                                 sums[32 * hh + HD:32 * hh + HD + 1, g % 2, :]).then_inc(den_landed[g % 2], 16)

            def rden_out(b, d_prev):
                sp.wait_ge(d_ready, d_prev)
                sp.wait_ge(rden_ready, b + 1)
                sp.dma_start(rden_h[:, :], rden[:, :]).then_inc(rden_landed, 16)

            for dst, name in ((wk, "wk"), (wq, "wq"), (wv, "wv"), (wo, "wo")):
                if dst is wq:
                    loads(0)
                    for small in ("bk", "bq", "bv"):
                        sp.dma_start({"bk": bk, "bq": bq, "bv": bv}[small][:], io[small]).then_inc(w_in, 16)
                sp.dma_start(dst[:], io[name].rearrange("(c p) n -> p c n", p=P)).then_inc(w_in, 16)
            sp.dma_start(bo[:], io["bo"].to_broadcast([P, D])).then_inc(w_in, 16)
            sp.wait_ge(consts, 5)
            mask_to_stack(0, 0)
            for k in range(4):
                stack(0, 0, k)

            def batch(b, par, first, last):
                if not last:
                    sp.wait_ge(maskf_ready, b + 1)
                    sp.wait_ge(a_ready, b * A_ITEMS + A_ITEMS)
                    loads(b + 1)
                    mask_to_stack(b + 1, 1 - par, first)
                if not first:
                    sums_out(b - 1, 1 - par, 3, False)
                if not last:
                    stack(b + 1, 1 - par, 0)
                if not first:
                    rden_out(b - 1, (b - 1) * len(D_LATER) + (1 + len(D_FIRST) + D_LATER.index("rden1") + 1 - len(D_LATER)))
                if not last:
                    stack(b + 1, 1 - par, 1)
                sums_out(b, par, 0, first)
                if not last:
                    stack(b + 1, 1 - par, 2)
                    stack(b + 1, 1 - par, 3)
                sums_out(b, par, 1, first)
                sums_out(b, par, 2, first)

            batches(sp, batch)
            sums_out(B - 1, (B - 1) % 2, 3, False)
            rden_out(B - 1, d_item(B - 1, False, "rden1") + 1)

        @block.scalar
        def _(act):
            def evacuate(bb, item, out, **kw):
                act.wait_ge(a_ready, bb * A_ITEMS + (item + 1))
                nc.scalar.activation(out, ps_a[:] if len(out.shape) == 2 else
                                     ps_a[:].rearrange("p (t h d) -> p t h d", t=2, h=H), ACT.Identity,
                                     **kw).then_inc(a_empty, 1)

            def project(bb, k):
                item, is_q, c = PROJ[k]
                if k >= 2:
                    act.wait_ge(rest_ready, bb * 4 + (k - 1))
                elif not (isinstance(bb, int) and bb == 0):
                    act.wait_ge(rest_ready, (bb - 1) * 4 + (k + 3))
                evacuate(bb, item, proj[:, k % 2, :], bias=(bq if is_q else bk)[:, c:c + 1])

            def transposed(bb, c):
                evacuate(bb, XT0 + c, xT[:, c, :])

            def v_tiles(bb, par, t):
                evacuate(bb, V0 + t, v_ones[par][:, 2 * t:2 * t + 2, :, 0:HD])

            def neg_in(b, par, g, d):
                act.wait_ge(d_empty, d + 1)
                act.dma_start(q_stack[par][K_MAX:K_ALL, HG * g:HG * (g + 1), :], neg_rows[:]).then_inc(neg_landed, 16)

            def sums_of(b, g):
                G = b * 4 + g
                act.wait_ge(pv_ready, G * NT + NT)
                if not (isinstance(b, int) and b * 4 + g < 2):
                    act.wait_ge(values_landed[g % 2], b * 128 + (g // 2) * 64)
                    act.wait_ge(den_landed[g % 2], b * 128 + (g // 2) * 64)
                nc.scalar.copy(sums[:, g % 2, :], ps_pv[g % 2][:]).then_inc(sums_ready, 1)

            act.dma_start(x[:, 0:NT, :], io["x"][0].rearrange("(t p) d -> p t d", p=P)).then_inc(x_first_in, 16)
            act.dma_start(x[:, NT:, :], io["x"][1:].rearrange("b (t p) d -> p (b t) d", p=P)).then_inc(x_rest_in, 16)
            act.wait_ge(w_in, 16 * 8)
            project(0, 0), project(0, 1)
            transposed(0, 0), transposed(0, 1)
            project(0, 2), project(0, 3)
            v_tiles(0, 0, 0), v_tiles(0, 0, 1)
            neg_in(0, 0, 0, 0)

            def batch(b, par, first, last):
                for u in range(QUADS):
                    g, kc = divmod(u, NT)
                    quad = b * QUADS + u
                    for hh in range(HG):
                        act.wait_ge(score_ready, quad * HG + (hh + 1))
                        if hh == 0 and not (first and u < NT):
                            act.wait_ge(pv_ready, quad + (1 - NT))
                        nc.scalar.activation(probs[:, kc, hh, :], ps_score[hh % 2][:], ACT.Exp, scale=SCALE
                                             ).then_inc(probs_ready, 1)
                    if u == 1 and not first:
                        sums_of(b - 1, 3)
                    if u % NT == 1 and u > 1:
                        sums_of(b, g - 1)
                    if not last:
                        {1: lambda: project(b + 1, 0),
                         2: lambda: (project(b + 1, 1), transposed(b + 1, 0)),
                         3: lambda: transposed(b + 1, 1),
                         4: lambda: project(b + 1, 2),
                         5: lambda: project(b + 1, 3),
                         11: lambda: v_tiles(b + 1, 1 - par, 0),
                         12: lambda: v_tiles(b + 1, 1 - par, 1)}.get(u, lambda: None)()
                    if u % NT == 2 and u < 12:
                        neg_in(b, par, g + 1, d_item(b, first, f"neg{g + 1}"))
                    if u == 14 and not last:
                        neg_in(b + 1, 1 - par, 0, d_item(b, first, "neg4"))

            batches(act, batch)
            sums_of(B - 1, 3)

        @block.gpsimd
        def _(pool):
            nc.gpsimd.memset(minus_half[:], -0.5).then_inc(consts, 1)
            for i in range(2):
                pool.wait_ge(consts, 2 * i + 1)
                nc.gpsimd.memset(q_stack[i][K_MASK:K_MASK + 1, :, :], MASK_Q).then_inc(consts, 1)
                pool.wait_ge(consts, 2 * i + 2)
                nc.gpsimd.memset(k_stack[i][K_MASK:K_ALL, :, :], 1.0).then_inc(consts, 1)
            pool.wait_ge(consts, 5)
            nc.gpsimd.memset(head_rows[:], 1.0).then_inc(consts, 1)
            pool.wait_ge(consts, 6)
            nc.gpsimd.affine_select(out=head_rows[:], in_=head_rows[:], compare_op=ALU.is_ge, fill=0.0, base=0,
                                    pattern=[[P, KC], [1, P]], channel_multiplier=-HD).then_inc(consts, 1)
            pool.wait_ge(consts, 7)
            nc.gpsimd.affine_select(out=head_rows[:], in_=head_rows[:], compare_op=ALU.is_ge, fill=0.0, base=HD - 1,
                                    pattern=[[-P, KC], [-1, P]], channel_multiplier=HD).then_inc(consts, 1)

            def invert_deviation(bb):
                pool.wait_ge(var_ready, bb + 1)
                nc.gpsimd.tensor_tensor(rstd[:], var_eps[:], minus_half[:], ALU.pow).then_inc(rstd_ready, 1)

            def split(bb, k, step):
                n = bb * 4 + k
                item, is_q, _ = PROJ[k]
                if step == 0:
                    pool.wait_ge(a_empty, bb * A_ITEMS + (item + 1))
                    pool.wait_ge(maskf_ready, bb + 1)
                    nc.gpsimd.tensor_tensor(proj[:, k % 2, :], proj[:, k % 2, :], maskf[:], ALU.mult).then_inc(masked, 1)
                elif step == 1:
                    pool.wait_ge(part0, n + 1)
                    if not (isinstance(n, int) and n < 2):
                        pool.wait_ge(part2, n - 1)
                    nc.gpsimd.tensor_tensor(rest[:, k % 2, :], proj[:, k % 2, :], parts[:, k % 2, 0, :],
                                            ALU.subtract).then_inc(rest_ready, 1)
                else:
                    pool.wait_ge(part1, n + 1)
                    nc.gpsimd.tensor_tensor(parts[:, k % 2, 2, :], rest[:, k % 2, :], parts[:, k % 2, 1, :],
                                            ALU.subtract).then_inc(part2, 1)

            def add_output_bias(b, first):
                for t in range(NT):
                    tile = x[:, bass.ds(b * NT + t, 1), :].rearrange("p a n -> p (a n)")
                    if t == 0:
                        pool.wait_ge(xn_ready, b * NT + NT)
                        pool.wait_ge(w_in, 16 * 8)
                    nc.gpsimd.tensor_tensor(tile, tile, bo[:], ALU.add).then_inc(residual, 1)

            def prepare(bb):
                invert_deviation(bb)
                split(bb, 0, 0)
                split(bb, 0, 1)
                split(bb, 1, 0)
                split(bb, 0, 2)
                split(bb, 1, 1)
                split(bb, 1, 2)
                split(bb, 2, 1)
                split(bb, 2, 2)
                split(bb, 3, 1)
                split(bb, 3, 2)

            pool.wait_ge(consts, 8)
            prepare(0)

            def batch(b, par, first, last):
                if not last:
                    prepare(b + 1)
                add_output_bias(b, first)

            batches(pool, batch)

        @block.vector
        def _(dve):
            def normalise(bb):
                dve.wait_ge(x_first_in if isinstance(bb, int) and bb == 0 else x_rest_in, 16)
                for t in range(NT):
                    nc.vector.bn_stats(stats[:, t, :], x[:, bass.ds(bb * NT + t, 1), :].rearrange("p a n -> p (a n)")
                                       ).then_inc(stats_ready, 1)
                dve.wait_ge(stats_ready, bb * NT + NT)
                nc.vector.memset(var_eps[:], EPS).then_inc(moments_ready, 1)
                for t in range(NT):
                    nc.vector.bn_aggr(moments[:, t, :], stats[:, t, :]).then_inc(moments_ready, 1)
                dve.wait_ge(moments_ready, bb * (NT + 1) + (NT + 1))
                nc.vector.tensor_tensor(var_eps[:], moments[:, :, 1], var_eps[:], ALU.add).then_inc(var_ready, 1)

            def centre(bb):
                dve.wait_ge(rstd_ready, bb + 1)
                if not (isinstance(bb, int) and bb == 0):
                    dve.wait_ge(a_ready, (bb - 1) * A_ITEMS + (XT1 + 1))
                for t in range(NT):
                    nc.vector.tensor_scalar(xn[:, t, :], x[:, bass.ds(bb * NT + t, 1), :].rearrange("p a n -> p (a n)"),
                                            moments[:, t, 0:1], rstd[:, t:t + 1], ALU.subtract, ALU.mult
                                            ).then_inc(xn_ready, 1)

            def read_mask(bb):
                dve.wait_ge(mask_in, (bb + 1) * 16)
                if not (isinstance(bb, int) and bb == 0):
                    dve.wait_ge(masked, bb * 2)
                    dve.wait_ge(mask_landed, bb * 16)
                nc.vector.tensor_copy(maskf[:], mask8[:]).then_inc(maskf_ready, 1)
                dve.wait_ge(maskf_ready, bb + 1)
                nc.vector.tensor_scalar(mask_row[96:97, :], maskf[96:97, :], -MASK_K, MASK_K, ALU.mult, ALU.add
                                        ).then_inc(mask_row_ready, 2)

            def part(bb, k, step):
                n = bb * 4 + k
                item, is_q, _ = PROJ[k]
                if step == 0:
                    dve.wait_ge(a_empty, bb * A_ITEMS + (item + 1))
                    if not is_q:
                        dve.wait_ge(masked, bb * 2 + (k + 1))
                    if not (isinstance(n, int) and n < 2):
                        dve.wait_ge(stacked[k % 2], bb * (2 * 96) + 96 * (k // 2))
                    nc.vector.tensor_copy(parts[:, k % 2, 0, :], proj[:, k % 2, :]).then_inc(part0, 1)
                else:
                    dve.wait_ge(rest_ready, n + 1)
                    nc.vector.tensor_copy(parts[:, k % 2, 1, :], rest[:, k % 2, :]).then_inc(part1, 1)

            def maxima(b, v):
                for s in range(NT):
                    n = b * 64 + (4 * v + s)
                    dve.wait_ge(max_ready, n + 1)
                    nc.vector.tensor_reduce(neg_max[:, (v // HG) % 2, s, v % HG:v % HG + 1], ps_max[s % 2][:], AX.X,
                                            ALU.max, negate=True).then_inc(max_read, 1)

            def split_maxima(b, g):
                G = b * 4 + g
                dve.wait_ge(max_read, G * 16 + 16)
                nm = neg_max[:, g % 2, :, :]
                nc.vector.tensor_copy(neg_parts[:, :, 0, :], nm).then_inc(neg_chain, 1)
                dve.wait_ge(neg_chain, G * 3 + 1)
                nc.vector.tensor_tensor(neg_rest[:], nm, neg_parts[:, :, 0, :], ALU.subtract).then_inc(neg_chain, 1)
                dve.wait_ge(neg_chain, G * 3 + 2)
                nc.vector.tensor_copy(neg_parts[:, :, 1, :], neg_rest[:]).then_inc(neg_chain, 1)
                dve.wait_ge(neg_chain, G * 3 + 3)
                nc.vector.tensor_tensor(neg_parts[:, :, 2, :], neg_rest[:], neg_parts[:, :, 1, :], ALU.subtract
                                        ).then_inc(neg_ready, 1)

            def rows_of_maxima(b, g, d):
                dve.wait_ge(d_ready, d + 1)
                if not (isinstance(b, int) and b * 4 + g == 0):
                    dve.wait_ge(neg_landed, (b * 4 + g) * 16)
                nc.vector.tensor_copy(neg_rows[:], ps_d[:].bitcast(BF16)[0:3 * HG, 0:S]).then_inc(d_empty, 1)

            def invert_denominators(b):
                for i in range(2):
                    dve.wait_ge(den_landed[i], b * 128 + 128)
                if not (isinstance(b, int) and b == 0):
                    dve.wait_ge(rden_landed, b * 16)
                nc.vector.reciprocal(rden[:], den[:]).then_inc(rden_ready, 1)

            def weigh(b, par, c, d):
                dve.wait_ge(d_ready, d + 1)
                if c == 0:
                    for i in range(2):
                        dve.wait_ge(values_landed[i], b * 128 + 128)
                nc.vector.tensor_tensor(oT[:, c, :], values[:, par, c, :], ps_d[:], ALU.mult).then_inc(d_empty, 1)
                dve.wait_ge(d_empty, d + 1)
                nc.vector.tensor_scalar(oT[:, c, :], oT[:, c, :], bv[:, c:c + 1], None, ALU.add).then_inc(ot_ready, 1)

            def output(b, t, d):
                dve.wait_ge(d_ready, d + 1)
                dve.wait_ge(residual, b * NT + NT)
                tiles = x[:, bass.ds(b * NT + 2 * t, 2), :]
                nc.vector.tensor_tensor(tiles, ps_d[:].rearrange("p (t n) -> p t n", t=2), tiles, ALU.add
                                        ).then_inc(d_empty, 1)

            for i in range(2):
                nc.vector.memset(v_ones[i][:, :, :, HD:], 1.0).then_inc(v_consts, 1)
            read_mask(0)
            normalise(0)
            centre(0)
            for k in range(4):
                part(0, k, 0)
                part(0, k, 1)
            for v in range(MX_LEAD):
                maxima(0, v)
                if v == 3:
                    split_maxima(0, 0)
            rows_of_maxima(0, 0, 0)

            def batch(b, par, first, last):
                for u in range(QUADS):
                    v = u + MX_LEAD
                    if v < H:
                        maxima(b, v)
                    elif not last:
                        maxima(b + 1, v - H)
                    if u % 4 == 1 and u < 12:
                        split_maxima(b, u // 4 + 1)
                    if u == 13 and not last:
                        split_maxima(b + 1, 0)
                    if not last:
                        if u == 0:
                            read_mask(b + 1)
                            normalise(b + 1)
                        elif u == 1:
                            centre(b + 1)
                        for k, at in ((0, 2), (1, 3), (2, 5), (3, 6)):
                            if u == at + 1:
                                part(b + 1, k, 1)
                            if u == at:
                                part(b + 1, k, 0)
                    if u == 3 and not first:
                        invert_denominators(b - 1)
                    if u % 4 == 2 and u < 12:
                        rows_of_maxima(b, u // 4 + 1, d_item(b, first, f"neg{u // 4 + 1}"))
                    if u == 14 and not last:
                        rows_of_maxima(b + 1, 0, d_item(b, first, "neg4"))
                    if not first:
                        if u in (7, 8):
                            weigh(b - 1, 1 - par, u - 7, d_item(b, first, f"rden{u - 7}"))
                        if u in (9, 11):
                            output(b - 1, (u - 9) // 2, d_item(b, first, f"out{(u - 9) // 2}"))

            batches(dve, batch)
            invert_denominators(B - 1)
            for c in range(KC):
                weigh(B - 1, (B - 1) % 2, c, D_END + c)
            for t in range(2):
                output(B - 1, t, D_END + 2 + t)

        @block.tensor
        def _(pe):
            def take_act(bb, item):
                if not (isinstance(bb, int) and bb * A_ITEMS + item == 0):
                    pe.wait_ge(a_empty, bb * A_ITEMS + item)

            def project(bb, k):
                item, is_q, c = PROJ[k]
                take_act(bb, item)
                if is_q:
                    pe.wait_ge(a_empty, bb * A_ITEMS + (XT1 + 1))
                else:
                    pe.wait_ge(ctx_in, (bb + 1) * 16)
                for kk in range(KC):
                    mm = nc.tensor.matmul(ps_a[:], (wq if is_q else wk)[:, kk, c * P:(c + 1) * P],
                                          (xT if is_q else ctxT)[:, kk, :], start=(kk == 0), stop=(kk == KC - 1))
                mm.then_inc(a_ready, 1)

            def transpose_x(bb, c):
                take_act(bb, XT0 + c)
                pe.wait_ge(xn_ready, bb * NT + NT)
                for t in range(NT):
                    mm = nc.tensor.transpose(ps_a[:, t * P:(t + 1) * P], xn[:, t, c * P:(c + 1) * P], ident[:])
                mm.then_inc(a_ready, 1)

            def v_tiles(bb, t):
                take_act(bb, V0 + t)
                for tt in range(2):
                    for kk in range(KC):
                        mm = nc.tensor.matmul(ps_a[:, tt * D:(tt + 1) * D],
                                              ctxT[:, kk, (2 * t + tt) * P:(2 * t + tt + 1) * P], wv[:, kk, :],
                                              start=(kk == 0), stop=(kk == KC - 1))
                mm.then_inc(a_ready, 1)

            def head_scores_max(b, par, v, s):
                n = b * 64 + (4 * v + s)
                if v == 0 and s == 0:
                    for i in range(2):
                        pe.wait_ge(stacked[i], b * 192 + 192)
                    pe.wait_ge(mask_landed, b * 16 + 16)
                if not (isinstance(n, int) and n < 2):
                    pe.wait_ge(max_read, n - 1)
                nc.tensor.matmul(ps_max[s % 2][:], q_stack[par][0:K_MAX, v, s * P:(s + 1) * P],
                                 k_stack[par][0:K_MAX, v, :], start=True, stop=True).then_inc(max_ready, 1)

            def rows_of_maxima(b, g, d):
                pe.wait_ge(neg_ready, b * 4 + (g + 1))
                if not (isinstance(d, int) and d == 0):
                    pe.wait_ge(d_empty, d)
                for t in range(NT):
                    mm = nc.tensor.transpose(ps_d[:].bitcast(BF16)[0:3 * HG, t * P:(t + 1) * P],
                                             neg_parts[:, t, :, :].rearrange("p j h -> p (j h)"), identb[:])
                mm.then_inc(d_ready, 1)

            def scores(b, par, u, hh):
                g, kc = divmod(u, NT)
                n = b * 64 + (4 * u + hh)
                if kc == 0 and hh == 0:
                    pe.wait_ge(neg_landed, (b * 4 + g) * 16 + 16)
                if not (isinstance(n, int) and n < 2):
                    pe.wait_ge(probs_ready, n - 1)
                nc.tensor.matmul(ps_score[hh % 2][:], k_stack[par][0:K_ALL, HG * g + hh, kc * P:(kc + 1) * P],
                                 q_stack[par][0:K_ALL, HG * g + hh, :], start=True, stop=True).then_inc(score_ready, 1)

            def weighted_values(b, par, w):
                g, kc = divmod(w, NT)
                G = b * 4 + g
                pe.wait_ge(probs_ready, b * 64 + (4 * w + 4))
                if w == 0:
                    pe.wait_ge(a_empty, b * A_ITEMS + A_ITEMS)
                    pe.wait_ge(v_consts, 2)
                if kc == 0 and not (isinstance(G, int) and G < 2):
                    pe.wait_ge(sums_ready, G - 1)
                for hh in range(HG):
                    mm = nc.tensor.matmul(ps_pv[g % 2][32 * hh:32 * hh + 32, :], v_ones[par][:, kc, HG * g + hh, :],
                                          probs[:, kc, hh, :], start=(kc == 0), stop=(kc == NT - 1),
                                          tile_position=(0, 32 * hh))
                mm.then_inc(pv_ready, 1)

            def spread_denominators(b, c, d):
                pe.wait_ge(rden_landed, b * 16 + 16)
                pe.wait_ge(d_empty, d)
                nc.tensor.matmul(ps_d[:], head_rows[:, c, :], rden_h[:, :], start=True, stop=True).then_inc(d_ready, 1)

            def output(b, t, d):
                pe.wait_ge(ot_ready, b * KC + KC)
                pe.wait_ge(d_empty, d)
                for tt in range(2):
                    for c in range(KC):
                        mm = nc.tensor.matmul(ps_d[:, tt * D:(tt + 1) * D], oT[:, c, (2 * t + tt) * P:(2 * t + tt + 1) * P],
                                              wo[:, c, :], start=(c == 0), stop=(c == KC - 1))
                mm.then_inc(d_ready, 1)

            pe.wait_ge(w_in, 16 * 8)
            project(0, 0), project(0, 1)
            transpose_x(0, 0), transpose_x(0, 1)
            project(0, 2), project(0, 3)
            v_tiles(0, 0), v_tiles(0, 1)
            pe.wait_ge(consts, 8)
            for v in range(MX_LEAD):
                for s in range(NT):
                    head_scores_max(0, 0, v, s)
            rows_of_maxima(0, 0, 0)

            def batch(b, par, first, last):
                for u in range(QUADS):
                    v = u + MX_LEAD
                    for half in range(2):
                        for s in (2 * half, 2 * half + 1):
                            scores(b, par, u, s)
                            if v < H:
                                head_scores_max(b, par, v, s)
                            elif not last:
                                head_scores_max(b + 1, 1 - par, v - H, s)
                        if half == 0 and u >= PV_LAG:
                            weighted_values(b, par, u - PV_LAG)
                        elif half == 0 and not first:
                            weighted_values(b - 1, 1 - par, QUADS + u - PV_LAG)
                    if not last:
                        if u in (1, 2):
                            project(b + 1, u - 1)
                        if u in (2, 3):
                            transpose_x(b + 1, u - 2)
                        if u in (4, 5):
                            project(b + 1, u - 2)
                        if u in (11, 12):
                            v_tiles(b + 1, u - 11)
                    if u % 4 == 2 and u < 12:
                        rows_of_maxima(b, u // 4 + 1, d_item(b, first, f"neg{u // 4 + 1}"))
                    if u == 14 and not last:
                        rows_of_maxima(b + 1, 0, d_item(b, first, "neg4"))
                    if not first:
                        if u in (7, 8):
                            spread_denominators(b - 1, u - 7, d_item(b, first, f"rden{u - 7}"))
                        if u in (9, 11):
                            output(b - 1, (u - 9) // 2, d_item(b, first, f"out{(u - 9) // 2}"))

            batches(pe, batch)
            for w in range(QUADS - PV_LAG, QUADS):
                weighted_values(B - 1, (B - 1) % 2, w)
            for c in range(KC):
                spread_denominators(B - 1, c, D_END + c)
            for t in range(2):
                output(B - 1, t, D_END + 2 + t)


def expert_per_batch(nc, io, x, ident):
    E, F = 8, 2 * D
    FC = F // P
    OUT_SCALE = 0.3
    ctx = ExitStack()
    with ctx:
        def sb(name, shape, dt=F32):
            return ctx.enter_context(nc.sbuf_tensor("b_" + name, shape, dt))

        def ps(name, shape, dt=F32):
            return ctx.enter_context(nc.psum_tensor("b_" + name, shape, dt))

        def sem(name):
            return ctx.enter_context(nc.semaphore("b_" + name))

        pw1, pb1, pw2, pb2 = sb("pw1", [P, KC, P]), sb("pb1", [P, 1]), sb("pw2", [P, E]), sb("pb2", [B, E])
        last = sb("last", [B, D])
        last_stats, last_moments = sb("last_stats", [B, 6]), sb("last_moments", [B, 2])
        last_var, last_rstd = sb("last_var", [B, 1]), sb("last_rstd", [B, 1])
        lastT, hiddenT = sb("lastT", [P, KC, B]), sb("hiddenT", [P, B])
        logits, neg_top, exps, total = sb("logits", [B, E]), sb("neg_top", [B, 1]), sb("exps", [B, E]), sb("total", [B, 1])
        inv_total, policy, top = sb("inv_total", [B, 1]), sb("policy", [B, E]), sb("top", [B, 1])
        countdown, winner, choice_f, choice = (sb("countdown", [B, E]), sb("winner", [B, E]), sb("choice_f", [B, 1]),
                                               sb("choice", [B, 1], I32))
        choices = sb("choices", [1, B], I32)
        minus_half = sb("minus_half", [P, NT])
        w1 = [sb(f"w1_{i}", [P, KC, F]) for i in range(2)]
        w2 = [sb(f"w2_{i}", [P, FC, D]) for i in range(2)]
        b1 = [sb(f"b1_{i}", [P, FC]) for i in range(2)]
        b2 = [sb(f"b2_{i}", [P, KC]) for i in range(2)]
        wo, bo = sb("wo", [P, KC, D]), sb("bo", [P, D])
        stats, moments = sb("stats", [P, NT, 6]), sb("moments", [P, NT, 2])
        var_eps, rstd = sb("var_eps", [P, NT]), sb("rstd", [P, NT])
        xn = [sb(f"xn{i}", [P, NT, D]) for i in range(2)]
        xT = [sb(f"xT{i}", [P, KC, S]) for i in range(2)]
        hT = sb("hT", [P, FC, S])
        rT = [sb(f"rT{i}", [P, KC, S]) for i in range(2)]

        ps_t = [ps(f"t{i}", [P, S]) for i in range(2)]
        ps_h = [ps(f"h{i}", [P, S]) for i in range(2)]
        ps_r = [ps(f"r{i}", [P, S]) for i in range(2)]
        ps_o = [ps(f"o{i}", [P, S]) for i in range(2)]

        policy_in, wo_in, bo_in, last_in, choices_in = (sem("policy_in"), sem("wo_in"), sem("bo_in"), sem("last_in"),
                                                        sem("choices_in"))
        weights_in = [sem(f"weights_in{i}") for i in range(2)]
        consts, policy_dve, last_rstd_ready = sem("consts"), sem("policy_dve"), sem("last_rstd_ready")
        policy_pe, policy_act, bo_scaled = sem("policy_pe"), sem("policy_act"), sem("bo_scaled")
        stats_ready, moments_ready, var_ready, rstd_ready, xn_ready = (
            sem("stats_ready"), sem("moments_ready"), sem("var_ready"), sem("rstd_ready"), sem("xn_ready"))
        turned, xT_ready, h_sum, hT_ready, r_sum, rT_ready, o_sum, x_done, residual = (
            sem("turned"), sem("xT_ready"), sem("h_sum"), sem("hT_ready"), sem("r_sum"), sem("rT_ready"),
            sem("o_sum"), sem("x_done"), sem("residual"))

        def batches(eng, batch):
            batch(0, 0, True, False)
            with eng.Fori(0, (B - 2) // 2) as i:
                batch(i * 2 + 1, 1, False, False)
                batch(i * 2 + 2, 0, False, False)
            batch(B - 1, (B - 1) % 2, False, True)

        def tiles(b, t, n):
            return x[:, bass.ds(b * NT + t, n), :]

        block = ctx.enter_context(nc.Block())

        @block.sync
        def _(sp):
            sp.dma_start(last[:], x[P - 1:P, NT - 1:B * NT:NT, :]).then_inc(last_in, 16)
            sp.dma_start(pw1[:], io["pw1"].rearrange("(c p) n -> p c n", p=P)).then_inc(policy_in, 16)
            sp.dma_start(pb1[:], io["pb1"]).then_inc(policy_in, 16)
            sp.dma_start(pw2[:], io["pw2"]).then_inc(policy_in, 16)
            sp.dma_start(pb2[:], io["pb2"].to_broadcast([B, E])).then_inc(policy_in, 16)
            sp.dma_start(bo[:], io["fbo"].to_broadcast([P, D])).then_inc(bo_in, 16)
            sp.dma_start(wo[:], io["fwo"].rearrange("(c p) n -> p c n", p=P)).then_inc(wo_in, 16)
            sp.wait_ge(policy_dve, 13)
            sp.dma_start(choices[:, :], choice[:, :]).then_inc(choices_in, 16)
            sp.wait_ge(choices_in, 16)

            def load(bb, par):
                e = sp.value_load(choices[0:1, bass.ds(bb, 1)], min_val=0, max_val=E - 1)
                sp.dma_start(w1[par][:], io["fw1"][bass.ds(e, 1)].rearrange("a (c p) f -> p (a c) f", p=P)
                             ).then_inc(weights_in[par], 16)
                sp.dma_start(b1[par][:], io["fb1"][bass.ds(e, 1)].rearrange("a p c -> p (a c)")
                             ).then_inc(weights_in[par], 16)
                sp.dma_start(w2[par][:], io["fw2"][bass.ds(e, 1)].rearrange("a (c p) f -> p (a c) f", p=P)
                             ).then_inc(weights_in[par], 16)
                sp.dma_start(b2[par][:], io["fb2"][bass.ds(e, 1)].rearrange("a p c -> p (a c)")
                             ).then_inc(weights_in[par], 16)

            load(0, 0)

            def batch(b, par, first, last):
                if not last:
                    if not first:
                        sp.wait_ge(rT_ready, b * KC)
                    load(b + 1, 1 - par)

            batches(sp, batch)

        @block.gpsimd
        def _(pool):
            nc.gpsimd.memset(minus_half[:], -0.5).then_inc(consts, 1)
            nc.gpsimd.iota(countdown[:], pattern=[[-1, E]], base=E, channel_multiplier=0,
                           allow_small_or_imprecise_dtypes=True).then_inc(consts, 1)
            pool.wait_ge(consts, 2)
            pool.wait_ge(policy_dve, 3)
            nc.gpsimd.tensor_tensor(last_rstd[:], last_var[:], minus_half[0:B, 0:1], ALU.pow).then_inc(last_rstd_ready, 1)

            def invert_deviation(bb):
                pool.wait_ge(var_ready, bb + 1)
                nc.gpsimd.tensor_tensor(rstd[:], var_eps[:], minus_half[:], ALU.pow).then_inc(rstd_ready, 1)

            pool.wait_ge(last_rstd_ready, 1)
            invert_deviation(0)
            pool.wait_ge(bo_scaled, 1)

            def batch(b, par, first, last):
                if not last:
                    invert_deviation(b + 1)
                pool.wait_ge(xn_ready, b * NT + NT)
                nc.gpsimd.tensor_tensor(tiles(b, 0, NT), tiles(b, 0, NT), xn[par][:], ALU.add).then_inc(residual, 1)
                for t in reversed(range(NT)):
                    tile = tiles(b, t, 1).rearrange("p a n -> p (a n)")
                    if t == NT - 1:
                        pool.wait_ge(residual, b * (NT + 1) + 1)
                    nc.gpsimd.tensor_tensor(tile, tile, bo[:], ALU.add).then_inc(residual, 1)

            batches(pool, batch)

        @block.vector
        def _(dve):
            step = [0]

            def chained(ins):
                step[0] += 1
                ins.then_inc(policy_dve, 1)
                dve.wait_ge(policy_dve, step[0])

            dve.wait_ge(last_in, 16)
            chained(nc.vector.bn_stats(last_stats[:], last[:]))
            chained(nc.vector.bn_aggr(last_moments[:], last_stats[:]))
            chained(nc.vector.tensor_scalar(last_var[:], last_moments[:, 1:2], EPS, None, ALU.add))
            dve.wait_ge(last_rstd_ready, 1)
            chained(nc.vector.tensor_scalar(last[:], last[:], last_moments[:, 0:1], last_rstd[:], ALU.subtract, ALU.mult))
            dve.wait_ge(policy_pe, 1)
            chained(nc.vector.tensor_copy(lastT[:], ps_t[0][:, 0:KC * B].rearrange("p (c b) -> p c b", c=KC)))

            def statistics(bb):
                for t in range(NT):
                    nc.vector.bn_stats(stats[:, t, :], tiles(bb, t, 1).rearrange("p a n -> p (a n)")
                                       ).then_inc(stats_ready, 1)
                dve.wait_ge(stats_ready, bb * NT + NT)
                nc.vector.memset(var_eps[:], EPS).then_inc(moments_ready, 1)
                for t in range(NT):
                    nc.vector.bn_aggr(moments[:, t, :], stats[:, t, :]).then_inc(moments_ready, 1)
                dve.wait_ge(moments_ready, bb * (NT + 1) + (NT + 1))
                nc.vector.tensor_tensor(var_eps[:], moments[:, :, 1], var_eps[:], ALU.add).then_inc(var_ready, 1)

            def centre(bb, par):
                dve.wait_ge(rstd_ready, bb + 1)
                for t in range(NT):
                    nc.vector.tensor_scalar(xn[par][:, t, :], tiles(bb, t, 1).rearrange("p a n -> p (a n)"),
                                            moments[:, t, 0:1], rstd[:, t:t + 1], ALU.subtract, ALU.mult
                                            ).then_inc(xn_ready, 1)

            statistics(0)
            centre(0, 0)
            dve.wait_ge(bo_in, 16)
            nc.vector.tensor_scalar(bo[:], bo[:], OUT_SCALE, None, ALU.mult).then_inc(bo_scaled, 1)
            dve.wait_ge(policy_pe, 3)
            dve.wait_ge(policy_in, 64)
            chained(nc.vector.tensor_tensor(logits[:], ps_t[0][0:B, 32:32 + E], pb2[:], ALU.add))
            chained(nc.vector.tensor_reduce(neg_top[:], logits[:], AX.X, ALU.max, negate=True))
            dve.wait_ge(policy_act, 2)
            chained(nc.vector.reciprocal(inv_total[:], total[:]))
            chained(nc.vector.tensor_scalar(policy[:], exps[:], inv_total[:], None, ALU.mult))
            chained(nc.vector.tensor_reduce(top[:], policy[:], AX.X, ALU.max))
            dve.wait_ge(consts, 2)
            chained(nc.vector.scalar_tensor_tensor(winner[:], policy[:], top[:], countdown[:], ALU.is_equal, ALU.mult))
            chained(nc.vector.tensor_reduce(choice_f[:], winner[:], AX.X, ALU.max))
            nc.vector.tensor_scalar(choice[:], choice_f[:], -1.0, float(E), ALU.mult, ALU.add).then_inc(policy_dve, 1)

            for t in range(2):
                nc.vector.engine_nop().then_inc(x_done, 1)

            def output(b, t):
                dve.wait_ge(o_sum, b * 2 + (t + 1))
                if t == 0:
                    dve.wait_ge(residual, b * (NT + 1) + (NT + 1))
                nc.vector.scalar_tensor_tensor(tiles(b, 2 * t, 2).rearrange("p t n -> p (t n)"), ps_o[t][:], OUT_SCALE,
                                               tiles(b, 2 * t, 2).rearrange("p t n -> p (t n)"), ALU.mult, ALU.add
                                               ).then_inc(x_done, 1)

            def batch(b, par, first, last):
                if not last:
                    statistics(b + 1)
                    if not first:
                        dve.wait_ge(turned, b * KC)
                        dve.wait_ge(residual, b * (NT + 1))
                    centre(b + 1, 1 - par)
                if not first:
                    output(b - 1, 0)
                    output(b - 1, 1)

            batches(dve, batch)
            output(B - 1, 0)
            output(B - 1, 1)

        @block.scalar
        def _(act):
            act.wait_ge(policy_in, 64)
            act.wait_ge(policy_pe, 2)
            nc.scalar.activation(hiddenT[:], ps_t[0][:, 64:64 + B], ACT.Gelu, bias=pb1[:, 0:1]).then_inc(policy_act, 1)
            act.wait_ge(policy_dve, 7)
            nc.scalar.activation(exps[:], logits[:], ACT.Exp, bias=neg_top[:], accum_out=total[:]).then_inc(policy_act, 1)

            def transposed(bb, par):
                for c in range(KC):
                    act.wait_ge(turned, bb * KC + (c + 1))
                    nc.scalar.copy(xT[par][:, c, :], ps_t[c][:]).then_inc(xT_ready, 1)

            transposed(0, 0)

            def batch(b, par, first, last):
                for f in range(FC):
                    act.wait_ge(h_sum, b * FC + (f + 1))
                    if f == 0:
                        act.wait_ge(weights_in[par], (b - par) * 32 + 64)
                        if not first:
                            act.wait_ge(r_sum, b * KC)
                    nc.scalar.activation(hT[:, f, :], ps_h[f % 2][:], ACT.Gelu, bias=b1[par][:, f:f + 1]
                                         ).then_inc(hT_ready, 1)
                for c in range(KC):
                    act.wait_ge(r_sum, b * KC + (c + 1))
                    nc.scalar.activation(rT[par][:, c, :], ps_r[c][:], ACT.Identity, bias=b2[par][:, c:c + 1]
                                         ).then_inc(rT_ready, 1)
                if not last:
                    transposed(b + 1, 1 - par)

            batches(act, batch)

        @block.tensor
        def _(pe):
            pe.wait_ge(policy_dve, 4)
            for c in range(KC):
                mm = nc.tensor.transpose(ps_t[0][:, c * B:(c + 1) * B], last[:, c * P:(c + 1) * P], ident[0:B, 0:B])
            mm.then_inc(policy_pe, 1)
            pe.wait_ge(policy_dve, 5)
            pe.wait_ge(policy_in, 64)
            for c in range(KC):
                mm = nc.tensor.matmul(ps_t[0][:, 64:64 + B], pw1[:, c, :], lastT[:, c, :], start=(c == 0), stop=(c == KC - 1))
            mm.then_inc(policy_pe, 1)
            pe.wait_ge(policy_act, 1)
            nc.tensor.matmul(ps_t[0][0:B, 32:32 + E], hiddenT[:], pw2[:], start=True, stop=True).then_inc(policy_pe, 1)
            pe.wait_ge(policy_dve, 6)

            def transpose_x(bb, par):
                pe.wait_ge(xn_ready, bb * NT + NT)
                for c in range(KC):
                    if not (isinstance(bb, int) and bb == 0):
                        pe.wait_ge(xT_ready, (bb - 1) * KC + (c + 1))
                    for t in range(NT):
                        mm = nc.tensor.transpose(ps_t[c][:, t * P:(t + 1) * P], xn[par][:, t, c * P:(c + 1) * P], ident[:])
                    mm.then_inc(turned, 1)

            def up(b, par, first):
                pe.wait_ge(xT_ready, b * KC + KC)
                pe.wait_ge(weights_in[par], (b - par) * 32 + 64)
                for f in range(FC):
                    if not (first and f < 2):
                        pe.wait_ge(hT_ready, b * FC + (f - 1))
                    for c in range(KC):
                        mm = nc.tensor.matmul(ps_h[f % 2][:], w1[par][:, c, f * P:(f + 1) * P], xT[par][:, c, :],
                                              start=(c == 0), stop=(c == KC - 1))
                    mm.then_inc(h_sum, 1)

            def down(b, par, first):
                pe.wait_ge(hT_ready, b * FC + FC)
                for c in range(KC):
                    if not first:
                        pe.wait_ge(rT_ready, (b - 1) * KC + (c + 1))
                    for f in range(FC):
                        mm = nc.tensor.matmul(ps_r[c][:], w2[par][:, f, c * P:(c + 1) * P], hT[:, f, :],
                                              start=(f == 0), stop=(f == FC - 1))
                    mm.then_inc(r_sum, 1)

            def output(b, par):
                pe.wait_ge(rT_ready, b * KC + KC)
                for t in range(2):
                    pe.wait_ge(x_done, b * 2 + (t + 1))
                    for tt in range(2):
                        for c in range(KC):
                            mm = nc.tensor.matmul(ps_o[t][:, tt * D:(tt + 1) * D],
                                                  rT[par][:, c, (2 * t + tt) * P:(2 * t + tt + 1) * P], wo[:, c, :],
                                                  start=(c == 0), stop=(c == KC - 1))
                    mm.then_inc(o_sum, 1)

            transpose_x(0, 0)
            pe.wait_ge(wo_in, 16)

            def batch(b, par, first, last):
                up(b, par, first)
                if not first:
                    output(b - 1, 1 - par)
                down(b, par, first)
                if not last:
                    transpose_x(b + 1, 1 - par)

            batches(pe, batch)
            output(B - 1, (B - 1) % 2)


def sigmoid_attention(nc, io, x, ident):
    QUADS = NG * NT
    PV_LAG = 2
    ctx = ExitStack()
    with ctx:
        def sb(name, shape, dt=F32):
            return ctx.enter_context(nc.sbuf_tensor("c_" + name, shape, dt))

        def ps(name, shape, dt=F32):
            return ctx.enter_context(nc.psum_tensor("c_" + name, shape, dt))

        def sem(name):
            return ctx.enter_context(nc.semaphore("c_" + name))

        wq, wk, wv, wo = (sb(n, [P, KC, D]) for n in ("wq", "wk", "wv", "wo"))
        w_mean = sb("w_mean", [P, 2, KC * KC, HC])
        gq, bq, gk, bk, eps = (sb(n, [P, 1]) for n in ("gq", "bq", "gk", "bk", "eps"))
        bo = sb("bo", [P, D])
        average = sb("average", [P, 4, HC])
        spread = sb("spread", [P, HD, HC])
        ctxT = sb("ctxT", [P, KC, S])
        stats, moments = sb("stats", [P, NT, 6]), sb("moments", [P, NT, 2])
        var_eps, rstd, minus_half = sb("var_eps", [P, NT]), sb("rstd", [P, NT]), sb("minus_half", [P, NT])
        xn, xT = sb("xn", [P, NT, D]), sb("xT", [P, KC, S])
        proj, square = sb("proj", [P, 4, S]), sb("square", [P, 4, S])
        head_std, head_rstd = sb("head_std", [P, S]), sb("head_rstd", [P, S])
        rest = sb("rest", [P, 2, S])
        parts = sb("parts", [P, 2, 3, S], BF16)
        q_stack = [sb(f"q_stack{i}", [K_MASK, H, S], BF16) for i in range(2)]
        k_stack = [sb(f"k_stack{i}", [K_MASK, H, S], BF16) for i in range(2)]
        v_pad = [sb(f"v_pad{i}", [P, NT, HC, 2, 2 * HD]) for i in range(2)]
        probs = sb("probs", [P, NT, HG, S])
        oT = sb("oT", [P, KC, S])

        ps_score = [ps(f"score{i}", [P, S]) for i in range(HG)]
        ps_pv = [ps(f"pv{i}", [P, S]) for i in range(KC)]
        ps_a = ps("act", [P, S])
        ps_d = ps("dve", [P, S])

        w_in, ctx_in = sem("w_in"), sem("ctx_in")
        consts, v_consts, means, centred, eps_set = (sem("consts"), sem("v_consts"), sem("means"), sem("centred"),
                                                     sem("eps_set"))
        stats_ready, moments_ready, var_ready, rstd_ready, xn_ready = (
            sem("stats_ready"), sem("moments_ready"), sem("var_ready"), sem("rstd_ready"), sem("xn_ready"))
        a_ready, a_empty, d_ready, d_empty = sem("a_ready"), sem("a_empty"), sem("d_ready"), sem("d_empty")
        squared, head_rstd_ready, scaled = sem("squared"), sem("head_rstd_ready"), sem("scaled")
        part0, rest_ready, part1, part2 = sem("part0"), sem("rest_ready"), sem("part1"), sem("part2")
        stacked = [sem(f"stacked{i}") for i in range(2)]
        score_ready, probs_ready, pv_ready, ot_ready = (sem("score_ready"), sem("probs_ready"), sem("pv_ready"),
                                                        sem("ot_ready"))
        residual = sem("residual")

        def batches(eng, batch):
            batch(0, 0, True, False)
            with eng.Fori(0, (B - 2) // 2) as i:
                batch(i * 2 + 1, 1, False, False)
                batch(i * 2 + 2, 0, False, False)
            batch(B - 1, (B - 1) % 2, False, True)

        KEYS0, KEYS1, XT0, XT1, QUERIES0, QUERIES1, VARIANCES, V0, V1 = range(9)
        A_ITEMS = 9
        PROJ = ((KEYS0, False, 0), (KEYS1, False, 1), (QUERIES0, True, 0), (QUERIES1, True, 1))
        D_FIRST = ("std0", "std1", "std2", "std3")
        D_LATER = ("out0", "out1") + D_FIRST
        D_END = 2 * len(D_FIRST) + (B - 1) * len(D_LATER) - len(D_FIRST)

        def d_item(b, first, name):
            if first:
                return len(D_FIRST) + D_FIRST.index(name)
            return (b - 1) * len(D_LATER) + (2 * len(D_FIRST) + D_LATER.index(name))

        def head_of(g, hh):
            return HC * (g // 2) + 2 * hh + g % 2

        AT = {KEYS0: 0, KEYS1: 1, XT0: 2, XT1: 3, QUERIES0: 4, QUERIES1: 5, VARIANCES: 7, V0: 13, V1: 14}
        STD_AT = (9, 10, 11, 12)
        OUT_AT = (3, 5)

        block = ctx.enter_context(nc.Block())

        @block.sync
        def _(sp):
            def load(bb):
                sp.dma_start(ctxT[:], io["ctxT"][bass.ds(bb, 1)].rearrange("a (c p) n -> p (a c) n", p=P)
                             ).then_inc(ctx_in, 16)

            def stack(bb, par, k):
                _, is_q, c = PROJ[k]
                dst = (q_stack if is_q else k_stack)[par]
                for part, ready in enumerate((part0, part1, part2)):
                    sp.wait_ge(ready, bb * 4 + (k + 1))
                    for j in range(PAIRS):
                        if (Q_PARTS if is_q else K_PARTS)[j] == part:
                            sp.dma_start(dst[HD * j:HD * (j + 1), HC * c:HC * (c + 1), :],
                                         parts[:, k % 2, part, :]).then_inc(stacked[k % 2], 16)

            sp.dma_start(wk[:], io["swk"].rearrange("(c p) n -> p c n", p=P)).then_inc(w_in, 16)
            sp.dma_start(wq[:], io["swq"].rearrange("(c p) n -> p c n", p=P)).then_inc(w_in, 16)
            load(0)
            for dst, name in ((gq, "sgq"), (bq, "sbq"), (gk, "sgk"), (bk, "sbk")):
                sp.dma_start(dst[:], io[name]).then_inc(w_in, 16)
            sp.dma_start(wv[:], io["swv"].rearrange("(c p) n -> p c n", p=P)).then_inc(w_in, 16)
            sp.dma_start(wo[:], io["swp"].rearrange("(c p) n -> p c n", p=P)).then_inc(w_in, 16)
            sp.dma_start(bo[:], io["sbp"].to_broadcast([P, D])).then_inc(w_in, 16)
            for k in range(4):
                stack(0, 0, k)

            def batch(b, par, first, last):
                if not last:
                    sp.wait_ge(a_ready, b * A_ITEMS + A_ITEMS)
                    load(b + 1)
                    if not first:
                        sp.wait_ge(score_ready, b * 64)
                    for k in range(4):
                        stack(b + 1, 1 - par, k)

            batches(sp, batch)

        @block.scalar
        def _(act):
            def evacuate(bb, item):
                act.wait_ge(a_ready, bb * A_ITEMS + (item + 1))
                if item in (XT0, XT1):
                    nc.scalar.copy(xT[:, item - XT0, :], ps_a[:]).then_inc(a_empty, 1)
                elif item == VARIANCES:
                    nc.scalar.activation(head_std[:], ps_a[:], ACT.Sqrt, bias=eps[:, 0:1]).then_inc(a_empty, 1)
                elif item in (V0, V1):
                    raise ValueError(item)
                else:
                    k = [i[0] for i in PROJ].index(item)
                    if not (isinstance(bb, int) and bb == 0):
                        act.wait_ge(rest_ready, (bb - 1) * 4 + (k + 1))
                    nc.scalar.copy(proj[:, k, :], ps_a[:]).then_inc(squared, 1)
                    nc.scalar.activation(square[:, k, :], ps_a[:], ACT.Square).then_inc(a_empty, 1)

            def v_tiles(bb, par, t):
                act.wait_ge(a_ready, bb * A_ITEMS + (V0 + t + 1))
                for odd in range(2):
                    ins = nc.scalar.copy(
                        v_pad[par][:, 2 * t:2 * t + 2, :, odd, HD * odd:HD * (odd + 1)],
                        ps_a[:].rearrange("p (t h o d) -> p t h o d", t=2, h=HC, o=2)[:, :, :, odd, :])
                    ins.then_inc(squared if odd == 0 else a_empty, 1)

            act.wait_ge(eps_set, 1)
            act.wait_ge(v_consts, 4)
            for item in range(V0):
                evacuate(0, item)
            v_tiles(0, 0, 0), v_tiles(0, 0, 1)

            def batch(b, par, first, last):
                for u in range(QUADS):
                    kc = u % NT
                    quad = b * QUADS + u
                    for hh in range(HG):
                        act.wait_ge(score_ready, quad * HG + (hh + 1))
                        if hh == 0 and not (first and u < NT):
                            act.wait_ge(pv_ready, quad + (1 - NT))
                        nc.scalar.activation(probs[:, kc, hh, :], ps_score[hh][:], ACT.Sigmoid, scale=SCALE
                                             ).then_inc(probs_ready, 1)
                    if not last:
                        for item in range(V0):
                            if AT[item] == u:
                                evacuate(b + 1, item)
                        for t in range(2):
                            if AT[V0 + t] == u:
                                v_tiles(b + 1, 1 - par, t)

            batches(act, batch)

        @block.gpsimd
        def _(pool):
            nc.gpsimd.memset(minus_half[:], -0.5).then_inc(consts, 1)
            nc.gpsimd.iota(average[:], pattern=[[0, 4], [-1, HC]], base=P, channel_multiplier=1,
                           allow_small_or_imprecise_dtypes=True).then_inc(consts, 1)
            nc.gpsimd.iota(spread[:], pattern=[[0, HD], [-1, HC]], base=P, channel_multiplier=1,
                           allow_small_or_imprecise_dtypes=True).then_inc(consts, 1)

            def invert_deviation(bb):
                pool.wait_ge(var_ready, bb + 1)
                nc.gpsimd.tensor_tensor(rstd[:], var_eps[:], minus_half[:], ALU.pow).then_inc(rstd_ready, 1)

            def remainder(bb, k):
                pool.wait_ge(part0, bb * 4 + (k + 1))
                if k >= 2:
                    pool.wait_ge(part2, bb * 4 + (k - 1))
                nc.gpsimd.tensor_tensor(rest[:, k % 2, :], proj[:, k, :], parts[:, k % 2, 0, :], ALU.subtract
                                        ).then_inc(rest_ready, 1)

            def third(bb, k):
                pool.wait_ge(part1, bb * 4 + (k + 1))
                nc.gpsimd.tensor_tensor(parts[:, k % 2, 2, :], rest[:, k % 2, :], parts[:, k % 2, 1, :], ALU.subtract
                                        ).then_inc(part2, 1)

            def prepare(bb):
                invert_deviation(bb)
                for k in range(4):
                    remainder(bb, k)
                    third(bb, k)

            pool.wait_ge(consts, 3)
            prepare(0)

            def batch(b, par, first, last):
                for t in range(NT):
                    tile = x[:, bass.ds(b * NT + t, 1), :].rearrange("p a n -> p (a n)")
                    if t == 0:
                        pool.wait_ge(xn_ready, b * NT + NT)
                        pool.wait_ge(w_in, 16 * 9)
                    nc.gpsimd.tensor_tensor(tile, tile, bo[:], ALU.add).then_inc(residual, 1)
                if not last:
                    prepare(b + 1)

            batches(pool, batch)

        @block.vector
        def _(dve):
            def statistics(bb):
                for t in range(NT):
                    nc.vector.bn_stats(stats[:, t, :], x[:, bass.ds(bb * NT + t, 1), :].rearrange("p a n -> p (a n)")
                                       ).then_inc(stats_ready, 1)
                dve.wait_ge(stats_ready, bb * NT + NT)
                nc.vector.memset(var_eps[:], EPS).then_inc(moments_ready, 1)
                for t in range(NT):
                    nc.vector.bn_aggr(moments[:, t, :], stats[:, t, :]).then_inc(moments_ready, 1)
                dve.wait_ge(moments_ready, bb * (NT + 1) + (NT + 1))
                nc.vector.tensor_tensor(var_eps[:], moments[:, :, 1], var_eps[:], ALU.add).then_inc(var_ready, 1)

            def centre(bb):
                dve.wait_ge(rstd_ready, bb + 1)
                if not (isinstance(bb, int) and bb == 0):
                    dve.wait_ge(a_ready, (bb - 1) * A_ITEMS + (XT1 + 1))
                for t in range(NT):
                    nc.vector.tensor_scalar(xn[:, t, :], x[:, bass.ds(bb * NT + t, 1), :].rearrange("p a n -> p (a n)"),
                                            moments[:, t, 0:1], rstd[:, t:t + 1], ALU.subtract, ALU.mult
                                            ).then_inc(xn_ready, 1)

            def invert_std(bb):
                dve.wait_ge(a_empty, bb * A_ITEMS + (VARIANCES + 1))
                if not (isinstance(bb, int) and bb == 0):
                    dve.wait_ge(d_ready, (bb - 1) * len(D_LATER) + 4)
                nc.vector.reciprocal(head_rstd[:], head_std[:]).then_inc(head_rstd_ready, 1)

            def scale(bb, k, d):
                _, is_q, _ = PROJ[k]
                n = bb * 4 + k
                dve.wait_ge(d_ready, d + 1)
                nc.vector.tensor_tensor(proj[:, k, :], proj[:, k, :], ps_d[:], ALU.mult).then_inc(d_empty, 1)
                dve.wait_ge(d_empty, d + 1)
                nc.vector.tensor_scalar(proj[:, k, :], proj[:, k, :], (gq if is_q else gk)[:, 0:1],
                                        (bq if is_q else bk)[:, 0:1], ALU.mult, ALU.add).then_inc(scaled, 1)
                dve.wait_ge(scaled, n + 1)
                dve.wait_ge(stacked[k % 2], bb * 192 + 96 * (k // 2))
                nc.vector.tensor_copy(parts[:, k % 2, 0, :], proj[:, k, :]).then_inc(part0, 1)

            def second(bb, k):
                dve.wait_ge(rest_ready, bb * 4 + (k + 1))
                nc.vector.tensor_copy(parts[:, k % 2, 1, :], rest[:, k % 2, :]).then_inc(part1, 1)

            def heads_out(b, c):
                dve.wait_ge(pv_ready, b * QUADS + 8 * (c + 1))
                if not (isinstance(b, int) and b == 0) and c == 0:
                    dve.wait_ge(d_ready, (b - 1) * len(D_LATER) + (2 * len(D_FIRST) + 2))
                nc.vector.tensor_copy(oT[:, c, :], ps_pv[c][:]).then_inc(ot_ready, 1)

            def output(b, t, d):
                dve.wait_ge(d_ready, d + 1)
                dve.wait_ge(residual, b * NT + NT)
                two = x[:, bass.ds(b * NT + 2 * t, 2), :]
                nc.vector.tensor_tensor(two, ps_d[:].rearrange("p (t n) -> p t n", t=2), two, ALU.add).then_inc(d_empty, 1)

            for i in range(2):
                for odd in range(2):
                    nc.vector.memset(v_pad[i][:, :, :, odd, HD * (1 - odd):HD * (2 - odd)], 0.0).then_inc(v_consts, 1)
            nc.vector.memset(eps[:], EPS).then_inc(eps_set, 1)
            dve.wait_ge(w_in, 16 * 9)
            for i, w in enumerate((wk, wq)):
                by_head = w[:].rearrange("p c (k d h) -> p (c k) h d", d=HD, h=HC)
                nc.vector.tensor_reduce(w_mean[:, i], by_head, AX.X, ALU.add).then_inc(means, 1)
                dve.wait_ge(means, 2 * i + 1)
                nc.vector.tensor_scalar(w_mean[:, i], w_mean[:, i], 1.0 / HD, None, ALU.mult).then_inc(means, 1)
                dve.wait_ge(means, 2 * i + 2)
                for ck in range(KC * KC):
                    part = w[:, ck // KC, P * (ck % KC):P * (ck % KC + 1)].rearrange("p (d h) -> p d h", d=HD)
                    mean = w_mean[:, i, ck:ck + 1, :]
                    mean = bass.AP(mean.tensor, mean.offset, [mean.ap[0], [0, HD], [1, HC]])
                    nc.vector.tensor_tensor(part, part, mean, ALU.subtract).then_inc(centred, 1)
            dve.wait_ge(consts, 3)
            for i, (m, value) in enumerate(((average, 1.0 / HD), (spread, 1.0))):
                m32 = m[:].rearrange("p a h -> p (a h)")
                as_int = proj[:, 2 * i, 0:m32.shape[1]].bitcast(I32)
                nc.vector.tensor_copy(as_int, m32).then_inc(means, 1)
                dve.wait_ge(means, 5 + 3 * i)
                nc.vector.tensor_scalar(as_int, as_int, HC - 1, None, ALU.bitwise_and).then_inc(means, 1)
                dve.wait_ge(means, 6 + 3 * i)
                nc.vector.tensor_scalar(m32, as_int, 0.0, value, ALU.is_equal, ALU.mult).then_inc(means, 1)
            statistics(0)
            centre(0)
            invert_std(0)
            for k in range(4):
                scale(0, k, k)
                second(0, k)

            def batch(b, par, first, last):
                for u in range(QUADS):
                    if not last:
                        if u == 0:
                            statistics(b + 1)
                        if u == 1:
                            centre(b + 1)
                    if u == 2 and not first:
                        heads_out(b - 1, 1)
                    if u == 10:
                        heads_out(b, 0)
                    if not last and u == AT[VARIANCES] + 1:
                        invert_std(b + 1)
                    for t in range(2):
                        if not first and u == OUT_AT[t]:
                            output(b - 1, t, d_item(b, first, f"out{t}"))
                    for k in range(4):
                        if not last and u == STD_AT[k]:
                            scale(b + 1, k, d_item(b, first, f"std{k}"))
                            second(b + 1, k)

            batches(dve, batch)
            heads_out(B - 1, 1)
            for t in range(2):
                output(B - 1, t, D_END + t)

        @block.tensor
        def _(pe):
            def take_act(bb, item):
                if not (isinstance(bb, int) and bb * A_ITEMS + item == 0):
                    pe.wait_ge(a_empty, bb * A_ITEMS + item)

            def prepare(bb, item):
                take_act(bb, item)
                if item in (XT0, XT1):
                    c = item - XT0
                    pe.wait_ge(xn_ready, bb * NT + NT)
                    for t in range(NT):
                        mm = nc.tensor.transpose(ps_a[:, t * P:(t + 1) * P], xn[:, t, c * P:(c + 1) * P], ident[:])
                elif item == VARIANCES:
                    for k in range(4):
                        mm = nc.tensor.matmul(ps_a[32 * k:32 * k + 32, :], average[:].rearrange("p a h -> p (a h)"),
                                              square[:, k, :], start=True, stop=True, tile_position=(0, 32 * k))
                elif item in (V0, V1):
                    for tt in range(2):
                        for kk in range(KC):
                            at = 2 * (item - V0) + tt
                            mm = nc.tensor.matmul(ps_a[:, tt * D:(tt + 1) * D], ctxT[:, kk, at * P:(at + 1) * P],
                                                  wv[:, kk, :], start=(kk == 0), stop=(kk == KC - 1))
                else:
                    _, is_q, c = PROJ[[i[0] for i in PROJ].index(item)]
                    if not is_q:
                        pe.wait_ge(ctx_in, (bb + 1) * 16)
                    for kk in range(KC):
                        mm = nc.tensor.matmul(ps_a[:], (wq if is_q else wk)[:, kk, c * P:(c + 1) * P],
                                              (xT if is_q else ctxT)[:, kk, :], start=(kk == 0), stop=(kk == KC - 1))
                mm.then_inc(a_ready, 1)

            def spread_deviations(bb, k, d):
                pe.wait_ge(head_rstd_ready, bb + 1)
                if not (isinstance(d, int) and d == 0):
                    pe.wait_ge(d_empty, d)
                nc.tensor.matmul(ps_d[:], spread[32 * k:32 * k + HC].rearrange("p a h -> p (a h)"),
                                 head_rstd[32 * k:32 * k + HC, :], start=True, stop=True,
                                 tile_position=(32 * k, 0)).then_inc(d_ready, 1)

            def scores(b, par, u, hh):
                g, kc = divmod(u, NT)
                n = b * 64 + (4 * u + hh)
                h = head_of(g, hh)
                if u == 0 and hh == 0:
                    for i in range(2):
                        pe.wait_ge(stacked[i], b * 192 + 192)
                if not (isinstance(n, int) and n < HG):
                    pe.wait_ge(probs_ready, n + (1 - HG))
                nc.tensor.matmul(ps_score[hh][:], k_stack[par][:, h, kc * P:(kc + 1) * P], q_stack[par][:, h, :],
                                 start=True, stop=True).then_inc(score_ready, 1)

            def weighted_values(b, par, w):
                g, kc = divmod(w, NT)
                c, odd = divmod(g, 2)
                pe.wait_ge(probs_ready, b * 64 + (4 * w + 4))
                if w == 0:
                    pe.wait_ge(a_empty, b * A_ITEMS + A_ITEMS)
                if kc == 0 and odd == 0 and not (isinstance(b, int) and b == 0):
                    pe.wait_ge(ot_ready, b * KC + (c - 1))
                for hh in range(HG):
                    mm = nc.tensor.matmul(ps_pv[c][32 * hh:32 * hh + 32, :], v_pad[par][:, kc, HG * c + hh, odd, :],
                                          probs[:, kc, hh, :], start=(kc == 0 and odd == 0),
                                          stop=(kc == NT - 1 and odd == 1), tile_position=(0, 32 * hh))
                mm.then_inc(pv_ready, 1)

            def output(b, t, d):
                pe.wait_ge(ot_ready, b * KC + KC)
                pe.wait_ge(d_empty, d)
                for tt in range(2):
                    for c in range(KC):
                        mm = nc.tensor.matmul(ps_d[:, tt * D:(tt + 1) * D], oT[:, c, (2 * t + tt) * P:(2 * t + tt + 1) * P],
                                              wo[:, c, :], start=(c == 0), stop=(c == KC - 1))
                mm.then_inc(d_ready, 1)

            pe.wait_ge(w_in, 16 * 9)
            pe.wait_ge(centred, 2 * KC * KC)
            pe.wait_ge(means, 10)
            for item in range(A_ITEMS):
                prepare(0, item)
            for k in range(4):
                spread_deviations(0, k, k)

            def batch(b, par, first, last):
                for u in range(QUADS):
                    for half in range(2):
                        for hh in (2 * half, 2 * half + 1):
                            scores(b, par, u, hh)
                        if half == 0 and u >= PV_LAG:
                            weighted_values(b, par, u - PV_LAG)
                        elif half == 0 and not first:
                            weighted_values(b - 1, 1 - par, QUADS + u - PV_LAG)
                    for t in range(2):
                        if not first and u == OUT_AT[t]:
                            output(b - 1, t, d_item(b, first, f"out{t}"))
                    if not last:
                        for item in range(A_ITEMS):
                            if AT[item] == u:
                                prepare(b + 1, item)
                        for k in range(4):
                            if STD_AT[k] == u:
                                spread_deviations(b + 1, k, d_item(b, first, f"std{k}"))

            batches(pe, batch)
            for w in range(QUADS - PV_LAG, QUADS):
                weighted_values(B - 1, (B - 1) % 2, w)
            for t in range(2):
                output(B - 1, t, D_END + t)


def mixture(nc, io, x, ident, out):
    E, F = 8, 4 * D
    FC = F // P
    T = B * NT
    N = T * P
    CAP = -(-(N // E * 5) // 4)
    CT = CAP // P
    HALF = CAP // 2
    LOW = -3.0e38
    PAYLOADS = 6
    assert CT * P == CAP
    n_rows = nc.dram_tensor("n_rows", [N + CAP, D], F32, kind="Internal").ap()
    sum_rows = nc.dram_tensor("sum_rows", [N + CAP, D], F32, kind="Internal").ap()
    outer = ExitStack()
    with outer:
        place = outer.enter_context(nc.sbuf_tensor("d_place", [P, E, CT], I32))
        gate = outer.enter_context(nc.sbuf_tensor("d_gate", [P, E, CT], F32))
        gamma = outer.enter_context(nc.sbuf_tensor("d_gamma", [P, D], F32))
        beta = outer.enter_context(nc.sbuf_tensor("d_beta", [P, D], F32))
        w1 = [outer.enter_context(nc.sbuf_tensor(f"d_w1_{i}", [P, KC, F], F32)) for i in range(2)]
        w2 = [outer.enter_context(nc.sbuf_tensor(f"d_w2_{i}", [P, FC, D], F32)) for i in range(2)]
        b1 = outer.enter_context(nc.sbuf_tensor("d_b1", [P, E, FC], F32))
        minus_half = outer.enter_context(nc.sbuf_tensor("d_minus_half", [P, T], F32))
        weights_in = [outer.enter_context(nc.semaphore(f"d_weights_in{i}")) for i in range(2)]
        small_in = outer.enter_context(nc.semaphore("d_small_in"))
        route(nc, io, x, ident, n_rows, sum_rows, place, gate, gamma, beta, w1, w2, b1, minus_half, weights_in,
              small_in, E, F, FC, T, N, CAP, CT, LOW, PAYLOADS)
        experts(nc, io, x, ident, n_rows, sum_rows, place, gate, gamma, beta, w1, w2, b1, minus_half, weights_in,
                E, F, FC, T, N, CAP, CT, HALF, out)


def load_expert(sp, io, e, w1, w2, weights_in):
    sp.dma_start(w1[:], io["mw1"][bass.ds(e, 1)].rearrange("a (c p) f -> p (a c) f", p=P)).then_inc(weights_in, 16)
    sp.dma_start(w2[:], io["mw2"][bass.ds(e, 1)].rearrange("a (c p) f -> p (a c) f", p=P)).then_inc(weights_in, 16)


def route(nc, io, x, ident, n_rows, sum_rows, place, gate, gamma, beta, w1, w2, b1, minus_half, weights_in,
          small_in, E, F, FC, T, N, CAP, CT, LOW, PAYLOADS):
    ctx = ExitStack()
    with ctx:
        def sb(name, shape, dt=F32):
            return ctx.enter_context(nc.sbuf_tensor("r_" + name, shape, dt))

        def ps(name, shape, dt=F32):
            return ctx.enter_context(nc.psum_tensor("r_ps_" + name, shape, dt))

        def sem(name):
            return ctx.enter_context(nc.semaphore("r_" + name))

        wr, br = sb("wr", [P, KC, E]), sb("br", [P, E])
        zeros = sb("zeros", [P, CT, D])
        stats, moments = sb("stats", [P, T, 6]), sb("moments", [P, T, 2])
        var_eps, rstd = sb("var_eps", [P, T]), sb("rstd", [P, T])
        xn = [sb(f"xn{i}", [P, NT, D]) for i in range(2)]
        xT = sb("xT", [P, KC, S])
        logits, work, work2, first, second, key = (sb(n, [P, E, T]) for n in ("logits", "work", "work2", "first", "second", "key"))
        countdown = sb("countdown", [P, E])
        v1, v2, w_first, w_second = (sb(n, [P, T]) for n in ("v1", "v2", "w_first", "w_second"))
        threshold, step, candidate, enough = (sb(n, [P, E], I32) for n in ("threshold", "step", "candidate", "enough"))
        count = sb("count", [P, E], BF16)
        needed = sb("needed", [P, E])
        marks = sb("marks", [P, E, T], BF16)
        keep_state = sb("keep_state", [P, E, T])
        ahead = sb("ahead", [P, E, T])
        ones, before = sb("ones", [P, P], BF16), sb("before", [P, P], BF16)
        slot, row, lane = sb("slot", [P, E, T]), sb("row", [P, E, T]), sb("lane", [P, E, T])
        gate_parts, gate_rest = sb("gate_parts", [P, 3, E, T], BF16), sb("gate_rest", [P, E, T])
        lanes = sb("lanes", [P, P])
        rows_of = sb("rows_of", [P, CT])
        numbers = sb("numbers", [P, 2, T])
        spare = sb("spare", [P, CT])
        lane_hot = [sb(f"lane_hot{i}", [P, T, P], BF16) for i in range(2)]
        row_hot = [sb(f"row_hot{i}", [P, T, PAYLOADS, CT], BF16) for i in range(2)]
        filled = sb("filled", [P, PAYLOADS, CT])
        index = sb("index", [P, 3, CT])

        ps_t = [ps(f"t{i}", [P, S]) for i in range(KC)]
        ps_l = [ps(f"l{i}", [P, S]) for i in range(2)]
        ps_count = ps("count", [P, S])
        ps_before, ps_total = ps("before", [P, S]), ps("total", [P, S])
        ps_slots = ps("slots", [P, S])

        wr_in, consts = sem("wr_in"), sem("consts")
        stats_ready, moments_ready, var_ready, rstd_ready, xn_ready = (
            sem("stats_ready"), sem("moments_ready"), sem("var_ready"), sem("rstd_ready"), sem("xn_ready"))
        rows_out = [sem(f"rows_out{i}") for i in range(2)]
        spare_out = sem("spare_out")
        turned, xT_ready, scored, logits_ready = sem("turned"), sem("xT_ready"), sem("scored"), sem("logits_ready")
        chain, exp_ready, search, counted = sem("chain"), sem("exp_ready"), sem("search"), sem("counted")
        marked, prefixed = sem("marked"), sem("prefixed")
        hot_ready, slots_ready, slots_read = sem("hot_ready"), sem("slots_ready"), sem("slots_read")
        beta_added = sem("beta_added")

        def over_tiles(ap):
            return bass.AP(ap.tensor, ap.offset, [ap.ap[0], [1, E], [0, T]])

        def over_experts(ap):
            return bass.AP(ap.tensor, ap.offset, [ap.ap[0], [0, E], [1, T]])

        block = ctx.enter_context(nc.Block())

        @block.sync
        def _(sp):
            sp.dma_start(wr[:], io["mwr"].rearrange("(c p) n -> p c n", p=P)).then_inc(wr_in, 16)
            sp.dma_start(br[:], io["mbr"].to_broadcast([P, E])).then_inc(wr_in, 16)
            sp.dma_start(gamma[:], io["mgamma"].to_broadcast([P, D])).then_inc(small_in, 16)
            sp.dma_start(beta[:], io["mbeta"].to_broadcast([P, D])).then_inc(small_in, 16)
            sp.dma_start(b1[:], io["mb1"].rearrange("e p c -> p e c")).then_inc(small_in, 16)
            sp.wait_ge(consts, 1)
            for rows in (n_rows, sum_rows):
                sp.dma_start(rows[N:N + CAP, :].rearrange("(t p) d -> p t d", p=P), zeros[:]).then_inc(spare_out, 16)
            for b in range(B):
                sp.wait_ge(xn_ready, NT * (b + 1))
                for rows in (n_rows, sum_rows):
                    sp.dma_start(rows[b * S:(b + 1) * S, :].rearrange("(t p) d -> p t d", p=P), xn[b % 2][:]
                                 ).then_inc(rows_out[b % 2], 16)
            for e in range(2):
                load_expert(sp, io, e, w1[e], w2[e], weights_in[e])
            sp.wait_ge(spare_out, 32)
            for i in range(2):
                sp.wait_ge(rows_out[i], 32 * (B // 2))

        @block.gpsimd
        def _(pool):
            def const(ins):
                const.n += 1
                ins.then_inc(consts, 1)
                pool.wait_ge(consts, const.n)
            const.n = 0
            fine = dict(allow_small_or_imprecise_dtypes=True)
            const(nc.gpsimd.memset(zeros[:], 0.0))
            const(nc.gpsimd.memset(minus_half[:], -0.5))
            const(nc.gpsimd.iota(countdown[:], pattern=[[-1, E]], base=E, channel_multiplier=0, **fine))
            const(nc.gpsimd.iota(lanes[:], pattern=[[1, P]], base=0, channel_multiplier=0, **fine))
            const(nc.gpsimd.iota(rows_of[:], pattern=[[1, CT]], base=0, channel_multiplier=0, **fine))
            const(nc.gpsimd.iota(numbers[:, 0, :], pattern=[[1, T]], base=0, channel_multiplier=0, **fine))
            const(nc.gpsimd.iota(numbers[:, 1, :], pattern=[[0, T]], base=0, channel_multiplier=1, **fine))
            const(nc.gpsimd.iota(spare[:], pattern=[[P, CT]], base=N, channel_multiplier=1, **fine))
            const(nc.gpsimd.memset(ones[:], 1.0))
            const(nc.gpsimd.memset(before[:], 1.0))
            const(nc.gpsimd.affine_select(out=before[:], in_=before[:], compare_op=ALU.is_ge, fill=0.0, base=-1,
                                          pattern=[[1, P]], channel_multiplier=-1))
            const(nc.gpsimd.memset(keep_state[:], 1.0))
            const(nc.gpsimd.memset(keep_state[:, :, 0], 0.0))
            pool.wait_ge(var_ready, 1)
            nc.gpsimd.tensor_tensor(rstd[:], var_eps[:], minus_half[:], ALU.pow).then_inc(rstd_ready, 1)
            pool.wait_ge(xn_ready, NT * B)
            pool.wait_ge(small_in, 48)
            with pool.Fori(0, T) as t:
                tile = x[:, bass.ds(t, 1), :].rearrange("p a n -> p (a n)")
                nc.gpsimd.tensor_tensor(tile, tile, beta[:], ALU.add).then_inc(beta_added, 1)

        @block.scalar
        def _(act):
            for b in range(B):
                for c in range(KC):
                    act.wait_ge(turned, b * KC + c + 1)
                    if b > 0 and c == 0:
                        act.wait_ge(scored, b)
                    nc.scalar.copy(xT[:, c, :], ps_t[c][:]).then_inc(xT_ready, 1)
            act.wait_ge(chain, 12)
            nc.scalar.activation(v2[:], v2[:], ACT.Exp).then_inc(exp_ready, 1)

        @block.vector
        def _(dve):
            class Chain:
                def __init__(self, sem, base=0):
                    self.sem, self.base, self.n = sem, base, 0

                def __call__(self, ins):
                    self.n += 1
                    ins.then_inc(self.sem, 1)
                    dve.wait_ge(self.sem, self.base + self.n)

                def beside(self, ins):
                    self.n += 1
                    ins.then_inc(self.sem, 1)

            V = nc.vector
            for t in range(T):
                V.bn_stats(stats[:, t, :], x[:, t, :]).then_inc(stats_ready, 1)
            dve.wait_ge(stats_ready, T)
            for t in range(T):
                V.bn_aggr(moments[:, t, :], stats[:, t, :]).then_inc(moments_ready, 1)
            dve.wait_ge(moments_ready, T)
            V.tensor_scalar(var_eps[:], moments[:, :, 1], EPS, None, ALU.add).then_inc(var_ready, 1)
            dve.wait_ge(rstd_ready, 1)
            for b in range(B):
                if b >= 2:
                    dve.wait_ge(rows_out[b % 2], 32 * (b // 2))
                    dve.wait_ge(turned, KC * (b - 1))
                for t in range(NT):
                    V.tensor_scalar(xn[b % 2][:, t, :], x[:, b * NT + t, :], moments[:, b * NT + t, 0:1],
                                    rstd[:, b * NT + t:b * NT + t + 1], ALU.subtract, ALU.mult).then_inc(xn_ready, 1)
                if b == 0:
                    dve.wait_ge(wr_in, 32)
                    dve.wait_ge(consts, 13)
                else:
                    score_out = b - 1
                    dve.wait_ge(scored, b)
                    V.tensor_tensor(logits[:, :, score_out * NT:b * NT].rearrange("p e t -> p t e"),
                                    ps_l[score_out % 2][:, 0:NT * E].rearrange("p (t e) -> p t e", t=NT),
                                    bass.AP(br[:].tensor, br[:].offset, [br[:].ap[0], [0, NT], [1, E]]), ALU.add
                                    ).then_inc(logits_ready, 1)
            dve.wait_ge(scored, B)
            V.tensor_tensor(logits[:, :, (B - 1) * NT:].rearrange("p e t -> p t e"),
                            ps_l[(B - 1) % 2][:, 0:NT * E].rearrange("p (t e) -> p t e", t=NT),
                            bass.AP(br[:].tensor, br[:].offset, [br[:].ap[0], [0, NT], [1, E]]), ALU.add
                            ).then_inc(logits_ready, 1)
            dve.wait_ge(logits_ready, B)

            by_token = "p e t -> p t e"
            step_of = Chain(chain)
            rank = bass.AP(countdown[:].tensor, countdown[:].offset, [countdown[:].ap[0], [1, E], [0, T]])

            def best(values, value, hot):
                step_of(V.tensor_tensor(work[:], values[:], over_experts(value[:]), ALU.is_equal))
                step_of(V.tensor_tensor(work[:], work[:], rank, ALU.mult))
                step_of(V.tensor_reduce(w_first[:], work[:].rearrange(by_token), AX.X, ALU.max))
                step_of(V.tensor_tensor(hot[:], work[:], over_experts(w_first[:]), ALU.is_equal))

            step_of(V.tensor_reduce(v1[:], logits[:].rearrange(by_token), AX.X, ALU.max))
            best(logits, v1, first)
            step_of(V.tensor_scalar(work[:], first[:], -1.0, 1.0, ALU.mult, ALU.add))
            step_of(V.tensor_tensor(work2[:], logits[:], work[:], ALU.mult))
            step_of(V.scalar_tensor_tensor(work2[:].rearrange("p e t -> p (e t)"), first[:].rearrange("p e t -> p (e t)"),
                                           LOW, work2[:].rearrange("p e t -> p (e t)"), ALU.mult, ALU.add))
            step_of(V.tensor_reduce(v2[:], work2[:].rearrange(by_token), AX.X, ALU.max))
            step_of(V.tensor_tensor(work[:], work2[:], over_experts(v2[:]), ALU.is_equal))
            step_of(V.tensor_tensor(work[:], work[:], rank, ALU.mult))
            step_of(V.tensor_tensor(v2[:], v2[:], v1[:], ALU.subtract))
            step_of(V.tensor_reduce(w_first[:], work[:].rearrange(by_token), AX.X, ALU.max))
            step_of(V.tensor_tensor(second[:], work[:], over_experts(w_first[:]), ALU.is_equal))
            dve.wait_ge(exp_ready, 1)
            step_of(V.tensor_scalar(v1[:], v2[:], 1.0, None, ALU.add))
            step_of(V.reciprocal(w_first[:], v1[:]))
            step_of(V.tensor_tensor(w_second[:], v2[:], w_first[:], ALU.mult))
            step_of(V.tensor_tensor(key[:], first[:], over_experts(w_first[:]), ALU.mult))
            step_of(V.tensor_tensor(work[:], second[:], over_experts(w_second[:]), ALU.mult))
            step_of(V.tensor_tensor(key[:], key[:], work[:], ALU.add))
            step_of(V.tensor_tensor(work[:], first[:], second[:], ALU.add))
            step_of(V.tensor_scalar(work[:], work[:], -1.0, None, ALU.add))
            step_of(V.tensor_tensor(key[:], key[:], work[:], ALU.add))
            step_of(V.memset(threshold[:], 0))
            step_of(V.memset(step[:], 1 << 29))

            ctx.enter_context(nc.allow_low_precision(reason="counts of at most 32 tiles are whole in bf16"))
            BITS = 30
            with dve.Fori(0, BITS) as i:
                bit = Chain(search, i * 6)
                bit(V.tensor_tensor(candidate[:], threshold[:], step[:], ALU.bitwise_or))
                bit(V.tensor_tensor(work[:], key[:], over_tiles(candidate[:].bitcast(F32)), ALU.is_ge))
                bit(V.tensor_reduce(count[:], work[:], AX.X, ALU.add))
                dve.wait_ge(counted, i + 1)
                bit(V.tensor_scalar(enough[:], ps_count[:, 0:E], float(CAP), None, ALU.is_ge))
                bit.beside(V.tensor_scalar(step[:], step[:], 1, None, ALU.logical_shift_right))
                bit(V.copy_predicated(threshold[:], enough[:], candidate[:]))

            limit = over_tiles(threshold[:].bitcast(F32))
            step_of(V.tensor_tensor(first[:], key[:], limit, ALU.is_gt))
            step_of(V.tensor_reduce(count[:], first[:], AX.X, ALU.add))
            step_of(V.tensor_tensor(second[:], key[:], limit, ALU.is_equal))
            dve.wait_ge(counted, BITS)
            step_of(V.tensor_copy(marks[:], second[:]))
            V.engine_nop().then_inc(marked, 1)
            dve.wait_ge(counted, BITS + 1)
            step_of(V.tensor_scalar(needed[:], ps_count[:, 0:E], -1.0, float(CAP), ALU.mult, ALU.add))

            def positions(n):
                dve.wait_ge(prefixed, n)
                step_of(V.tensor_tensor_scan(ahead[:].rearrange("p e t -> p (e t)"), keep_state[:].rearrange("p e t -> p (e t)"),
                                             ps_total[:, 0:E * T], 0.0, ALU.mult, ALU.add))
                step_of(V.tensor_tensor(ahead[:].rearrange("p e t -> p (e t)"), ahead[:].rearrange("p e t -> p (e t)"),
                                        ps_total[:, 0:E * T], ALU.subtract))
                step_of(V.tensor_tensor(slot[:].rearrange("p e t -> p (e t)"), ahead[:].rearrange("p e t -> p (e t)"),
                                        ps_before[:, 0:E * T], ALU.add))

            positions(1)
            step_of(V.tensor_tensor(work[:], slot[:], over_tiles(needed[:]), ALU.is_lt))
            step_of(V.tensor_tensor(work[:], work[:], second[:], ALU.mult))
            step_of(V.tensor_tensor(first[:], first[:], work[:], ALU.add))
            step_of(V.tensor_copy(marks[:], first[:]))
            V.engine_nop().then_inc(marked, 1)
            positions(2)
            step_of(V.tensor_scalar(row[:], slot[:], float(P), None, ALU.is_ge))
            for k in range(2, CT):
                step_of(V.tensor_scalar(work[:], slot[:], float(k * P), None, ALU.is_ge))
                step_of(V.tensor_tensor(row[:], row[:], work[:], ALU.add))
            flat = "p e t -> p (e t)"
            step_of(V.scalar_tensor_tensor(lane[:].rearrange(flat), row[:].rearrange(flat), -float(P),
                                           slot[:].rearrange(flat), ALU.mult, ALU.add))
            step_of(V.scalar_tensor_tensor(lane[:].rearrange(flat), lane[:].rearrange(flat), 1.0,
                                           first[:].rearrange(flat), ALU.add, ALU.mult))
            step_of(V.tensor_scalar(lane[:], lane[:], -1.0, None, ALU.add))
            step_of(V.tensor_copy(gate_parts[:, 0], key[:]))
            step_of(V.tensor_tensor(gate_rest[:], key[:], gate_parts[:, 0], ALU.subtract))
            step_of(V.tensor_copy(gate_parts[:, 1], gate_rest[:]))
            step_of(V.tensor_tensor(gate_parts[:, 2], gate_rest[:], gate_parts[:, 1], ALU.subtract))

            def one_hot(e):
                if e >= 2:
                    dve.wait_ge(slots_ready, e - 1)
                lane_e, row_e = lane[:, e, :], row[:, e, :]
                V.tensor_tensor(lane_hot[e % 2][:], bass.AP(lanes[:].tensor, lanes[:].offset, [lanes[:].ap[0], [0, T], [1, P]]),
                                bass.AP(lane_e.tensor, lane_e.offset, [lane_e.ap[0], [1, T], [0, P]]), ALU.is_equal
                                ).then_inc(hot_ready, 1)
                hot = row_hot[e % 2]
                step_of(V.tensor_tensor(hot[:, :, 0, :], bass.AP(rows_of[:].tensor, rows_of[:].offset,
                                                                [rows_of[:].ap[0], [0, T], [1, CT]]),
                                        bass.AP(row_e.tensor, row_e.offset, [row_e.ap[0], [1, T], [0, CT]]), ALU.is_equal))
                for j in range(1, PAYLOADS):
                    load = numbers[:, j - 1, :] if j < 3 else gate_parts[:, j - 3, e, :]
                    V.tensor_tensor(hot[:, :, j, :], hot[:, :, 0, :],
                                    bass.AP(load.tensor, load.offset, [load.ap[0], [1, T], [0, CT]]), ALU.mult
                                    ).then_inc(hot_ready, 1)

            def read_slots(e):
                dve.wait_ge(slots_ready, e + 1)
                step_of(V.tensor_copy(filled[:], ps_slots[:, 0:PAYLOADS * CT].rearrange("p (j c) -> p j c", j=PAYLOADS)))
                V.engine_nop().then_inc(slots_read, 1)
                step_of(V.tensor_tensor(index[:, 2, :], filled[:, 3, :], filled[:, 4, :], ALU.add))
                step_of(V.tensor_tensor(gate[:, e, :], index[:, 2, :], filled[:, 5, :], ALU.add))
                step_of(V.scalar_tensor_tensor(index[:, 0, :], filled[:, 1, :], float(P), filled[:, 2, :], ALU.mult, ALU.add))
                step_of(V.tensor_tensor(index[:, 1, :], filled[:, 0, :], spare[:], ALU.mult))
                step_of(V.tensor_tensor(index[:, 1, :], spare[:], index[:, 1, :], ALU.subtract))
                step_of(V.tensor_tensor(place[:, e, :], index[:, 0, :], index[:, 1, :], ALU.add))

            for e in range(E):
                one_hot(e)
                if e >= 1:
                    read_slots(e - 1)
            read_slots(E - 1)

        @block.tensor
        def _(pe):
            pe.wait_ge(wr_in, 32)

            def transpose_x(b):
                pe.wait_ge(xn_ready, NT * (b + 1))
                for c in range(KC):
                    if b > 0:
                        pe.wait_ge(xT_ready, (b - 1) * KC + c + 1)
                    for t in range(NT):
                        mm = nc.tensor.transpose(ps_t[c][:, t * P:(t + 1) * P], xn[b % 2][:, t, c * P:(c + 1) * P], ident[:])
                    mm.then_inc(turned, 1)

            transpose_x(0)
            for b in range(B):
                pe.wait_ge(xT_ready, (b + 1) * KC)
                if b >= 2:
                    pe.wait_ge(logits_ready, b - 1)
                for t in range(NT):
                    for c in range(KC):
                        mm = nc.tensor.matmul(ps_l[b % 2][:, t * E:(t + 1) * E], xT[:, c, t * P:(t + 1) * P], wr[:, c, :],
                                              start=(c == 0), stop=(c == KC - 1))
                mm.then_inc(scored, 1)
                if b + 1 < B:
                    transpose_x(b + 1)
            with pe.Fori(0, 30) as i:
                pe.wait_ge(search, i * 6 + 3)
                nc.tensor.matmul(ps_count[:, 0:E], ones[:], count[:], start=True, stop=True).then_inc(counted, 1)
            pe.wait_ge(search, 30 * 6)
            for n in range(2):
                pe.wait_ge(marked, n + 1)
                if n == 0:
                    nc.tensor.matmul(ps_count[:, 0:E], ones[:], count[:], start=True, stop=True).then_inc(counted, 1)
                nc.tensor.matmul(ps_before[:, 0:E * T], before[:], marks[:].rearrange("p e t -> p (e t)"), start=True, stop=True)
                nc.tensor.matmul(ps_total[:, 0:E * T], ones[:], marks[:].rearrange("p e t -> p (e t)"), start=True, stop=True
                                 ).then_inc(prefixed, 1)
            for e in range(E):
                pe.wait_ge(hot_ready, PAYLOADS * (e + 1))
                if e > 0:
                    pe.wait_ge(slots_read, e)
                for t in range(T):
                    mm = nc.tensor.matmul(ps_slots[:, 0:PAYLOADS * CT], lane_hot[e % 2][:, t, :],
                                          row_hot[e % 2][:, t].rearrange("p j c -> p (j c)"), start=(t == 0), stop=(t == T - 1))
                mm.then_inc(slots_ready, 1)


def experts(nc, io, x, ident, n_rows, sum_rows, place, gate, gamma, beta, w1, w2, b1, minus_half, weights_in,
            E, F, FC, T, N, CAP, CT, HALF, out):
    ctx = ExitStack()
    with ctx:
        def sb(name, shape, dt=F32):
            return ctx.enter_context(nc.sbuf_tensor("e_" + name, shape, dt))

        def ps(name, shape, dt=F32):
            return ctx.enter_context(nc.psum_tensor("e_ps_" + name, shape, dt))

        def sem(name):
            return ctx.enter_context(nc.semaphore("e_" + name))

        b2 = sb("b2", [P, 2, D])
        xe = [sb(f"xe{i}", [P, CT, D]) for i in range(2)]
        xT = [sb(f"xT{i}", [P, KC, CAP]) for i in range(2)]
        hT = sb("hT", [P, FC, CAP])
        y = [sb(f"y{i}", [P, CT, D]) for i in range(2)]
        raw = sb("raw", [P, 2, D])
        total = [sb(f"total{i}", [P, NT, D]) for i in range(2)]
        stats, moments = sb("stats", [P, T, 6]), sb("moments", [P, T, 2])
        var_eps, rstd = sb("var_eps", [P, T]), sb("rstd", [P, T])
        ps_t = [ps(f"t{i}", [P, S]) for i in range(2)]
        ps_h = [ps(f"h{i}", [P, 2, S]) for i in range(2)]
        ps_y = [ps(f"y{i}", [P, S]) for i in range(2)]

        b2_in, added, total_in, stored = sem("b2_in"), sem("added"), [sem(f"total_in{i}") for i in range(2)], sem("stored")
        gathered = [sem(f"gathered{i}") for i in range(2)]
        turned, xT_ready, h_sum, hT_ready, y_sum, biased, y_ready = (
            sem("turned"), sem("xT_ready"), sem("h_sum"), sem("hT_ready"), sem("y_sum"), sem("biased"), sem("y_ready"))
        stats_ready, moments_ready, var_ready, rstd_ready, done, scaled_by = (
            sem("stats_ready"), sem("moments_ready"), sem("var_ready"), sem("rstd_ready"), sem("done"), sem("scaled_by"))

        block = ctx.enter_context(nc.Block())

        @block.sync
        def _(sp):
            for e in range(E):
                if e >= 2:
                    sp.wait_ge(y_ready, CT * (e - 1))
                    load_expert(sp, io, e, w1[e % 2], w2[e % 2], weights_in[e % 2])
                    sp.wait_ge(biased, CT * (e - 1))
                sp.dma_start(b2[:, e % 2, :], io["mb2"][e:e + 1, :].to_broadcast([P, D])).then_inc(weights_in[e % 2], 16)
            sp.wait_ge(added, 16 * CT * E)
            for b in range(B):
                if b >= 2:
                    sp.wait_ge(stored, 16 * (b - 1))
                sp.dma_start(total[b % 2][:], sum_rows[b * S:(b + 1) * S, :].rearrange("(t p) d -> p t d", p=P)
                             ).then_inc(total_in[b % 2], 16)
                if b >= 1:
                    sp.wait_ge(done, b)
                    sp.dma_start(out[b - 1].rearrange("(t p) d -> p t d", p=P), total[(b - 1) % 2][:]).then_inc(stored, 16)
            sp.wait_ge(done, B)
            sp.dma_start(out[B - 1].rearrange("(t p) d -> p t d", p=P), total[(B - 1) % 2][:]).then_inc(stored, 16)
            sp.wait_ge(stored, 16 * B)

        @block.gpsimd
        def _(pool):
            def gather(e):
                if e >= 2:
                    pool.wait_ge(turned, 3 * (e - 1))
                for c in range(CT):
                    nc.gpsimd.indirect_dma_start(
                        out=xe[e % 2][:, c, :], out_offset=None, in_=n_rows,
                        in_offset=bass.IndirectOffsetOnAxis(ap=place[:, e, c:c + 1], axis=0)).then_inc(gathered[e % 2], 16)

            gather(0)
            gather(1)
            for e in range(E):
                for c in range(CT):
                    pool.wait_ge(y_ready, CT * e + c + 1)
                    if c == 0 and e > 0:
                        pool.wait_ge(added, 16 * CT * e)
                    nc.gpsimd.indirect_dma_start(
                        out=sum_rows, out_offset=bass.IndirectOffsetOnAxis(ap=place[:, e, c:c + 1], axis=0),
                        in_=y[e % 2][:, c, :], in_offset=None, compute_op=ALU.add).then_inc(added, 16)
                if e + 2 < E:
                    gather(e + 2)
            for b in range(B):
                pool.wait_ge(var_ready, b + 1)
                nc.gpsimd.tensor_tensor(rstd[:, b * NT:(b + 1) * NT], var_eps[:, b * NT:(b + 1) * NT],
                                        minus_half[:, 0:NT], ALU.pow).then_inc(rstd_ready, 1)

        @block.scalar
        def _(act):
            def turned_in(e):
                for i in range(3):
                    act.wait_ge(turned, 3 * e + i + 1)
                    if i < KC:
                        nc.scalar.copy(xT[e % 2][:, i, 0:S], ps_t[(3 * e + i) % 2][:]).then_inc(xT_ready, 1)
                    else:
                        nc.scalar.copy(xT[e % 2][:, :, S:], ps_t[(3 * e + i) % 2][:, 0:KC * P].rearrange("p (c n) -> p c n", c=KC)
                                       ).then_inc(xT_ready, 1)

            turned_in(0)
            for e in range(E):
                for f in range(FC):
                    n = FC * e + f
                    act.wait_ge(h_sum, n + 1)
                    if f == 0 and e > 0:
                        act.wait_ge(y_sum, CT * e)
                    nc.scalar.activation(hT[:, f, :].rearrange("p (a n) -> p a n", a=2), ps_h[f % 2][:, :, 0:HALF], ACT.Gelu,
                                         bias=b1[:, e, f:f + 1]).then_inc(hT_ready, 1)
                if e + 1 < E:
                    turned_in(e + 1)

        @block.vector
        def _(dve):
            V = nc.vector
            for e in range(E):
                for c in range(CT):
                    n = CT * e + c
                    dve.wait_ge(y_sum, n + 1)
                    if c == 0:
                        dve.wait_ge(weights_in[e % 2], 48 * (e // 2 + 1))
                        if e >= 2:
                            dve.wait_ge(added, 16 * CT * (e - 1))
                    if n >= 2:
                        dve.wait_ge(y_ready, n - 1)
                    V.tensor_tensor(raw[:, n % 2, :], ps_y[n % 2][:, 0:D], b2[:, e % 2, :], ALU.add).then_inc(biased, 1)
                    dve.wait_ge(biased, n + 1)
                    V.tensor_scalar(y[e % 2][:, c, :], raw[:, n % 2, :], gate[:, e, c:c + 1], None, ALU.mult).then_inc(y_ready, 1)
            for b in range(B):
                tot = total[b % 2]
                dve.wait_ge(total_in[b % 2], 16 * (b // 2 + 1))
                for t in range(NT):
                    V.bn_stats(stats[:, b * NT + t, :], tot[:, t, :]).then_inc(stats_ready, 1)
                dve.wait_ge(stats_ready, NT * (b + 1))
                for t in range(NT):
                    V.bn_aggr(moments[:, b * NT + t, :], stats[:, b * NT + t, :]).then_inc(moments_ready, 1)
                dve.wait_ge(moments_ready, NT * (b + 1))
                V.tensor_scalar(var_eps[:, b * NT:(b + 1) * NT], moments[:, b * NT:(b + 1) * NT, 1], EPS, None, ALU.add
                                ).then_inc(var_ready, 1)
                dve.wait_ge(rstd_ready, b + 1)
                for t in range(NT):
                    V.tensor_scalar(tot[:, t, :], tot[:, t, :], moments[:, b * NT + t, 0:1],
                                    rstd[:, b * NT + t:b * NT + t + 1], ALU.subtract, ALU.mult).then_inc(scaled_by, 1)
                dve.wait_ge(scaled_by, (NT + 1) * b + NT)
                V.tensor_tensor(tot[:], tot[:], bass.AP(gamma[:].tensor, gamma[:].offset, [gamma[:].ap[0], [0, NT], [1, D]]),
                                ALU.mult).then_inc(scaled_by, 1)
                dve.wait_ge(scaled_by, (NT + 1) * (b + 1))
                V.tensor_tensor(tot[:], tot[:], x[:, b * NT:(b + 1) * NT, :], ALU.add).then_inc(done, 1)

        @block.tensor
        def _(pe):
            def transposes(e):
                pe.wait_ge(gathered[e % 2], 16 * CT * (e // 2 + 1))
                for i in range(3):
                    n = 3 * e + i
                    if n >= 2:
                        pe.wait_ge(xT_ready, n - 1)
                    if i < KC:
                        for c in range(NT):
                            mm = nc.tensor.transpose(ps_t[n % 2][:, c * P:(c + 1) * P], xe[e % 2][:, c, i * P:(i + 1) * P], ident[:])
                    else:
                        for k in range(KC):
                            mm = nc.tensor.transpose(ps_t[n % 2][:, k * P:(k + 1) * P], xe[e % 2][:, NT, k * P:(k + 1) * P], ident[:])
                    mm.then_inc(turned, 1)

            transposes(0)
            for e in range(E):
                pe.wait_ge(xT_ready, 3 * (e + 1))
                pe.wait_ge(weights_in[e % 2], 48 * (e // 2 + 1))
                for f in range(FC):
                    n = FC * e + f
                    if n >= 2:
                        pe.wait_ge(hT_ready, n - 1)
                    for half in range(2):
                        for c in range(KC):
                            mm = nc.tensor.matmul(ps_h[f % 2][:, half, 0:HALF], w1[e % 2][:, c, f * P:(f + 1) * P],
                                                  xT[e % 2][:, c, half * HALF:(half + 1) * HALF], start=(c == 0), stop=(c == KC - 1))
                    mm.then_inc(h_sum, 1)
                if e + 1 < E:
                    transposes(e + 1)
                pe.wait_ge(hT_ready, FC * (e + 1))
                for c in range(CT):
                    n = CT * e + c
                    if n >= 2:
                        pe.wait_ge(biased, n - 1)
                    for f in range(FC):
                        mm = nc.tensor.matmul(ps_y[n % 2][:, 0:D], hT[:, f, c * P:(c + 1) * P], w2[e % 2][:, f, :],
                                              start=(f == 0), stop=(f == FC - 1))
                    mm.then_inc(y_sum, 1)


def program(nc, io, out):
    ctx = ExitStack()
    with ctx:
        x = ctx.enter_context(nc.sbuf_tensor("x_sb", [P, B * NT, D], F32))
        ident = ctx.enter_context(nc.sbuf_tensor("ident", [P, P], F32))
        identb = ctx.enter_context(nc.sbuf_tensor("identb", [P, P], BF16))
        ident_set = ctx.enter_context(nc.semaphore("ident_set"))
        with nc.Block() as block:
            @block.gpsimd
            def _(pool):
                nc.gpsimd.memset(ident[:], 0.0).then_inc(ident_set, 1)
                pool.wait_ge(ident_set, 1)
                nc.gpsimd.affine_select(out=ident[:], in_=ident[:], compare_op=ALU.not_equal, fill=1.0, base=0,
                                        pattern=[[-1, P]], channel_multiplier=1).then_inc(ident_set, 1)
                pool.wait_ge(ident_set, 2)
                nc.gpsimd.tensor_copy(identb[:], ident[:]).then_inc(ident_set, 1)
        softmax_attention(nc, io, x, ident, identb)
        expert_per_batch(nc, io, x, ident)
        sigmoid_attention(nc, io, x, ident)
        mixture(nc, io, x, ident, out)


def laid_out(inputs):
    a = {k: np.asarray(v) for k, v in inputs.items()}
    order = np.arange(D).reshape(KC, HC, HD).transpose(0, 2, 1).reshape(D)
    cols = lambda v: v.reshape(KC, P).T
    m = {
        "x": a["x"],
        "ctxT": a["ctx_1024"].transpose(0, 2, 1),
        "mask": a["mask_BxS2_bf1"].view(np.uint8),
        "wq": a["L0_xattn_Wq"][order].T, "wk": a["L0_xattn_Wk"][order].T,
        "wv": a["L0_xattn_Wv"].T, "wo": a["L0_xattn_Wo"].T,
        "bq": cols(a["L0_xattn_bq"][order]), "bk": cols(a["L0_xattn_bk"][order]), "bv": cols(a["L0_xattn_bv"]),
        "bo": a["L0_xattn_bo"].reshape(1, D),
        "pw1": a["L0_ffn_Wp1"], "pb1": a["L0_ffn_bp1"].reshape(P, 1), "pw2": a["L0_ffn_Wp2"],
        "pb2": a["L0_ffn_bp2"].reshape(1, -1),
        "fw1": a["L0_ffn_W1"], "fb1": a["L0_ffn_b1"].reshape(8, 4, P).transpose(0, 2, 1),
        "fw2": a["L0_ffn_W2"], "fb2": a["L0_ffn_b2"].reshape(8, KC, P).transpose(0, 2, 1),
        "fwo": a["L0_ffn_Wo"], "fbo": a["L0_ffn_bo"].reshape(1, D),
        "swq": a["L1_xattn_Wq"][order].T, "swk": a["L1_xattn_Wk"][order].T, "swv": a["L1_xattn_Wv"].T,
        "swp": a["L1_xattn_Wp"].T,
        "sgq": a["L1_xattn_gq"].repeat(HC).reshape(P, 1), "sbq": a["L1_xattn_bq"].repeat(HC).reshape(P, 1),
        "sgk": a["L1_xattn_gk"].repeat(HC).reshape(P, 1), "sbk": a["L1_xattn_bk"].repeat(HC).reshape(P, 1),
        "sbp": a["L1_xattn_bp"].reshape(1, D),
        "mwr": a["L1_ffn_Wr"], "mbr": a["L1_ffn_br"].reshape(1, -1),
        "mw1": a["L1_ffn_W1"], "mb1": a["L1_ffn_b1"].reshape(8, 8, P).transpose(0, 2, 1),
        "mw2": a["L1_ffn_W2"], "mb2": a["L1_ffn_b2"],
        "mgamma": a["L1_ffn_gamma"].reshape(1, D), "mbeta": a["L1_ffn_beta"].reshape(1, D),
    }
    return {k: np.ascontiguousarray(v) for k, v in m.items()}


def kernel(**inputs):
    import concourse.bacc as bacc
    from concourse.bass_utils import run_bass_kernel_spmd

    arrays = laid_out(inputs)
    nc = bacc.Bacc("TRN2", target_bir_lowering=False, num_devices=1)
    io = {k: nc.dram_tensor(k, v.shape, mybir.dt.from_np(v.dtype), kind="ExternalInput").ap() for k, v in arrays.items()}
    out = nc.dram_tensor("out", (B, S, D), F32, kind="ExternalOutput").ap()
    program(nc, io, out)
    r = run_bass_kernel_spmd(nc, [arrays], core_ids=[0])
    return r.results[0]["out"]
```

```python
from contextlib import ExitStack

import numpy as np

import concourse.bass as bass
from concourse import mybir

F32 = mybir.dt.float32
BF16 = mybir.dt.bfloat16
I32 = mybir.dt.int32
U8 = mybir.dt.uint8
ALU = mybir.AluOpType
ACT = mybir.ActivationFunctionType
AX = mybir.AxisListType

P = 128
B, S, D = 8, 512, 256
NT = S // P
KC = D // P
H, HD = 16, 16
HC = H // KC
HG = 4
NG = H // HG
NE = 8
EPS = 1e-5
PAIRS = 6
K_MASK = PAIRS * HD
K_MAX = K_MASK + 1
K_ALL = K_MASK + 4
Q_PARTS = (0, 0, 0, 1, 1, 2)
K_PARTS = (0, 1, 2, 0, 1, 0)
SCALE = 1.0 / np.sqrt(HD)
MASK_Q, MASK_K = 250.0, -160.0
assert MASK_Q * MASK_K * SCALE == -10000.0

CAP = -(-(B * S // NE * 5) // 4)
SPARE = CAP


def softmax_attention(nc, io, x, ident, identb):
    QUADS = NG * NT
    MX_LEAD = 7
    MX_RING = 3
    PV_LAG = 2
    STACK_DMAS = 4 * PAIRS + 1
    ctx = ExitStack()
    with ctx:
        def sb(name, shape, dt=F32):
            return ctx.enter_context(nc.sbuf_tensor("a_" + name, shape, dt))

        def ps(name, shape, dt=F32):
            return ctx.enter_context(nc.psum_tensor("a_" + name, shape, dt))

        def sem(name):
            return ctx.enter_context(nc.semaphore("a_" + name))

        wq, wk, wv, wo = (sb(n, [P, KC, D]) for n in ("wq", "wk", "wv", "wo"))
        bq, bk, bv = (sb(n, [P, KC]) for n in ("bq", "bk", "bv"))
        bo = sb("bo", [P, D])
        head_rows = sb("head_rows", [H, KC, P])
        ctxT = sb("ctxT", [P, KC, S])
        mask8 = sb("mask8", [P, S], U8)
        maskf = sb("maskf", [P, S])
        mask_row = sb("mask_row", [P, S], BF16)
        q_row, k_rows = sb("q_row", [1, S], BF16), sb("k_rows", [3, S], BF16)
        stats = sb("stats", [P, NT, 6])
        moments = sb("moments", [P, NT, 2])
        var_eps = sb("var_eps", [P, NT])
        rstd = sb("rstd", [P, NT])
        minus_half = sb("minus_half", [P, NT])
        xn = sb("xn", [P, NT, D])
        xT = sb("xT", [P, KC, S])
        proj = sb("proj", [P, 2, S])
        rest = sb("rest", [P, 2, S])
        parts = sb("parts", [P, 2, 3, S], BF16)
        q_stack = [sb(f"q_stack{i}", [P, H, S], BF16) for i in range(2)]
        k_stack = [sb(f"k_stack{i}", [P, H, S], BF16) for i in range(2)]
        v_ones = [sb(f"v_ones{i}", [P, NT, H, 2 * HD]) for i in range(2)]
        probs = sb("probs", [P, NT, HG, S])
        neg_max = sb("neg_max", [P, 2, NT, HG])
        neg_rest = sb("neg_rest", [P, NT, HG])
        neg_parts = sb("neg_parts", [P, NT, 3, HG], BF16)
        neg_rows = sb("neg_rows", [3 * HG, S], BF16)
        sums = sb("sums", [P, 2, S])
        values = sb("values", [P, 2, KC, S])
        den = sb("den", [P, 64])
        rden = sb("rden", [P, 64])
        rden_h = sb("rden_h", [H, S])
        oT = sb("oT", [P, KC, S])

        ps_score = [ps(f"score{i}", [P, S]) for i in range(2)]
        ps_max = [ps(f"max{i}", [P, S]) for i in range(MX_RING)]
        ps_pv = ps("pv", [P, S])
        ps_a = ps("act", [P, S])
        ps_d = ps("dve", [P, S])

        x_first_in, x_rest_in = sem("x_first_in"), sem("x_rest_in")
        w_in, ctx_in, mask_in = sem("w_in"), sem("ctx_in"), sem("mask_in")
        consts, v_consts, rows_set = sem("consts"), sem("v_consts"), sem("rows_set")
        stats_ready, moments_ready, var_ready = sem("stats_ready"), sem("moments_ready"), sem("var_ready")
        rstd_ready, xn_ready = sem("rstd_ready"), sem("xn_ready")
        a_ready, a_empty = sem("a_ready"), sem("a_empty")
        d_ready, d_empty = sem("d_ready"), sem("d_empty")
        maskf_ready, mask_row_ready, mask_landed = sem("maskf_ready"), sem("mask_row_ready"), sem("mask_landed")
        masked, part0, rest_ready, part1, part2 = (
            sem("masked"), sem("part0"), sem("rest_ready"), sem("part1"), sem("part2"))
        stacked = [sem(f"stacked{i}") for i in range(2)]
        score_ready, probs_ready, pv_ready, sums_ready = (
            sem("score_ready"), sem("probs_ready"), sem("pv_ready"), sem("sums_ready"))
        max_ready, max_read, neg_chain, neg_ready, neg_landed = (
            sem("max_ready"), sem("max_read"), sem("neg_chain"), sem("neg_ready"), sem("neg_landed"))
        values_landed = [sem(f"values_landed{i}") for i in range(2)]
        den_landed = [sem(f"den_landed{i}") for i in range(2)]
        rden_ready, rden_landed = sem("rden_ready"), sem("rden_landed")
        weighted, ot_ready, residual, x_done = sem("weighted"), sem("ot_ready"), sem("residual"), sem("x_done")

        def batches(eng, batch):
            batch(0, 0, True, False)
            with eng.Fori(0, (B - 2) // 2) as i:
                batch(i * 2 + 1, 1, False, False)
                batch(i * 2 + 2, 0, False, False)
            batch(B - 1, (B - 1) % 2, False, True)

        KEYS0, KEYS1, XT0, XT1, QUERIES0, QUERIES1, V0, V1 = range(8)
        A_ITEMS = 8
        PROJ = ((KEYS0, False, 0), (KEYS1, False, 1), (QUERIES0, True, 0), (QUERIES1, True, 1))

        D_FIRST = ("neg1", "neg2", "neg3", "neg4")
        D_LATER = ("neg1", "neg2", "rden0", "rden1", "neg3", "out0", "out1", "neg4")
        D_END = 1 + len(D_FIRST) + len(D_LATER) * (B - 1) - 1

        def d_item(b, first, name):
            if first:
                return 1 + D_FIRST.index(name)
            return (b - 1) * len(D_LATER) + (1 + len(D_FIRST) + D_LATER.index(name))

        block = ctx.enter_context(nc.Block())

        @block.sync
        def _(sp):
            def loads(bb):
                sp.dma_start(ctxT[:], io["ctxT"][bass.ds(bb, 1)].rearrange("a (c p) n -> p (a c) n", p=P)
                             ).then_inc(ctx_in, 16)
                sp.dma_start(mask8[:], io["mask"][bass.ds(bb, 1), :].to_broadcast([P, S])).then_inc(mask_in, 16)

            def mask_to_stack(bb, par, unused=True):
                if not unused:
                    sp.wait_ge(score_ready, (bb - 1) * 64)
                sp.wait_ge(mask_row_ready, bb * 2 + 2)
                row = mask_row[96:97, :]
                sp.dma_start(k_stack[par][K_MASK:K_MASK + 1, :, :],
                             bass.AP(row.tensor, row.offset, [[S, 1], [0, H], [1, S]])).then_inc(mask_landed, 16)

            def stack(bb, par, k):
                _, is_q, c = PROJ[k]
                dst = (q_stack if is_q else k_stack)[par]
                for part, ready in enumerate((part0, part1, part2)):
                    sp.wait_ge(ready, bb * 4 + (k + 1))
                    for j in range(PAIRS):
                        if (Q_PARTS if is_q else K_PARTS)[j] == part:
                            sp.dma_start(dst[HD * j:HD * (j + 1), HC * c:HC * (c + 1), :],
                                         parts[:, k % 2, part, :]).then_inc(stacked[k % 2], 16)

            def sums_out(b, par, g, first):
                if g == 0 and not first:
                    sp.wait_ge(ot_ready, (b - 1) * KC)
                    sp.wait_ge(rden_ready, b)
                sp.wait_ge(sums_ready, b * 4 + (g + 1))
                for hh in range(HG):
                    h = HG * g + hh
                    sp.dma_start(values[HD * (h % HC):HD * (h % HC + 1), par, h // HC, :],
                                 sums[32 * hh:32 * hh + HD, g % 2, :]).then_inc(values_landed[g % 2], 16)
                    sp.dma_start(den[8 * h:8 * h + 8, :],
                                 sums[32 * hh + HD:32 * hh + HD + 1, g % 2, :]).then_inc(den_landed[g % 2], 16)

            def rden_out(b, d_prev):
                sp.wait_ge(d_ready, d_prev)
                sp.wait_ge(rden_ready, b + 1)
                sp.dma_start(rden_h[:, :], rden[:, :]).then_inc(rden_landed, 16)

            for dst, name in ((wk, "wk"), (wq, "wq"), (wv, "wv"), (wo, "wo")):
                if dst is wq:
                    loads(0)
                    for small in ("bk", "bq", "bv"):
                        sp.dma_start({"bk": bk, "bq": bq, "bv": bv}[small][:], io[small]).then_inc(w_in, 16)
                sp.dma_start(dst[:], io[name].rearrange("(c p) n -> p c n", p=P)).then_inc(w_in, 16)
            sp.dma_start(bo[:], io["bo"].to_broadcast([P, D])).then_inc(w_in, 16)
            sp.dma_start(x[:, NT:, :], io["x"][1:].rearrange("b (t p) d -> p (b t) d", p=P)).then_inc(x_rest_in, 16)
            sp.wait_ge(consts, 3)
            for i in range(2):
                for rows, source, n in ((q_stack[i][K_MASK:K_MASK + 1], q_row[:], 1), (k_stack[i][K_MAX:K_ALL], k_rows[:], 3)):
                    sp.dma_start(rows, bass.AP(source.tensor, source.offset, [[S, n], [0, H], [1, S]])).then_inc(rows_set, 16)
            mask_to_stack(0, 0)
            for k in range(4):
                stack(0, 0, k)

            def batch(b, par, first, last):
                if not last:
                    sp.wait_ge(maskf_ready, b + 1)
                    sp.wait_ge(a_ready, b * A_ITEMS + A_ITEMS)
                    loads(b + 1)
                    if not first:
                        sums_out(b - 1, 1 - par, 2, False)
                    mask_to_stack(b + 1, 1 - par, first)
                if not first:
                    if last:
                        sums_out(b - 1, 1 - par, 2, False)
                    sums_out(b - 1, 1 - par, 3, False)
                if not last:
                    stack(b + 1, 1 - par, 0)
                if not first:
                    rden_out(b - 1, (b - 1) * len(D_LATER) + (1 + len(D_FIRST) + D_LATER.index("rden1") + 1 - len(D_LATER)))
                if not last:
                    stack(b + 1, 1 - par, 1)
                if not last:
                    stack(b + 1, 1 - par, 2)
                    stack(b + 1, 1 - par, 3)
                sums_out(b, par, 0, first)
                sums_out(b, par, 1, first)

            batches(sp, batch)
            sums_out(B - 1, (B - 1) % 2, 2, False)
            sums_out(B - 1, (B - 1) % 2, 3, False)
            rden_out(B - 1, d_item(B - 1, False, "rden1") + 1)

        @block.scalar
        def _(act):
            def evacuate(bb, item, out, **kw):
                act.wait_ge(a_ready, bb * A_ITEMS + (item + 1))
                nc.scalar.activation(out, ps_a[:] if len(out.shape) == 2 else
                                     ps_a[:].rearrange("p (t h d) -> p t h d", t=2, h=H), ACT.Identity,
                                     **kw).then_inc(a_empty, 1)

            def project(bb, k):
                item, is_q, c = PROJ[k]
                if k >= 2:
                    act.wait_ge(rest_ready, bb * 4 + (k - 1))
                elif not (isinstance(bb, int) and bb == 0):
                    act.wait_ge(rest_ready, (bb - 1) * 4 + (k + 3))
                evacuate(bb, item, proj[:, k % 2, :], bias=(bq if is_q else bk)[:, c:c + 1])

            def transposed(bb, c):
                evacuate(bb, XT0 + c, xT[:, c, :])

            def v_tiles(bb, par, t):
                evacuate(bb, V0 + t, v_ones[par][:, 2 * t:2 * t + 2, :, 0:HD])

            def neg_in(b, par, g, d):
                act.wait_ge(d_empty, d + 1)
                act.dma_start(q_stack[par][K_MAX:K_ALL, HG * g:HG * (g + 1), :], neg_rows[:]).then_inc(neg_landed, 16)

            def sums_of(b, g):
                G = b * 4 + g
                act.wait_ge(pv_ready, G * NT + NT)
                if not (isinstance(b, int) and b * 4 + g < 2):
                    act.wait_ge(values_landed[g % 2], b * 128 + (g // 2) * 64)
                    act.wait_ge(den_landed[g % 2], b * 128 + (g // 2) * 64)
                nc.scalar.copy(sums[:, g % 2, :], ps_pv[:]).then_inc(sums_ready, 1)

            act.dma_start(x[:, 0:NT, :], io["x"][0].rearrange("(t p) d -> p t d", p=P)).then_inc(x_first_in, 16)
            act.wait_ge(w_in, 16 * 8)
            project(0, 0), project(0, 1)
            transposed(0, 0), transposed(0, 1)
            project(0, 2), project(0, 3)
            v_tiles(0, 0, 0), v_tiles(0, 0, 1)
            neg_in(0, 0, 0, 0)

            def batch(b, par, first, last):
                for u in range(QUADS):
                    g, kc = divmod(u, NT)
                    quad = b * QUADS + u
                    for hh in range(HG):
                        act.wait_ge(score_ready, quad * HG + (hh + 1))
                        if hh == 0 and not (first and u < NT):
                            act.wait_ge(pv_ready, quad + (1 - NT))
                        nc.scalar.activation(probs[:, kc, hh, :], ps_score[hh % 2][:], ACT.Exp, scale=SCALE
                                             ).then_inc(probs_ready, 1)
                    if u == 1 and not first:
                        sums_of(b - 1, 3)
                    if u % NT == 1 and u > 1:
                        sums_of(b, g - 1)
                    if not last:
                        {0: lambda: project(b + 1, 0),
                         1: lambda: project(b + 1, 1),
                         2: lambda: (transposed(b + 1, 0), transposed(b + 1, 1)),
                         3: lambda: project(b + 1, 2),
                         4: lambda: project(b + 1, 3),
                         11: lambda: v_tiles(b + 1, 1 - par, 0),
                         12: lambda: v_tiles(b + 1, 1 - par, 1)}.get(u, lambda: None)()
                    if u % NT == 2 and u < 12:
                        neg_in(b, par, g + 1, d_item(b, first, f"neg{g + 1}"))
                    if u == 14 and not last:
                        neg_in(b + 1, 1 - par, 0, d_item(b, first, "neg4"))

            batches(act, batch)
            sums_of(B - 1, 3)

        @block.gpsimd
        def _(pool):
            nc.gpsimd.memset(minus_half[:], -0.5).then_inc(consts, 1)
            nc.gpsimd.memset(q_row[:], MASK_Q).then_inc(consts, 1)
            nc.gpsimd.memset(k_rows[:], 1.0).then_inc(consts, 1)
            pool.wait_ge(consts, 3)
            nc.gpsimd.memset(head_rows[:], 1.0).then_inc(consts, 1)
            pool.wait_ge(consts, 4)
            nc.gpsimd.affine_select(out=head_rows[:], in_=head_rows[:], compare_op=ALU.is_ge, fill=0.0, base=0,
                                    pattern=[[P, KC], [1, P]], channel_multiplier=-HD).then_inc(consts, 1)
            pool.wait_ge(consts, 5)
            nc.gpsimd.affine_select(out=head_rows[:], in_=head_rows[:], compare_op=ALU.is_ge, fill=0.0, base=HD - 1,
                                    pattern=[[-P, KC], [-1, P]], channel_multiplier=HD).then_inc(consts, 1)

            def invert_deviation(bb):
                pool.wait_ge(var_ready, bb + 1)
                nc.gpsimd.tensor_tensor(rstd[:], var_eps[:], minus_half[:], ALU.pow).then_inc(rstd_ready, 1)

            def split(bb, k, step):
                n = bb * 4 + k
                item, is_q, _ = PROJ[k]
                if step == 0:
                    pool.wait_ge(a_empty, bb * A_ITEMS + (item + 1))
                    pool.wait_ge(maskf_ready, bb + 1)
                    nc.gpsimd.tensor_tensor(proj[:, k % 2, :], proj[:, k % 2, :], maskf[:], ALU.mult).then_inc(masked, 1)
                elif step == 1:
                    pool.wait_ge(part0, n + 1)
                    if not (isinstance(n, int) and n < 2):
                        pool.wait_ge(part2, n - 1)
                    nc.gpsimd.tensor_tensor(rest[:, k % 2, :], proj[:, k % 2, :], parts[:, k % 2, 0, :],
                                            ALU.subtract).then_inc(rest_ready, 1)
                else:
                    pool.wait_ge(part1, n + 1)
                    nc.gpsimd.tensor_tensor(parts[:, k % 2, 2, :], rest[:, k % 2, :], parts[:, k % 2, 1, :],
                                            ALU.subtract).then_inc(part2, 1)

            def add_output_bias(b, first):
                for t in range(NT):
                    tile = x[:, bass.ds(b * NT + t, 1), :].rearrange("p a n -> p (a n)")
                    if t == 0:
                        pool.wait_ge(xn_ready, b * NT + NT)
                        pool.wait_ge(w_in, 16 * 8)
                    nc.gpsimd.tensor_tensor(tile, tile, bo[:], ALU.add).then_inc(residual, 1)

            def prepare(bb):
                invert_deviation(bb)
                split(bb, 0, 0)
                split(bb, 0, 1)
                split(bb, 1, 0)
                split(bb, 0, 2)
                split(bb, 1, 1)
                split(bb, 1, 2)
                split(bb, 2, 1)
                split(bb, 2, 2)
                split(bb, 3, 1)
                split(bb, 3, 2)

            pool.wait_ge(consts, 6)
            prepare(0)

            def batch(b, par, first, last):
                if not last:
                    prepare(b + 1)
                add_output_bias(b, first)

            batches(pool, batch)

        @block.vector
        def _(dve):
            def normalise(bb):
                dve.wait_ge(x_first_in if isinstance(bb, int) and bb == 0 else x_rest_in, 16)
                for t in range(NT):
                    nc.vector.bn_stats(stats[:, t, :], x[:, bass.ds(bb * NT + t, 1), :].rearrange("p a n -> p (a n)")
                                       ).then_inc(stats_ready, 1)
                dve.wait_ge(stats_ready, bb * NT + NT)
                nc.vector.memset(var_eps[:], EPS).then_inc(moments_ready, 1)
                for t in range(NT):
                    nc.vector.bn_aggr(moments[:, t, :], stats[:, t, :]).then_inc(moments_ready, 1)
                dve.wait_ge(moments_ready, bb * (NT + 1) + (NT + 1))
                nc.vector.tensor_tensor(var_eps[:], moments[:, :, 1], var_eps[:], ALU.add).then_inc(var_ready, 1)

            def centre(bb):
                dve.wait_ge(rstd_ready, bb + 1)
                if not (isinstance(bb, int) and bb == 0):
                    dve.wait_ge(a_ready, (bb - 1) * A_ITEMS + (XT1 + 1))
                for t in range(NT):
                    nc.vector.tensor_scalar(xn[:, t, :], x[:, bass.ds(bb * NT + t, 1), :].rearrange("p a n -> p (a n)"),
                                            moments[:, t, 0:1], rstd[:, t:t + 1], ALU.subtract, ALU.mult
                                            ).then_inc(xn_ready, 1)

            def read_mask(bb):
                dve.wait_ge(mask_in, (bb + 1) * 16)
                if not (isinstance(bb, int) and bb == 0):
                    dve.wait_ge(masked, bb * 2)
                    dve.wait_ge(mask_landed, bb * 16)
                nc.vector.tensor_copy(maskf[:], mask8[:]).then_inc(maskf_ready, 1)
                dve.wait_ge(maskf_ready, bb + 1)
                nc.vector.tensor_scalar(mask_row[96:97, :], maskf[96:97, :], -MASK_K, MASK_K, ALU.mult, ALU.add
                                        ).then_inc(mask_row_ready, 2)

            def part(bb, k, step):
                n = bb * 4 + k
                item, is_q, _ = PROJ[k]
                if step == 0:
                    dve.wait_ge(a_empty, bb * A_ITEMS + (item + 1))
                    if not is_q:
                        dve.wait_ge(masked, bb * 2 + (k + 1))
                    if not (isinstance(n, int) and n < 2):
                        dve.wait_ge(stacked[k % 2], bb * (2 * 96) + 96 * (k // 2))
                    nc.vector.tensor_copy(parts[:, k % 2, 0, :], proj[:, k % 2, :]).then_inc(part0, 1)
                else:
                    dve.wait_ge(rest_ready, n + 1)
                    nc.vector.tensor_copy(parts[:, k % 2, 1, :], rest[:, k % 2, :]).then_inc(part1, 1)

            def maxima(b, v):
                for s in range(NT):
                    n = b * 64 + (4 * v + s)
                    dve.wait_ge(max_ready, n + 1)
                    nc.vector.tensor_reduce(neg_max[:, (v // HG) % 2, s, v % HG:v % HG + 1], ps_max[(4 * v + s) % MX_RING][:], AX.X,
                                            ALU.max, negate=True).then_inc(max_read, 1)

            def split_maxima(b, g):
                G = b * 4 + g
                dve.wait_ge(max_read, G * 16 + 16)
                nm = neg_max[:, g % 2, :, :]
                nc.vector.tensor_copy(neg_parts[:, :, 0, :], nm).then_inc(neg_chain, 1)
                dve.wait_ge(neg_chain, G * 3 + 1)
                nc.vector.tensor_tensor(neg_rest[:], nm, neg_parts[:, :, 0, :], ALU.subtract).then_inc(neg_chain, 1)
                dve.wait_ge(neg_chain, G * 3 + 2)
                nc.vector.tensor_copy(neg_parts[:, :, 1, :], neg_rest[:]).then_inc(neg_chain, 1)
                dve.wait_ge(neg_chain, G * 3 + 3)
                nc.vector.tensor_tensor(neg_parts[:, :, 2, :], neg_rest[:], neg_parts[:, :, 1, :], ALU.subtract
                                        ).then_inc(neg_ready, 1)

            def rows_of_maxima(b, g, d):
                dve.wait_ge(d_ready, d + 1)
                if not (isinstance(b, int) and b * 4 + g == 0):
                    dve.wait_ge(neg_landed, (b * 4 + g) * 16)
                nc.vector.tensor_copy(neg_rows[:], ps_d[:].bitcast(BF16)[0:3 * HG, 0:S]).then_inc(d_empty, 1)

            def invert_denominators(b):
                for i in range(2):
                    dve.wait_ge(den_landed[i], b * 128 + 128)
                if not (isinstance(b, int) and b == 0):
                    dve.wait_ge(rden_landed, b * 16)
                nc.vector.reciprocal(rden[:], den[:]).then_inc(rden_ready, 1)

            def weigh(b, par, c, d):
                dve.wait_ge(d_ready, d + 1)
                if c == 0:
                    for i in range(2):
                        dve.wait_ge(values_landed[i], b * 128 + 128)
                nc.vector.tensor_tensor(oT[:, c, :], values[:, par, c, :], ps_d[:], ALU.mult).then_inc(d_empty, 1)
                dve.wait_ge(d_empty, d + 1)
                nc.vector.tensor_scalar(oT[:, c, :], oT[:, c, :], bv[:, c:c + 1], None, ALU.add).then_inc(ot_ready, 1)

            def output(b, t, d):
                dve.wait_ge(d_ready, d + 1)
                dve.wait_ge(residual, b * NT + NT)
                tiles = x[:, bass.ds(b * NT + 2 * t, 2), :]
                nc.vector.tensor_tensor(tiles, ps_d[:].rearrange("p (t n) -> p t n", t=2), tiles, ALU.add
                                        ).then_inc(d_empty, 1)

            for i in range(2):
                nc.vector.memset(v_ones[i][:, :, :, HD:], 1.0).then_inc(v_consts, 1)
            read_mask(0)
            normalise(0)
            centre(0)
            for k in range(4):
                part(0, k, 0)
                part(0, k, 1)
            for v in range(MX_LEAD):
                maxima(0, v)
                if v == HG - 1:
                    split_maxima(0, 0)
                if v == HG:
                    rows_of_maxima(0, 0, 0)

            def batch(b, par, first, last):
                for u in range(QUADS):
                    v = u + MX_LEAD
                    if v < H:
                        maxima(b, v)
                    elif not last:
                        maxima(b + 1, v - H)
                    if u % 4 == 0 and u < 12:
                        split_maxima(b, u // 4 + 1)
                    if u == 12 and not last:
                        split_maxima(b + 1, 0)
                    if not last:
                        if u == 0:
                            read_mask(b + 1)
                            normalise(b + 1)
                        elif u == 1:
                            centre(b + 1)
                        for k, at in ((0, 1), (1, 2), (2, 4), (3, 5)):
                            if u == at + 1:
                                part(b + 1, k, 1)
                            if u == at:
                                part(b + 1, k, 0)
                    if u == 3 and not first:
                        invert_denominators(b - 1)
                    if u % 4 == 1 and u < 12:
                        rows_of_maxima(b, u // 4 + 1, d_item(b, first, f"neg{u // 4 + 1}"))
                    if u == 13 and not last:
                        rows_of_maxima(b + 1, 0, d_item(b, first, "neg4"))
                    if not first:
                        if u in (7, 8):
                            weigh(b - 1, 1 - par, u - 7, d_item(b, first, f"rden{u - 7}"))
                        if u in (10, 11):
                            output(b - 1, u - 10, d_item(b, first, f"out{u - 10}"))

            batches(dve, batch)
            invert_denominators(B - 1)
            for c in range(KC):
                weigh(B - 1, (B - 1) % 2, c, D_END + c)
            for t in range(2):
                output(B - 1, t, D_END + 2 + t)

        @block.tensor
        def _(pe):
            def take_act(bb, item):
                if not (isinstance(bb, int) and bb * A_ITEMS + item == 0):
                    pe.wait_ge(a_empty, bb * A_ITEMS + item)

            def project(bb, k):
                item, is_q, c = PROJ[k]
                take_act(bb, item)
                if is_q:
                    pe.wait_ge(a_empty, bb * A_ITEMS + (XT1 + 1))
                else:
                    pe.wait_ge(ctx_in, (bb + 1) * 16)
                for kk in range(KC):
                    mm = nc.tensor.matmul(ps_a[:], (wq if is_q else wk)[:, kk, c * P:(c + 1) * P],
                                          (xT if is_q else ctxT)[:, kk, :], start=(kk == 0), stop=(kk == KC - 1))
                mm.then_inc(a_ready, 1)

            def transpose_x(bb, c):
                take_act(bb, XT0 + c)
                pe.wait_ge(xn_ready, bb * NT + NT)
                for t in range(NT):
                    mm = nc.tensor.transpose(ps_a[:, t * P:(t + 1) * P], xn[:, t, c * P:(c + 1) * P], ident[:])
                mm.then_inc(a_ready, 1)

            def v_tiles(bb, t):
                take_act(bb, V0 + t)
                for tt in range(2):
                    for kk in range(KC):
                        mm = nc.tensor.matmul(ps_a[:, tt * D:(tt + 1) * D],
                                              ctxT[:, kk, (2 * t + tt) * P:(2 * t + tt + 1) * P], wv[:, kk, :],
                                              start=(kk == 0), stop=(kk == KC - 1))
                mm.then_inc(a_ready, 1)

            def head_scores_max(b, par, v, s):
                n = b * 64 + (4 * v + s)
                if v == 0 and s == 0:
                    for i in range(2):
                        pe.wait_ge(stacked[i], b * 192 + 192)
                    pe.wait_ge(mask_landed, b * 16 + 16)
                if 4 * v + s >= MX_RING:
                    pe.wait_ge(max_read, n + (1 - MX_RING))
                elif v == 0 and s == 0 and not (isinstance(b, int) and b == 0):
                    pe.wait_ge(max_read, n)
                nc.tensor.matmul(ps_max[(4 * v + s) % MX_RING][:], q_stack[par][0:K_MAX, v, s * P:(s + 1) * P],
                                 k_stack[par][0:K_MAX, v, :], start=True, stop=True).then_inc(max_ready, 1)

            def rows_of_maxima(b, g, d):
                pe.wait_ge(neg_ready, b * 4 + (g + 1))
                if not (isinstance(d, int) and d == 0):
                    pe.wait_ge(d_empty, d)
                for t in range(NT):
                    mm = nc.tensor.transpose(ps_d[:].bitcast(BF16)[0:3 * HG, t * P:(t + 1) * P],
                                             neg_parts[:, t, :, :].rearrange("p j h -> p (j h)"), identb[:])
                mm.then_inc(d_ready, 1)

            def scores(b, par, u, hh):
                g, kc = divmod(u, NT)
                n = b * 64 + (4 * u + hh)
                if kc == 0 and hh == 0:
                    pe.wait_ge(neg_landed, (b * 4 + g) * 16 + 16)
                if not (isinstance(n, int) and n < 2):
                    pe.wait_ge(probs_ready, n - 1)
                nc.tensor.matmul(ps_score[hh % 2][:], k_stack[par][0:K_ALL, HG * g + hh, kc * P:(kc + 1) * P],
                                 q_stack[par][0:K_ALL, HG * g + hh, :], start=True, stop=True).then_inc(score_ready, 1)

            def weighted_values(b, par, w):
                g, kc = divmod(w, NT)
                G = b * 4 + g
                pe.wait_ge(probs_ready, b * 64 + (4 * w + 4))
                if w == 0:
                    pe.wait_ge(a_empty, b * A_ITEMS + A_ITEMS)
                    pe.wait_ge(v_consts, 2)
                if kc == 0 and not (isinstance(G, int) and G == 0):
                    pe.wait_ge(sums_ready, G)
                for hh in range(HG):
                    mm = nc.tensor.matmul(ps_pv[32 * hh:32 * hh + 32, :], v_ones[par][:, kc, HG * g + hh, :],
                                          probs[:, kc, hh, :], start=(kc == 0), stop=(kc == NT - 1),
                                          tile_position=(0, 32 * hh))
                mm.then_inc(pv_ready, 1)

            def spread_denominators(b, c, d):
                pe.wait_ge(rden_landed, b * 16 + 16)
                pe.wait_ge(d_empty, d)
                nc.tensor.matmul(ps_d[:], head_rows[:, c, :], rden_h[:, :], start=True, stop=True).then_inc(d_ready, 1)

            def output(b, t, d):
                pe.wait_ge(ot_ready, b * KC + KC)
                pe.wait_ge(d_empty, d)
                for tt in range(2):
                    for c in range(KC):
                        mm = nc.tensor.matmul(ps_d[:, tt * D:(tt + 1) * D], oT[:, c, (2 * t + tt) * P:(2 * t + tt + 1) * P],
                                              wo[:, c, :], start=(c == 0), stop=(c == KC - 1))
                mm.then_inc(d_ready, 1)

            pe.wait_ge(w_in, 16 * 8)
            project(0, 0), project(0, 1)
            transpose_x(0, 0), transpose_x(0, 1)
            project(0, 2), project(0, 3)
            v_tiles(0, 0), v_tiles(0, 1)
            pe.wait_ge(consts, 6)
            pe.wait_ge(rows_set, 16 * 4)
            for v in range(MX_LEAD):
                for s in range(NT):
                    head_scores_max(0, 0, v, s)
                if v == HG:
                    rows_of_maxima(0, 0, 0)

            def batch(b, par, first, last):
                for u in range(QUADS):
                    v = u + MX_LEAD
                    for half in range(2):
                        for s in (2 * half, 2 * half + 1):
                            scores(b, par, u, s)
                            if v < H:
                                head_scores_max(b, par, v, s)
                            elif not last:
                                head_scores_max(b + 1, 1 - par, v - H, s)
                        if half == 0 and u >= PV_LAG:
                            weighted_values(b, par, u - PV_LAG)
                        elif half == 0 and not first:
                            weighted_values(b - 1, 1 - par, QUADS + u - PV_LAG)
                    if not last:
                        if u in (0, 1):
                            project(b + 1, u)
                        if u == 2:
                            transpose_x(b + 1, 0)
                            transpose_x(b + 1, 1)
                        if u in (3, 4):
                            project(b + 1, u - 1)
                        if u in (11, 12):
                            v_tiles(b + 1, u - 11)
                    if u % 4 == 1 and u < 12:
                        rows_of_maxima(b, u // 4 + 1, d_item(b, first, f"neg{u // 4 + 1}"))
                    if u == 13 and not last:
                        rows_of_maxima(b + 1, 0, d_item(b, first, "neg4"))
                    if not first:
                        if u in (7, 8):
                            spread_denominators(b - 1, u - 7, d_item(b, first, f"rden{u - 7}"))
                        if u in (10, 11):
                            output(b - 1, u - 10, d_item(b, first, f"out{u - 10}"))

            batches(pe, batch)
            for w in range(QUADS - PV_LAG, QUADS):
                weighted_values(B - 1, (B - 1) % 2, w)
            for c in range(KC):
                spread_denominators(B - 1, c, D_END + c)
            for t in range(2):
                output(B - 1, t, D_END + 2 + t)


def expert_per_batch(nc, io, x, ident):
    E, F = 8, 2 * D
    FC = F // P
    OUT_SCALE = 0.3
    ctx = ExitStack()
    with ctx:
        def sb(name, shape, dt=F32):
            return ctx.enter_context(nc.sbuf_tensor("b_" + name, shape, dt))

        def ps(name, shape, dt=F32):
            return ctx.enter_context(nc.psum_tensor("b_" + name, shape, dt))

        def sem(name):
            return ctx.enter_context(nc.semaphore("b_" + name))

        pw1, pb1, pw2, pb2 = sb("pw1", [P, KC, P]), sb("pb1", [P, 1]), sb("pw2", [P, E]), sb("pb2", [B, E])
        last = sb("last", [B, D])
        last_stats, last_moments = sb("last_stats", [B, 6]), sb("last_moments", [B, 2])
        last_var, last_rstd = sb("last_var", [B, 1]), sb("last_rstd", [B, 1])
        lastT, hiddenT = sb("lastT", [P, KC, B]), sb("hiddenT", [P, B])
        logits, neg_top, exps, total = sb("logits", [B, E]), sb("neg_top", [B, 1]), sb("exps", [B, E]), sb("total", [B, 1])
        inv_total, policy, top = sb("inv_total", [B, 1]), sb("policy", [B, E]), sb("top", [B, 1])
        countdown, winner, choice_f, choice = (sb("countdown", [B, E]), sb("winner", [B, E]), sb("choice_f", [B, 1]),
                                               sb("choice", [B, 1], I32))
        choices = sb("choices", [1, B], I32)
        minus_half = sb("minus_half", [P, NT])
        w1 = [sb(f"w1_{i}", [P, KC, F]) for i in range(2)]
        w2 = [sb(f"w2_{i}", [P, FC, D]) for i in range(2)]
        b1 = [sb(f"b1_{i}", [P, FC]) for i in range(2)]
        b2 = [sb(f"b2_{i}", [P, KC]) for i in range(2)]
        wo, bo = sb("wo", [P, KC, D]), sb("bo", [P, D])
        stats, moments = sb("stats", [P, NT, 6]), sb("moments", [P, NT, 2])
        var_eps, rstd = sb("var_eps", [P, NT]), sb("rstd", [P, NT])
        xn = [sb(f"xn{i}", [P, NT, D]) for i in range(2)]
        xT = [sb(f"xT{i}", [P, KC, S]) for i in range(2)]
        hT = sb("hT", [P, FC, S])
        rT = [sb(f"rT{i}", [P, KC, S]) for i in range(2)]

        ps_t = [ps(f"t{i}", [P, S]) for i in range(2)]
        ps_h = [ps(f"h{i}", [P, S]) for i in range(2)]
        ps_r = [ps(f"r{i}", [P, S]) for i in range(2)]
        ps_o = [ps(f"o{i}", [P, S]) for i in range(2)]

        policy_in, wo_in, bo_in, last_in, choices_in = (sem("policy_in"), sem("wo_in"), sem("bo_in"), sem("last_in"),
                                                        sem("choices_in"))
        weights_in = [sem(f"weights_in{i}") for i in range(2)]
        consts, policy_dve, last_rstd_ready = sem("consts"), sem("policy_dve"), sem("last_rstd_ready")
        policy_pe, policy_act, bo_scaled = sem("policy_pe"), sem("policy_act"), sem("bo_scaled")
        stats_ready, moments_ready, var_ready, rstd_ready, xn_ready = (
            sem("stats_ready"), sem("moments_ready"), sem("var_ready"), sem("rstd_ready"), sem("xn_ready"))
        turned, xT_ready, h_sum, hT_ready, r_sum, rT_ready, o_sum, x_done, residual = (
            sem("turned"), sem("xT_ready"), sem("h_sum"), sem("hT_ready"), sem("r_sum"), sem("rT_ready"),
            sem("o_sum"), sem("x_done"), sem("residual"))

        def batches(eng, batch):
            batch(0, 0, True, False)
            with eng.Fori(0, (B - 2) // 2) as i:
                batch(i * 2 + 1, 1, False, False)
                batch(i * 2 + 2, 0, False, False)
            batch(B - 1, (B - 1) % 2, False, True)

        def tiles(b, t, n):
            return x[:, bass.ds(b * NT + t, n), :]

        block = ctx.enter_context(nc.Block())

        @block.sync
        def _(sp):
            sp.dma_start(last[:], x[P - 1:P, NT - 1:B * NT:NT, :]).then_inc(last_in, 16)
            sp.dma_start(pw1[:], io["pw1"].rearrange("(c p) n -> p c n", p=P)).then_inc(policy_in, 16)
            sp.dma_start(pb1[:], io["pb1"]).then_inc(policy_in, 16)
            sp.dma_start(pw2[:], io["pw2"]).then_inc(policy_in, 16)
            sp.dma_start(pb2[:], io["pb2"].to_broadcast([B, E])).then_inc(policy_in, 16)
            sp.dma_start(bo[:], io["fbo"].to_broadcast([P, D])).then_inc(bo_in, 16)
            sp.dma_start(wo[:], io["fwo"].rearrange("(c p) n -> p c n", p=P)).then_inc(wo_in, 16)
            sp.wait_ge(policy_dve, 13)
            sp.dma_start(choices[:, :], choice[:, :]).then_inc(choices_in, 16)
            sp.wait_ge(choices_in, 16)

            def load(bb, par):
                e = sp.value_load(choices[0:1, bass.ds(bb, 1)], min_val=0, max_val=E - 1)
                sp.dma_start(w1[par][:], io["fw1"][bass.ds(e, 1)].rearrange("a (c p) f -> p (a c) f", p=P)
                             ).then_inc(weights_in[par], 16)
                sp.dma_start(b1[par][:], io["fb1"][bass.ds(e, 1)].rearrange("a p c -> p (a c)")
                             ).then_inc(weights_in[par], 16)
                sp.dma_start(w2[par][:], io["fw2"][bass.ds(e, 1)].rearrange("a (c p) f -> p (a c) f", p=P)
                             ).then_inc(weights_in[par], 16)
                sp.dma_start(b2[par][:], io["fb2"][bass.ds(e, 1)].rearrange("a p c -> p (a c)")
                             ).then_inc(weights_in[par], 16)

            load(0, 0)

            def batch(b, par, first, last):
                if not last:
                    if not first:
                        sp.wait_ge(rT_ready, b * KC)
                    load(b + 1, 1 - par)

            batches(sp, batch)

        @block.gpsimd
        def _(pool):
            nc.gpsimd.memset(minus_half[:], -0.5).then_inc(consts, 1)
            nc.gpsimd.iota(countdown[:], pattern=[[-1, E]], base=E, channel_multiplier=0,
                           allow_small_or_imprecise_dtypes=True).then_inc(consts, 1)
            pool.wait_ge(consts, 2)
            pool.wait_ge(policy_dve, 3)
            nc.gpsimd.tensor_tensor(last_rstd[:], last_var[:], minus_half[0:B, 0:1], ALU.pow).then_inc(last_rstd_ready, 1)

            def invert_deviation(bb):
                pool.wait_ge(var_ready, bb + 1)
                nc.gpsimd.tensor_tensor(rstd[:], var_eps[:], minus_half[:], ALU.pow).then_inc(rstd_ready, 1)

            pool.wait_ge(last_rstd_ready, 1)
            invert_deviation(0)
            pool.wait_ge(bo_scaled, 1)

            def batch(b, par, first, last):
                if not last:
                    invert_deviation(b + 1)
                pool.wait_ge(xn_ready, b * NT + NT)
                nc.gpsimd.tensor_tensor(tiles(b, 0, NT), tiles(b, 0, NT), xn[par][:], ALU.add).then_inc(residual, 1)
                for t in reversed(range(NT)):
                    tile = tiles(b, t, 1).rearrange("p a n -> p (a n)")
                    if t == NT - 1:
                        pool.wait_ge(residual, b * (NT + 1) + 1)
                    nc.gpsimd.tensor_tensor(tile, tile, bo[:], ALU.add).then_inc(residual, 1)

            batches(pool, batch)

        @block.vector
        def _(dve):
            step = [0]

            def chained(ins):
                step[0] += 1
                ins.then_inc(policy_dve, 1)
                dve.wait_ge(policy_dve, step[0])

            dve.wait_ge(last_in, 16)
            chained(nc.vector.bn_stats(last_stats[:], last[:]))
            chained(nc.vector.bn_aggr(last_moments[:], last_stats[:]))
            chained(nc.vector.tensor_scalar(last_var[:], last_moments[:, 1:2], EPS, None, ALU.add))
            dve.wait_ge(last_rstd_ready, 1)
            chained(nc.vector.tensor_scalar(last[:], last[:], last_moments[:, 0:1], last_rstd[:], ALU.subtract, ALU.mult))
            dve.wait_ge(policy_pe, 1)
            chained(nc.vector.tensor_copy(lastT[:], ps_t[0][:, 0:KC * B].rearrange("p (c b) -> p c b", c=KC)))

            def statistics(bb):
                for t in range(NT):
                    nc.vector.bn_stats(stats[:, t, :], tiles(bb, t, 1).rearrange("p a n -> p (a n)")
                                       ).then_inc(stats_ready, 1)
                dve.wait_ge(stats_ready, bb * NT + NT)
                nc.vector.memset(var_eps[:], EPS).then_inc(moments_ready, 1)
                for t in range(NT):
                    nc.vector.bn_aggr(moments[:, t, :], stats[:, t, :]).then_inc(moments_ready, 1)
                dve.wait_ge(moments_ready, bb * (NT + 1) + (NT + 1))
                nc.vector.tensor_tensor(var_eps[:], moments[:, :, 1], var_eps[:], ALU.add).then_inc(var_ready, 1)

            def centre(bb, par):
                dve.wait_ge(rstd_ready, bb + 1)
                for t in range(NT):
                    nc.vector.tensor_scalar(xn[par][:, t, :], tiles(bb, t, 1).rearrange("p a n -> p (a n)"),
                                            moments[:, t, 0:1], rstd[:, t:t + 1], ALU.subtract, ALU.mult
                                            ).then_inc(xn_ready, 1)

            statistics(0)
            centre(0, 0)
            dve.wait_ge(bo_in, 16)
            nc.vector.tensor_scalar(bo[:], bo[:], OUT_SCALE, None, ALU.mult).then_inc(bo_scaled, 1)
            dve.wait_ge(policy_pe, 3)
            dve.wait_ge(policy_in, 64)
            chained(nc.vector.tensor_tensor(logits[:], ps_t[0][0:B, 32:32 + E], pb2[:], ALU.add))
            chained(nc.vector.tensor_reduce(neg_top[:], logits[:], AX.X, ALU.max, negate=True))
            dve.wait_ge(policy_act, 2)
            chained(nc.vector.reciprocal(inv_total[:], total[:]))
            chained(nc.vector.tensor_scalar(policy[:], exps[:], inv_total[:], None, ALU.mult))
            chained(nc.vector.tensor_reduce(top[:], policy[:], AX.X, ALU.max))
            dve.wait_ge(consts, 2)
            chained(nc.vector.scalar_tensor_tensor(winner[:], policy[:], top[:], countdown[:], ALU.is_equal, ALU.mult))
            chained(nc.vector.tensor_reduce(choice_f[:], winner[:], AX.X, ALU.max))
            nc.vector.tensor_scalar(choice[:], choice_f[:], -1.0, float(E), ALU.mult, ALU.add).then_inc(policy_dve, 1)

            for t in range(2):
                nc.vector.engine_nop().then_inc(x_done, 1)

            def output(b, t):
                dve.wait_ge(o_sum, b * 2 + (t + 1))
                if t == 0:
                    dve.wait_ge(residual, b * (NT + 1) + (NT + 1))
                nc.vector.scalar_tensor_tensor(tiles(b, 2 * t, 2).rearrange("p t n -> p (t n)"), ps_o[t][:], OUT_SCALE,
                                               tiles(b, 2 * t, 2).rearrange("p t n -> p (t n)"), ALU.mult, ALU.add
                                               ).then_inc(x_done, 1)

            def batch(b, par, first, last):
                if not last:
                    statistics(b + 1)
                    if not first:
                        dve.wait_ge(turned, b * KC)
                        dve.wait_ge(residual, b * (NT + 1))
                    centre(b + 1, 1 - par)
                if not first:
                    output(b - 1, 0)
                    output(b - 1, 1)

            batches(dve, batch)
            output(B - 1, 0)
            output(B - 1, 1)

        @block.scalar
        def _(act):
            act.wait_ge(policy_in, 64)
            act.wait_ge(policy_pe, 2)
            nc.scalar.activation(hiddenT[:], ps_t[0][:, 64:64 + B], ACT.Gelu, bias=pb1[:, 0:1]).then_inc(policy_act, 1)
            act.wait_ge(policy_dve, 7)
            nc.scalar.activation(exps[:], logits[:], ACT.Exp, bias=neg_top[:], accum_out=total[:]).then_inc(policy_act, 1)

            def transposed(bb, par):
                for c in range(KC):
                    act.wait_ge(turned, bb * KC + (c + 1))
                    nc.scalar.copy(xT[par][:, c, :], ps_t[c][:]).then_inc(xT_ready, 1)

            transposed(0, 0)

            def batch(b, par, first, last):
                for f in range(FC):
                    act.wait_ge(h_sum, b * FC + (f + 1))
                    if f == 0:
                        act.wait_ge(weights_in[par], (b - par) * 32 + 64)
                        if not first:
                            act.wait_ge(r_sum, b * KC)
                    nc.scalar.activation(hT[:, f, :], ps_h[f % 2][:], ACT.Gelu, bias=b1[par][:, f:f + 1]
                                         ).then_inc(hT_ready, 1)
                for c in range(KC):
                    act.wait_ge(r_sum, b * KC + (c + 1))
                    nc.scalar.activation(rT[par][:, c, :], ps_r[c][:], ACT.Identity, bias=b2[par][:, c:c + 1]
                                         ).then_inc(rT_ready, 1)
                if not last:
                    transposed(b + 1, 1 - par)

            batches(act, batch)

        @block.tensor
        def _(pe):
            pe.wait_ge(policy_dve, 4)
            for c in range(KC):
                mm = nc.tensor.transpose(ps_t[0][:, c * B:(c + 1) * B], last[:, c * P:(c + 1) * P], ident[0:B, 0:B])
            mm.then_inc(policy_pe, 1)
            pe.wait_ge(policy_dve, 5)
            pe.wait_ge(policy_in, 64)
            for c in range(KC):
                mm = nc.tensor.matmul(ps_t[0][:, 64:64 + B], pw1[:, c, :], lastT[:, c, :], start=(c == 0), stop=(c == KC - 1))
            mm.then_inc(policy_pe, 1)
            pe.wait_ge(policy_act, 1)
            nc.tensor.matmul(ps_t[0][0:B, 32:32 + E], hiddenT[:], pw2[:], start=True, stop=True).then_inc(policy_pe, 1)
            pe.wait_ge(policy_dve, 6)

            def transpose_x(bb, par):
                pe.wait_ge(xn_ready, bb * NT + NT)
                for c in range(KC):
                    if not (isinstance(bb, int) and bb == 0):
                        pe.wait_ge(xT_ready, (bb - 1) * KC + (c + 1))
                    for t in range(NT):
                        mm = nc.tensor.transpose(ps_t[c][:, t * P:(t + 1) * P], xn[par][:, t, c * P:(c + 1) * P], ident[:])
                    mm.then_inc(turned, 1)

            def up(b, par, first):
                pe.wait_ge(xT_ready, b * KC + KC)
                pe.wait_ge(weights_in[par], (b - par) * 32 + 64)
                for f in range(FC):
                    if not (first and f < 2):
                        pe.wait_ge(hT_ready, b * FC + (f - 1))
                    for c in range(KC):
                        mm = nc.tensor.matmul(ps_h[f % 2][:], w1[par][:, c, f * P:(f + 1) * P], xT[par][:, c, :],
                                              start=(c == 0), stop=(c == KC - 1))
                    mm.then_inc(h_sum, 1)

            def down(b, par, first):
                pe.wait_ge(hT_ready, b * FC + FC)
                for c in range(KC):
                    if not first:
                        pe.wait_ge(rT_ready, (b - 1) * KC + (c + 1))
                    for f in range(FC):
                        mm = nc.tensor.matmul(ps_r[c][:], w2[par][:, f, c * P:(c + 1) * P], hT[:, f, :],
                                              start=(f == 0), stop=(f == FC - 1))
                    mm.then_inc(r_sum, 1)

            def output(b, par):
                pe.wait_ge(rT_ready, b * KC + KC)
                for t in range(2):
                    pe.wait_ge(x_done, b * 2 + (t + 1))
                    for tt in range(2):
                        for c in range(KC):
                            mm = nc.tensor.matmul(ps_o[t][:, tt * D:(tt + 1) * D],
                                                  rT[par][:, c, (2 * t + tt) * P:(2 * t + tt + 1) * P], wo[:, c, :],
                                                  start=(c == 0), stop=(c == KC - 1))
                    mm.then_inc(o_sum, 1)

            transpose_x(0, 0)
            pe.wait_ge(wo_in, 16)

            def batch(b, par, first, last):
                up(b, par, first)
                if not first:
                    output(b - 1, 1 - par)
                down(b, par, first)
                if not last:
                    transpose_x(b + 1, 1 - par)

            batches(pe, batch)
            output(B - 1, (B - 1) % 2)


def sigmoid_attention(nc, io, x, ident, logits, n_rows, sum_rows):
    QUADS = NG * NT
    PV_LAG = 2
    ctx = ExitStack()
    with ctx:
        def sb(name, shape, dt=F32):
            return ctx.enter_context(nc.sbuf_tensor("c_" + name, shape, dt))

        def ps(name, shape, dt=F32):
            return ctx.enter_context(nc.psum_tensor("c_" + name, shape, dt))

        def sem(name):
            return ctx.enter_context(nc.semaphore("c_" + name))

        wq, wk, wv, wo = (sb(n, [P, KC, D]) for n in ("wq", "wk", "wv", "wo"))
        w_mean = sb("w_mean", [P, 2, KC * KC, HC])
        gq, bq, gk, bk, eps = (sb(n, [P, 1]) for n in ("gq", "bq", "gk", "bk", "eps"))
        bo = sb("bo", [P, D])
        average = sb("average", [P, 4, HC])
        spread = sb("spread", [P, HD, HC])
        ctxT = sb("ctxT", [P, KC, S])
        wr, br = sb("wr", [P, KC, NE]), sb("br", [P, NE])
        stats, moments = sb("stats", [P, NT, 6]), sb("moments", [P, NT, 2])
        var_eps, rstd, minus_half = sb("var_eps", [P, NT]), sb("rstd", [P, NT]), sb("minus_half", [P, NT])
        xn, xT = sb("xn", [P, NT, D]), sb("xT", [P, KC, S])
        proj, square = sb("proj", [P, 4, S]), sb("square", [P, 4, S])
        head_std, head_rstd = sb("head_std", [P, S]), sb("head_rstd", [P, S])
        rest = sb("rest", [P, 2, S])
        parts = sb("parts", [P, 2, 3, S], BF16)
        q_stack = [sb(f"q_stack{i}", [K_MASK, H, S], BF16) for i in range(2)]
        k_stack = [sb(f"k_stack{i}", [K_MASK, H, S], BF16) for i in range(2)]
        v_pad = [sb(f"v_pad{i}", [P, NT, HC, 2, 2 * HD]) for i in range(2)]
        probs = sb("probs", [P, NT, HG, S])
        oT = sb("oT", [P, KC, S])

        ps_score = [ps(f"score{i}", [P, S]) for i in range(HG)]
        ps_pv = [ps(f"pv{i}", [P, S]) for i in range(KC)]
        ps_a = ps("act", [P, S])
        ps_d = ps("dve", [P, S])

        w_in, ctx_in = sem("w_in"), sem("ctx_in")
        consts, v_consts, means, centred, eps_set = (sem("consts"), sem("v_consts"), sem("means"), sem("centred"),
                                                     sem("eps_set"))
        stats_ready, moments_ready, var_ready, rstd_ready, xn_ready = (
            sem("stats_ready"), sem("moments_ready"), sem("var_ready"), sem("rstd_ready"), sem("xn_ready"))
        a_ready, a_empty, d_ready, d_empty = sem("a_ready"), sem("a_empty"), sem("d_ready"), sem("d_empty")
        squared, head_rstd_ready, scaled = sem("squared"), sem("head_rstd_ready"), sem("scaled")
        part0, rest_ready, part1, part2 = sem("part0"), sem("rest_ready"), sem("part1"), sem("part2")
        stacked = [sem(f"stacked{i}") for i in range(2)]
        score_ready, probs_ready, pv_ready, ot_ready = (sem("score_ready"), sem("probs_ready"), sem("pv_ready"),
                                                        sem("ot_ready"))
        residual = sem("residual")
        row_stats, row_moments, row_var, row_rstd, rows_ready = (
            sem("row_stats"), sem("row_moments"), sem("row_var"), sem("row_rstd"), sem("rows_ready"))
        router_in, rows_out = sem("router_in"), sem("rows_out")

        def batches(eng, batch):
            batch(0, 0, True, False)
            with eng.Fori(0, (B - 2) // 2) as i:
                batch(i * 2 + 1, 1, False, False)
                batch(i * 2 + 2, 0, False, False)
            batch(B - 1, (B - 1) % 2, False, True)

        KEYS0, KEYS1, XT0, XT1, QUERIES0, QUERIES1, VARIANCES, V0, V1 = range(9)
        A_ITEMS = 9
        PROJ = ((KEYS0, False, 0), (KEYS1, False, 1), (QUERIES0, True, 0), (QUERIES1, True, 1))
        D_FIRST = ("std0", "std1", "std2", "std3")
        D_ROWS = ("turn0", "turn1", "route")
        D_LATER = ("out0", "out1") + D_FIRST + D_ROWS
        D_LAST = ("out0", "out1") + D_ROWS
        D_END = 2 * len(D_FIRST) + (B - 2) * len(D_LATER) + len(D_LAST)

        def d_before(b):
            return (b - 1) * len(D_LATER) + 2 * len(D_FIRST)

        def d_item(b, first, last, name):
            if first:
                return len(D_FIRST) + D_FIRST.index(name)
            return d_before(b) + (D_LAST if last else D_LATER).index(name)

        def head_of(g, hh):
            return HC * (g // 2) + 2 * hh + g % 2

        AT = {KEYS0: 0, KEYS1: 1, XT0: 2, XT1: 3, QUERIES0: 4, QUERIES1: 5, VARIANCES: 7, V0: 13, V1: 14}
        STD_AT = (9, 10, 11, 12)
        OUT_AT = (3, 5)
        ROW_STATS_AT, ROWS_AT, TURN_AT, ROUTE_AT = 7, 10, (13, 14), 15

        block = ctx.enter_context(nc.Block())

        @block.sync
        def _(sp):
            def load(bb):
                sp.dma_start(ctxT[:], io["ctxT"][bass.ds(bb, 1)].rearrange("a (c p) n -> p (a c) n", p=P)
                             ).then_inc(ctx_in, 16)

            def stack(bb, par, k):
                _, is_q, c = PROJ[k]
                dst = (q_stack if is_q else k_stack)[par]
                for part, ready in enumerate((part0, part1, part2)):
                    sp.wait_ge(ready, bb * 4 + (k + 1))
                    for j in range(PAIRS):
                        if (Q_PARTS if is_q else K_PARTS)[j] == part:
                            sp.dma_start(dst[HD * j:HD * (j + 1), HC * c:HC * (c + 1), :],
                                         parts[:, k % 2, part, :]).then_inc(stacked[k % 2], 16)

            sp.dma_start(wk[:], io["swk"].rearrange("(c p) n -> p c n", p=P)).then_inc(w_in, 16)
            sp.dma_start(wq[:], io["swq"].rearrange("(c p) n -> p c n", p=P)).then_inc(w_in, 16)
            load(0)
            for dst, name in ((gq, "sgq"), (bq, "sbq"), (gk, "sgk"), (bk, "sbk")):
                sp.dma_start(dst[:], io[name]).then_inc(w_in, 16)
            sp.dma_start(wv[:], io["swv"].rearrange("(c p) n -> p c n", p=P)).then_inc(w_in, 16)
            sp.dma_start(wo[:], io["swp"].rearrange("(c p) n -> p c n", p=P)).then_inc(w_in, 16)
            sp.dma_start(bo[:], io["sbp"].to_broadcast([P, D])).then_inc(w_in, 16)
            sp.dma_start(wr[:], io["mwr"].rearrange("(c p) n -> p c n", p=P)).then_inc(router_in, 16)
            sp.dma_start(br[:], io["mbr"].to_broadcast([P, NE])).then_inc(router_in, 16)
            for k in range(4):
                stack(0, 0, k)

            def rows_to_dram(r):
                sp.wait_ge(rows_ready, r * NT + NT)
                for rows in (n_rows, sum_rows):
                    sp.dma_start(rows[bass.ds(r * S, S), :].rearrange("(t p) d -> p t d", p=P), xn[:]).then_inc(rows_out, 16)

            def batch(b, par, first, last):
                if not last:
                    sp.wait_ge(a_ready, b * A_ITEMS + A_ITEMS)
                    load(b + 1)
                    if not first:
                        sp.wait_ge(score_ready, b * 64)
                    for k in range(4):
                        stack(b + 1, 1 - par, k)
                        if k == 1 and not first:
                            rows_to_dram(b - 1)
                else:
                    rows_to_dram(b - 1)

            batches(sp, batch)
            rows_to_dram(B - 1)
            sp.wait_ge(rows_out, 32 * B + 1)

        @block.scalar
        def _(act):
            def evacuate(bb, item):
                act.wait_ge(a_ready, bb * A_ITEMS + (item + 1))
                if item in (XT0, XT1):
                    if item == XT0 and not (isinstance(bb, int) and bb < 2):
                        act.wait_ge(d_ready, d_before(bb - 1))
                    nc.scalar.copy(xT[:, item - XT0, :], ps_a[:]).then_inc(a_empty, 1)
                elif item == VARIANCES:
                    nc.scalar.activation(head_std[:], ps_a[:], ACT.Sqrt, bias=eps[:, 0:1]).then_inc(a_empty, 1)
                elif item in (V0, V1):
                    raise ValueError(item)
                else:
                    k = [i[0] for i in PROJ].index(item)
                    if not (isinstance(bb, int) and bb == 0):
                        act.wait_ge(rest_ready, (bb - 1) * 4 + (k + 1))
                    nc.scalar.copy(proj[:, k, :], ps_a[:]).then_inc(squared, 1)
                    nc.scalar.activation(square[:, k, :], ps_a[:], ACT.Square).then_inc(a_empty, 1)

            def v_tiles(bb, par, t):
                act.wait_ge(a_ready, bb * A_ITEMS + (V0 + t + 1))
                for odd in range(2):
                    ins = nc.scalar.copy(
                        v_pad[par][:, 2 * t:2 * t + 2, :, odd, HD * odd:HD * (odd + 1)],
                        ps_a[:].rearrange("p (t h o d) -> p t h o d", t=2, h=HC, o=2)[:, :, :, odd, :])
                    ins.then_inc(squared if odd == 0 else a_empty, 1)

            act.wait_ge(eps_set, 1)
            act.wait_ge(v_consts, 4)
            for item in range(V0):
                evacuate(0, item)
            v_tiles(0, 0, 0), v_tiles(0, 0, 1)

            def batch(b, par, first, last):
                for u in range(QUADS):
                    kc = u % NT
                    quad = b * QUADS + u
                    for hh in range(HG):
                        act.wait_ge(score_ready, quad * HG + (hh + 1))
                        if hh == 0 and not (first and u < NT):
                            act.wait_ge(pv_ready, quad + (1 - NT))
                        nc.scalar.activation(probs[:, kc, hh, :], ps_score[hh][:], ACT.Sigmoid, scale=SCALE
                                             ).then_inc(probs_ready, 1)
                    if not last:
                        for item in range(V0):
                            if AT[item] == u:
                                evacuate(b + 1, item)
                        for t in range(2):
                            if AT[V0 + t] == u:
                                v_tiles(b + 1, 1 - par, t)

            batches(act, batch)

        @block.gpsimd
        def _(pool):
            nc.gpsimd.memset(minus_half[:], -0.5).then_inc(consts, 1)
            nc.gpsimd.iota(average[:], pattern=[[0, 4], [-1, HC]], base=P, channel_multiplier=1,
                           allow_small_or_imprecise_dtypes=True).then_inc(consts, 1)
            nc.gpsimd.iota(spread[:], pattern=[[0, HD], [-1, HC]], base=P, channel_multiplier=1,
                           allow_small_or_imprecise_dtypes=True).then_inc(consts, 1)

            def invert_deviation(bb):
                pool.wait_ge(var_ready, bb + 1)
                nc.gpsimd.tensor_tensor(rstd[:], var_eps[:], minus_half[:], ALU.pow).then_inc(rstd_ready, 1)

            def remainder(bb, k):
                pool.wait_ge(part0, bb * 4 + (k + 1))
                if k >= 2:
                    pool.wait_ge(part2, bb * 4 + (k - 1))
                nc.gpsimd.tensor_tensor(rest[:, k % 2, :], proj[:, k, :], parts[:, k % 2, 0, :], ALU.subtract
                                        ).then_inc(rest_ready, 1)

            def third(bb, k):
                pool.wait_ge(part1, bb * 4 + (k + 1))
                nc.gpsimd.tensor_tensor(parts[:, k % 2, 2, :], rest[:, k % 2, :], parts[:, k % 2, 1, :], ALU.subtract
                                        ).then_inc(part2, 1)

            def invert_row_deviation(r):
                pool.wait_ge(row_var, r + 1)
                nc.gpsimd.tensor_tensor(rstd[:], var_eps[:], minus_half[:], ALU.pow).then_inc(row_rstd, 1)

            def prepare(bb, row):
                invert_deviation(bb)
                if row is not None:
                    invert_row_deviation(row)
                for k in range(4):
                    remainder(bb, k)
                    third(bb, k)

            pool.wait_ge(consts, 3)
            prepare(0, None)

            def batch(b, par, first, last):
                for t in range(NT):
                    tile = x[:, bass.ds(b * NT + t, 1), :].rearrange("p a n -> p (a n)")
                    if t == 0:
                        pool.wait_ge(xn_ready, b * NT + NT)
                        pool.wait_ge(w_in, 16 * 9)
                    nc.gpsimd.tensor_tensor(tile, tile, bo[:], ALU.add).then_inc(residual, 1)
                if not last:
                    prepare(b + 1, None if first else b - 1)
                else:
                    invert_row_deviation(b - 1)

            batches(pool, batch)
            invert_row_deviation(B - 1)

        @block.vector
        def _(dve):
            def statistics(bb):
                for t in range(NT):
                    nc.vector.bn_stats(stats[:, t, :], x[:, bass.ds(bb * NT + t, 1), :].rearrange("p a n -> p (a n)")
                                       ).then_inc(stats_ready, 1)
                dve.wait_ge(stats_ready, bb * NT + NT)
                nc.vector.memset(var_eps[:], EPS).then_inc(moments_ready, 1)
                for t in range(NT):
                    nc.vector.bn_aggr(moments[:, t, :], stats[:, t, :]).then_inc(moments_ready, 1)
                dve.wait_ge(moments_ready, bb * (NT + 1) + (NT + 1))
                nc.vector.tensor_tensor(var_eps[:], moments[:, :, 1], var_eps[:], ALU.add).then_inc(var_ready, 1)

            def centre(bb):
                dve.wait_ge(rstd_ready, bb + 1)
                if not (isinstance(bb, int) and bb == 0):
                    dve.wait_ge(a_ready, (bb - 1) * A_ITEMS + (XT1 + 1))
                if not (isinstance(bb, int) and bb < 2):
                    dve.wait_ge(rows_out, (bb - 2) * 32 + 1)
                    dve.wait_ge(d_ready, d_before(bb - 1))
                for t in range(NT):
                    nc.vector.tensor_scalar(xn[:, t, :], x[:, bass.ds(bb * NT + t, 1), :].rearrange("p a n -> p (a n)"),
                                            moments[:, t, 0:1], rstd[:, t:t + 1], ALU.subtract, ALU.mult
                                            ).then_inc(xn_ready, 1)

            def invert_std(bb):
                dve.wait_ge(a_empty, bb * A_ITEMS + (VARIANCES + 1))
                if not (isinstance(bb, int) and bb == 0):
                    spread_before = len(D_FIRST) if isinstance(bb, int) and bb == 1 else d_before(bb - 1)
                    dve.wait_ge(d_ready, spread_before)
                nc.vector.reciprocal(head_rstd[:], head_std[:]).then_inc(head_rstd_ready, 1)

            def scale(bb, k, d):
                _, is_q, _ = PROJ[k]
                n = bb * 4 + k
                dve.wait_ge(d_ready, d + 1)
                nc.vector.tensor_tensor(proj[:, k, :], proj[:, k, :], ps_d[:], ALU.mult).then_inc(d_empty, 1)
                dve.wait_ge(d_empty, d + 1)
                nc.vector.tensor_scalar(proj[:, k, :], proj[:, k, :], (gq if is_q else gk)[:, 0:1],
                                        (bq if is_q else bk)[:, 0:1], ALU.mult, ALU.add).then_inc(scaled, 1)
                dve.wait_ge(scaled, n + 1)
                dve.wait_ge(stacked[k % 2], bb * 192 + 96 * (k // 2))
                nc.vector.tensor_copy(parts[:, k % 2, 0, :], proj[:, k, :]).then_inc(part0, 1)

            def second(bb, k):
                dve.wait_ge(rest_ready, bb * 4 + (k + 1))
                nc.vector.tensor_copy(parts[:, k % 2, 1, :], rest[:, k % 2, :]).then_inc(part1, 1)

            def heads_out(b, c):
                dve.wait_ge(pv_ready, b * QUADS + 8 * (c + 1))
                if not (isinstance(b, int) and b == 0) and c == 0:
                    dve.wait_ge(d_ready, d_before(b) + 2)
                nc.vector.tensor_copy(oT[:, c, :], ps_pv[c][:]).then_inc(ot_ready, 1)

            def output(b, t, d):
                dve.wait_ge(d_ready, d + 1)
                dve.wait_ge(residual, b * NT + NT)
                two = x[:, bass.ds(b * NT + 2 * t, 2), :]
                nc.vector.tensor_tensor(two, ps_d[:].rearrange("p (t n) -> p t n", t=2), two, ALU.add).then_inc(d_empty, 1)

            def row_statistics(r, out_item):
                dve.wait_ge(d_empty, out_item + 1)
                nc.vector.memset(var_eps[:, 0:2], EPS).then_inc(row_moments, 1)
                for t in range(NT):
                    nc.vector.bn_stats(stats[:, t, :], x[:, bass.ds(r * NT + t, 1), :].rearrange("p a n -> p (a n)")
                                       ).then_inc(row_stats, 1)
                dve.wait_ge(row_stats, r * NT + NT)
                nc.vector.memset(var_eps[:, 2:NT], EPS).then_inc(row_moments, 1)
                for t in range(NT):
                    nc.vector.bn_aggr(moments[:, t, :], stats[:, t, :]).then_inc(row_moments, 1)
                dve.wait_ge(row_moments, r * (NT + 2) + (NT + 2))
                nc.vector.tensor_tensor(var_eps[:], moments[:, :, 1], var_eps[:], ALU.add).then_inc(row_var, 1)

            def normalised_rows(r):
                dve.wait_ge(row_rstd, r + 1)
                for t in range(NT):
                    nc.vector.tensor_scalar(xn[:, t, :], x[:, bass.ds(r * NT + t, 1), :].rearrange("p a n -> p (a n)"),
                                            moments[:, t, 0:1], rstd[:, t:t + 1], ALU.subtract, ALU.mult
                                            ).then_inc(rows_ready, 1)

            def turned_rows(c, d):
                dve.wait_ge(d_ready, d + 1)
                nc.vector.tensor_copy(xT[:, c, :], ps_d[:]).then_inc(d_empty, 1)

            def routed(r, d):
                dve.wait_ge(d_ready, d + 1)
                nc.vector.tensor_tensor(logits[:, :, bass.ds(r * NT, NT)].rearrange("p e t -> p t e"),
                                        ps_d[:, 0:NT * NE].rearrange("p (t e) -> p t e", t=NT),
                                        bass.AP(br[:].tensor, br[:].offset, [br[:].ap[0], [0, NT], [1, NE]]), ALU.add
                                        ).then_inc(d_empty, 1)

            nc.vector.engine_nop().then_inc(rows_out, 1)
            for i in range(2):
                for odd in range(2):
                    nc.vector.memset(v_pad[i][:, :, :, odd, HD * (1 - odd):HD * (2 - odd)], 0.0).then_inc(v_consts, 1)
            nc.vector.memset(eps[:], EPS).then_inc(eps_set, 1)
            dve.wait_ge(w_in, 16 * 9)
            for i, w in enumerate((wk, wq)):
                by_head = w[:].rearrange("p c (k d h) -> p (c k) h d", d=HD, h=HC)
                nc.vector.tensor_reduce(w_mean[:, i], by_head, AX.X, ALU.add).then_inc(means, 1)
                dve.wait_ge(means, 2 * i + 1)
                nc.vector.tensor_scalar(w_mean[:, i], w_mean[:, i], 1.0 / HD, None, ALU.mult).then_inc(means, 1)
                dve.wait_ge(means, 2 * i + 2)
                for ck in range(KC * KC):
                    part = w[:, ck // KC, P * (ck % KC):P * (ck % KC + 1)].rearrange("p (d h) -> p d h", d=HD)
                    mean = w_mean[:, i, ck:ck + 1, :]
                    mean = bass.AP(mean.tensor, mean.offset, [mean.ap[0], [0, HD], [1, HC]])
                    nc.vector.tensor_tensor(part, part, mean, ALU.subtract).then_inc(centred, 1)
            dve.wait_ge(consts, 3)
            for i, (m, value) in enumerate(((average, 1.0 / HD), (spread, 1.0))):
                m32 = m[:].rearrange("p a h -> p (a h)")
                as_int = proj[:, 2 * i, 0:m32.shape[1]].bitcast(I32)
                nc.vector.tensor_copy(as_int, m32).then_inc(means, 1)
                dve.wait_ge(means, 5 + 3 * i)
                nc.vector.tensor_scalar(as_int, as_int, HC - 1, None, ALU.bitwise_and).then_inc(means, 1)
                dve.wait_ge(means, 6 + 3 * i)
                nc.vector.tensor_scalar(m32, as_int, 0.0, value, ALU.is_equal, ALU.mult).then_inc(means, 1)
            statistics(0)
            centre(0)
            invert_std(0)
            for k in range(4):
                scale(0, k, k)
                second(0, k)

            def batch(b, par, first, last):
                for u in range(QUADS):
                    if not last:
                        if u == 0:
                            statistics(b + 1)
                        if u == 1:
                            centre(b + 1)
                    if u == 2 and not first:
                        heads_out(b - 1, 1)
                    if u == 10:
                        heads_out(b, 0)
                    if not last and u == AT[VARIANCES] + 1:
                        invert_std(b + 1)
                    for t in range(2):
                        if not first and u == OUT_AT[t]:
                            output(b - 1, t, d_item(b, first, last, f"out{t}"))
                    for k in range(4):
                        if not last and u == STD_AT[k]:
                            scale(b + 1, k, d_item(b, first, last, f"std{k}"))
                            second(b + 1, k)
                    if not first:
                        if u == ROW_STATS_AT:
                            row_statistics(b - 1, d_item(b, first, last, "out1"))
                        if u == ROWS_AT:
                            if last:
                                dve.wait_ge(rows_out, (b - 1) * 32 + 1)
                                dve.wait_ge(d_ready, d_before(b))
                            else:
                                dve.wait_ge(a_ready, b * A_ITEMS + (A_ITEMS + QUERIES1 + 1))
                            normalised_rows(b - 1)
                        for c in range(KC):
                            if u == TURN_AT[c]:
                                turned_rows(c, d_item(b, first, last, f"turn{c}"))
                        if u == ROUTE_AT:
                            dve.wait_ge(router_in, 32)
                            routed(b - 1, d_item(b, first, last, "route"))

            batches(dve, batch)
            heads_out(B - 1, 1)
            for t in range(2):
                output(B - 1, t, D_END + t)
            row_statistics(B - 1, D_END + 1)
            dve.wait_ge(rows_out, (B - 1) * 32 + 1)
            dve.wait_ge(d_ready, D_END)
            normalised_rows(B - 1)
            for c in range(KC):
                turned_rows(c, D_END + 2 + c)
            routed(B - 1, D_END + 2 + KC)

        @block.tensor
        def _(pe):
            def take_act(bb, item):
                if not (isinstance(bb, int) and bb * A_ITEMS + item == 0):
                    pe.wait_ge(a_empty, bb * A_ITEMS + item)

            def prepare(bb, item):
                take_act(bb, item)
                if item in (XT0, XT1):
                    c = item - XT0
                    pe.wait_ge(xn_ready, bb * NT + NT)
                    for t in range(NT):
                        mm = nc.tensor.transpose(ps_a[:, t * P:(t + 1) * P], xn[:, t, c * P:(c + 1) * P], ident[:])
                elif item == VARIANCES:
                    for k in range(4):
                        mm = nc.tensor.matmul(ps_a[32 * k:32 * k + 32, :], average[:].rearrange("p a h -> p (a h)"),
                                              square[:, k, :], start=True, stop=True, tile_position=(0, 32 * k))
                elif item in (V0, V1):
                    for tt in range(2):
                        for kk in range(KC):
                            at = 2 * (item - V0) + tt
                            mm = nc.tensor.matmul(ps_a[:, tt * D:(tt + 1) * D], ctxT[:, kk, at * P:(at + 1) * P],
                                                  wv[:, kk, :], start=(kk == 0), stop=(kk == KC - 1))
                else:
                    _, is_q, c = PROJ[[i[0] for i in PROJ].index(item)]
                    if not is_q:
                        pe.wait_ge(ctx_in, (bb + 1) * 16)
                    for kk in range(KC):
                        mm = nc.tensor.matmul(ps_a[:], (wq if is_q else wk)[:, kk, c * P:(c + 1) * P],
                                              (xT if is_q else ctxT)[:, kk, :], start=(kk == 0), stop=(kk == KC - 1))
                mm.then_inc(a_ready, 1)

            def spread_deviations(bb, k, d):
                pe.wait_ge(head_rstd_ready, bb + 1)
                if not (isinstance(d, int) and d == 0):
                    pe.wait_ge(d_empty, d)
                nc.tensor.matmul(ps_d[:], spread[32 * k:32 * k + HC].rearrange("p a h -> p (a h)"),
                                 head_rstd[32 * k:32 * k + HC, :], start=True, stop=True,
                                 tile_position=(32 * k, 0)).then_inc(d_ready, 1)

            def scores(b, par, u, hh):
                g, kc = divmod(u, NT)
                n = b * 64 + (4 * u + hh)
                h = head_of(g, hh)
                if u == 0 and hh == 0:
                    for i in range(2):
                        pe.wait_ge(stacked[i], b * 192 + 192)
                if not (isinstance(n, int) and n < HG):
                    pe.wait_ge(probs_ready, n + (1 - HG))
                nc.tensor.matmul(ps_score[hh][:], k_stack[par][:, h, kc * P:(kc + 1) * P], q_stack[par][:, h, :],
                                 start=True, stop=True).then_inc(score_ready, 1)

            def weighted_values(b, par, w):
                g, kc = divmod(w, NT)
                c, odd = divmod(g, 2)
                pe.wait_ge(probs_ready, b * 64 + (4 * w + 4))
                if w == 0:
                    pe.wait_ge(a_empty, b * A_ITEMS + A_ITEMS)
                if kc == 0 and odd == 0 and not (isinstance(b, int) and b == 0):
                    pe.wait_ge(ot_ready, b * KC + (c - 1))
                for hh in range(HG):
                    mm = nc.tensor.matmul(ps_pv[c][32 * hh:32 * hh + 32, :], v_pad[par][:, kc, HG * c + hh, odd, :],
                                          probs[:, kc, hh, :], start=(kc == 0 and odd == 0),
                                          stop=(kc == NT - 1 and odd == 1), tile_position=(0, 32 * hh))
                mm.then_inc(pv_ready, 1)

            def output(b, t, d):
                pe.wait_ge(ot_ready, b * KC + KC)
                pe.wait_ge(d_empty, d)
                for tt in range(2):
                    for c in range(KC):
                        mm = nc.tensor.matmul(ps_d[:, tt * D:(tt + 1) * D], oT[:, c, (2 * t + tt) * P:(2 * t + tt + 1) * P],
                                              wo[:, c, :], start=(c == 0), stop=(c == KC - 1))
                mm.then_inc(d_ready, 1)

            def turn_rows(r, c, d):
                pe.wait_ge(rows_ready, r * NT + NT)
                pe.wait_ge(d_empty, d)
                for t in range(NT):
                    mm = nc.tensor.transpose(ps_d[:, t * P:(t + 1) * P], xn[:, t, c * P:(c + 1) * P], ident[:])
                mm.then_inc(d_ready, 1)

            def route(d):
                pe.wait_ge(d_empty, d)
                for t in range(NT):
                    for c in range(KC):
                        mm = nc.tensor.matmul(ps_d[:, t * NE:(t + 1) * NE], xT[:, c, t * P:(t + 1) * P], wr[:, c, :],
                                              start=(c == 0), stop=(c == KC - 1))
                mm.then_inc(d_ready, 1)

            pe.wait_ge(w_in, 16 * 9)
            pe.wait_ge(centred, 2 * KC * KC)
            pe.wait_ge(means, 10)
            for item in range(A_ITEMS):
                prepare(0, item)
            for k in range(4):
                spread_deviations(0, k, k)

            def batch(b, par, first, last):
                for u in range(QUADS):
                    for half in range(2):
                        for hh in (2 * half, 2 * half + 1):
                            scores(b, par, u, hh)
                        if half == 0 and u >= PV_LAG:
                            weighted_values(b, par, u - PV_LAG)
                        elif half == 0 and not first:
                            weighted_values(b - 1, 1 - par, QUADS + u - PV_LAG)
                    for t in range(2):
                        if not first and u == OUT_AT[t]:
                            output(b - 1, t, d_item(b, first, last, f"out{t}"))
                    if not first:
                        for c in range(KC):
                            if u == TURN_AT[c]:
                                turn_rows(b - 1, c, d_item(b, first, last, f"turn{c}"))
                        if u == ROUTE_AT:
                            pe.wait_ge(router_in, 32)
                            route(d_item(b, first, last, "route"))
                    if not last:
                        for item in range(A_ITEMS):
                            if AT[item] == u:
                                prepare(b + 1, item)
                        for k in range(4):
                            if STD_AT[k] == u:
                                spread_deviations(b + 1, k, d_item(b, first, last, f"std{k}"))

            batches(pe, batch)
            for w in range(QUADS - PV_LAG, QUADS):
                weighted_values(B - 1, (B - 1) % 2, w)
            for t in range(2):
                output(B - 1, t, D_END + t)
            for c in range(KC):
                turn_rows(B - 1, c, D_END + 2 + c)
            route(D_END + 2 + KC)


def mixture(nc, io, x, ident, logits, n_rows, sum_rows, out):
    E, F = NE, 4 * D
    FC = F // P
    T = B * NT
    N = T * P
    CT = CAP // P
    assert CT * P == CAP
    outer = ExitStack()
    with outer:
        def sb(name, shape, dt=F32):
            return outer.enter_context(nc.sbuf_tensor("d_" + name, shape, dt))

        t = dict(
            gamma=sb("gamma", [P, D]), beta=sb("beta", [P, D]), b1=sb("b1", [P, E, FC]),
            w1=[sb(f"w1_{i}", [P, KC, F]) for i in range(2)], w2=[sb(f"w2_{i}", [P, FC, D]) for i in range(2)],
            minus_half=sb("minus_half", [P, T]),
            key=sb("key", [P, E, T]),
            gate_parts=sb("gate_parts", [P, 3, E, T], BF16),
            row=sb("row", [P, E, T]), lane=sb("lane", [P, E, T]),
            lanes=sb("lanes", [P, P]),
            rows_of=sb("rows_of", [P, CT]),
            numbers=sb("numbers", [P, 2, T]),
            spare=sb("spare", [P, CT]))
        weights_in = [outer.enter_context(nc.semaphore(f"d_weights_in{i}")) for i in range(2)]
        route(nc, io, x, ident, logits, n_rows, sum_rows, weights_in, E, F, FC, T, N, CT, **t)
        experts(nc, io, x, ident, n_rows, sum_rows, weights_in, E, F, FC, T, N, CT, out, **t)


def load_expert(sp, io, e, w1, w2, weights_in):
    sp.dma_start(w1[:], io["mw1"][bass.ds(e, 1)].rearrange("a (c p) f -> p (a c) f", p=P)).then_inc(weights_in, 16)
    sp.dma_start(w2[:], io["mw2"][bass.ds(e, 1)].rearrange("a (c p) f -> p (a c) f", p=P)).then_inc(weights_in, 16)


def repeated(ap, *pattern):
    return bass.AP(ap.tensor, ap.offset, [ap.ap[0], *[list(p) for p in pattern]])


def route(nc, io, x, ident, logits, n_rows, sum_rows, weights_in, E, F, FC, T, N, CT, gamma, beta, b1, w1, w2,
          minus_half, key, gate_parts, row, lane, lanes, rows_of, numbers, spare):
    LOW = -3.0e38
    BITS = 30
    STEPS, UNROLLED = 6, 5
    HALVES = 2
    EXPERTS = E // HALVES
    assert EXPERTS * T == P
    ctx = ExitStack()
    with ctx:
        def sb(name, shape, dt=F32):
            return ctx.enter_context(nc.sbuf_tensor("r_" + name, shape, dt))

        def ps(name, shape, dt=F32):
            return ctx.enter_context(nc.psum_tensor("r_ps_" + name, shape, dt))

        def sem(name):
            return ctx.enter_context(nc.semaphore("r_" + name))

        zeros = sb("zeros", [P, CT, D])
        work, work2, first, second = (sb(n, [P, E, T]) for n in ("work", "work2", "first", "second"))
        countdown = sb("countdown", [P, E])
        v1, v2, w_first, w_second = (sb(n, [P, T]) for n in ("v1", "v2", "w_first", "w_second"))
        gate_rest = sb("gate_rest", [P, E, T])
        keyT, above, ties, rank, taken = (sb(n, [P, HALVES, P]) for n in ("keyT", "above", "ties", "rank", "taken"))
        no_carry = sb("no_carry", [P, HALVES, P])
        threshold, step, candidate, enough = (sb(n, [P, HALVES], I32) for n in ("threshold", "step", "candidate", "enough"))
        count, tie_count, fits = sb("count", [P, HALVES], BF16), sb("tie_count", [P, HALVES], BF16), sb("fits", [P, HALVES])
        same, earlier = sb("same", [P, P], BF16), sb("earlier", [P, P], BF16)
        slot = sb("slot", [P, E, T])

        ps_key = [ps(f"key{h}", [P, S]) for h in range(HALVES)]
        ps_count, ps_earlier = ps("count", [P, S]), ps("earlier", [P, S])
        ps_slot = ps("slot", [P, S])

        consts, small_in, spare_out = sem("consts"), sem("small_in"), sem("spare_out")
        chain, exp_ready, search, counted = sem("chain"), sem("exp_ready"), sem("search"), sem("counted")
        key_ready, key_turned, ties_ready, ties_summed = sem("key_ready"), sem("key_turned"), sem("ties_ready"), sem("ties_summed")
        taken_ready, taken_summed, slot_ready, slot_turned = (sem("taken_ready"), sem("taken_summed"), sem("slot_ready"),
                                                              sem("slot_turned"))
        beta_added = sem("beta_added")

        def over_experts(ap):
            return repeated(ap, (0, E), (1, T))

        block = ctx.enter_context(nc.Block())

        @block.sync
        def _(sp):
            sp.dma_start(gamma[:], io["mgamma"].to_broadcast([P, D])).then_inc(small_in, 16)
            sp.dma_start(beta[:], io["mbeta"].to_broadcast([P, D])).then_inc(small_in, 16)
            sp.dma_start(b1[:], io["mb1"].rearrange("e p c -> p e c")).then_inc(small_in, 16)
            for e in range(2):
                load_expert(sp, io, e, w1[e], w2[e], weights_in[e])
            sp.wait_ge(consts, 1)
            for rows in (n_rows, sum_rows):
                sp.dma_start(rows[N:N + CAP, :].rearrange("(t p) d -> p t d", p=P), zeros[:]).then_inc(spare_out, 16)
            sp.wait_ge(small_in, 48)
            sp.wait_ge(spare_out, 32)

        @block.gpsimd
        def _(pool):
            def const(ins):
                const.n += 1
                ins.then_inc(consts, 1)
                pool.wait_ge(consts, const.n)
            const.n = 0
            fine = dict(allow_small_or_imprecise_dtypes=True)
            const(nc.gpsimd.memset(zeros[:], 0.0))
            const(nc.gpsimd.iota(countdown[:], pattern=[[-1, E]], base=E, channel_multiplier=0, **fine))
            const(nc.gpsimd.memset(same[:], 0.0))
            for k in range(EXPERTS):
                const(nc.gpsimd.memset(same[T * k:T * (k + 1), T * k:T * (k + 1)], 1.0))
            const(nc.gpsimd.affine_select(out=earlier[:], in_=same[:], compare_op=ALU.is_ge, fill=0.0, base=-1,
                                          pattern=[[1, P]], channel_multiplier=-1))
            const(nc.gpsimd.memset(no_carry[:], 1.0))
            const(nc.gpsimd.memset(no_carry[:, :, 0], 0.0))
            const(nc.gpsimd.memset(minus_half[:], -0.5))
            const(nc.gpsimd.iota(lanes[:], pattern=[[1, P]], base=0, channel_multiplier=0, **fine))
            const(nc.gpsimd.iota(rows_of[:], pattern=[[1, CT]], base=0, channel_multiplier=0, **fine))
            const(nc.gpsimd.iota(numbers[:, 0, :], pattern=[[1, T]], base=0, channel_multiplier=0, **fine))
            const(nc.gpsimd.iota(numbers[:, 1, :], pattern=[[0, T]], base=0, channel_multiplier=1, **fine))
            const(nc.gpsimd.iota(spare[:], pattern=[[P, CT]], base=N, channel_multiplier=1, **fine))
            pool.wait_ge(small_in, 48)
            with pool.Fori(0, T) as t:
                tile = x[:, bass.ds(t, 1), :].rearrange("p a n -> p (a n)")
                nc.gpsimd.tensor_tensor(tile, tile, beta[:], ALU.add).then_inc(beta_added, 1)

        @block.scalar
        def _(act):
            act.wait_ge(chain, 12)
            nc.scalar.activation(v2[:], v2[:], ACT.Exp).then_inc(exp_ready, 1)

        @block.vector
        def _(dve):
            class Chain:
                def __init__(self, sem, base=0):
                    self.sem, self.base, self.n = sem, base, 0

                def __call__(self, ins):
                    self.beside(ins)
                    dve.wait_ge(self.sem, self.base + self.n)

                def beside(self, ins):
                    self.n += 1
                    ins.then_inc(self.sem, 1)

            V = nc.vector
            flat = "p e t -> p (e t)"
            by_token = "p e t -> p t e"
            step_of = Chain(chain)
            preference = repeated(countdown[:], (1, E), (0, T))
            dve.wait_ge(consts, 2)

            def best(values, value, hot):
                step_of(V.tensor_tensor(work[:], values[:], over_experts(value[:]), ALU.is_equal))
                step_of(V.tensor_tensor(work[:], work[:], preference, ALU.mult))
                step_of(V.tensor_reduce(w_first[:], work[:].rearrange(by_token), AX.X, ALU.max))
                step_of(V.tensor_tensor(hot[:], work[:], over_experts(w_first[:]), ALU.is_equal))

            step_of(V.tensor_reduce(v1[:], logits[:].rearrange(by_token), AX.X, ALU.max))
            best(logits, v1, first)
            step_of(V.tensor_scalar(work[:], first[:], -1.0, 1.0, ALU.mult, ALU.add))
            step_of(V.tensor_tensor(work2[:], logits[:], work[:], ALU.mult))
            step_of(V.scalar_tensor_tensor(work2[:].rearrange(flat), first[:].rearrange(flat),
                                           LOW, work2[:].rearrange(flat), ALU.mult, ALU.add))
            step_of(V.tensor_reduce(v2[:], work2[:].rearrange(by_token), AX.X, ALU.max))
            step_of(V.tensor_tensor(work[:], work2[:], over_experts(v2[:]), ALU.is_equal))
            step_of(V.tensor_tensor(work[:], work[:], preference, ALU.mult))
            step_of(V.tensor_tensor(v2[:], v2[:], v1[:], ALU.subtract))
            step_of(V.tensor_reduce(w_first[:], work[:].rearrange(by_token), AX.X, ALU.max))
            step_of(V.tensor_tensor(second[:], work[:], over_experts(w_first[:]), ALU.is_equal))
            dve.wait_ge(exp_ready, 1)
            step_of(V.tensor_scalar(v1[:], v2[:], 1.0, None, ALU.add))
            step_of(V.reciprocal(w_first[:], v1[:]))
            step_of(V.tensor_tensor(w_second[:], v2[:], w_first[:], ALU.mult))
            step_of(V.tensor_tensor(key[:], first[:], over_experts(w_first[:]), ALU.mult))
            step_of(V.tensor_tensor(work[:], second[:], over_experts(w_second[:]), ALU.mult))
            step_of(V.tensor_tensor(key[:], key[:], work[:], ALU.add))
            step_of(V.tensor_tensor(work[:], first[:], second[:], ALU.add))
            step_of(V.tensor_scalar(work[:], work[:], -1.0, None, ALU.add))
            step_of(V.tensor_tensor(key[:], key[:], work[:], ALU.add))
            V.engine_nop().then_inc(key_ready, 1)
            step_of(V.memset(threshold[:], 0))
            step_of(V.memset(step[:], 1 << (BITS - 1)))
            for h in range(HALVES):
                dve.wait_ge(key_turned, h + 1)
                step_of(V.tensor_copy(keyT[:, h, :], ps_key[h][:, 0:P]))

            ctx.enter_context(nc.allow_low_precision(reason="counts of at most 128 columns are whole in bf16"))
            with dve.Fori(0, BITS // UNROLLED) as i:
                for j in range(UNROLLED):
                    bit = Chain(search, i * (STEPS * UNROLLED) + STEPS * j)
                    bit(V.tensor_tensor(candidate[:], threshold[:], step[:], ALU.bitwise_or))
                    for h in range(HALVES):
                        (bit if h else bit.beside)(V.tensor_scalar(
                            taken[:, h, :], keyT[:, h, :], candidate[:, h:h + 1].bitcast(F32), 0.0, ALU.is_ge, ALU.add,
                            accum_out=count[:, h:h + 1]))
                    dve.wait_ge(counted, i * UNROLLED + (j + 1))
                    bit(V.tensor_scalar(enough[:], ps_count[:, 0:HALVES], float(CAP), None, ALU.is_ge))
                    bit.beside(V.tensor_scalar(step[:], step[:], 1, None, ALU.logical_shift_right))
                    bit(V.copy_predicated(threshold[:], enough[:], candidate[:]))

            for h in range(HALVES):
                limit = threshold[:, h:h + 1].bitcast(F32)
                step_of.beside(V.tensor_scalar(above[:, h, :], keyT[:, h, :], limit, 0.0, ALU.is_gt, ALU.add,
                                               accum_out=count[:, h:h + 1]))
                step_of.beside(V.tensor_scalar(ties[:, h, :], keyT[:, h, :], limit, 0.0, ALU.is_equal, ALU.add,
                                               accum_out=tie_count[:, h:h + 1]))
            dve.wait_ge(chain, step_of.n)
            V.engine_nop().then_inc(ties_ready, 1)
            dve.wait_ge(consts, 6 + EXPERTS)
            scanned, carry = "p h n -> p (h n)", no_carry[:].rearrange("p h n -> p (h n)")
            step_of.beside(V.tensor_tensor_scan(rank[:].rearrange(scanned), carry, ties[:].rearrange(scanned), 0.0,
                                                ALU.mult, ALU.add))
            dve.wait_ge(ties_summed, 1)
            step_of(V.tensor_scalar(fits[:], ps_count[:, 0:HALVES], -1.0, float(CAP), ALU.mult, ALU.add))
            step_of(V.tensor_tensor(fits[:], fits[:], ps_earlier[:, 0:HALVES], ALU.subtract))
            for h in range(HALVES):
                step_of.beside(V.scalar_tensor_tensor(taken[:, h, :], rank[:, h, :], fits[:, h:h + 1], ties[:, h, :],
                                                      ALU.is_le, ALU.mult))
            dve.wait_ge(chain, step_of.n)
            step_of(V.tensor_tensor(taken[:], taken[:], above[:], ALU.add))
            step_of(V.tensor_reduce(count[:], taken[:], AX.X, ALU.add))
            V.engine_nop().then_inc(taken_ready, 1)
            step_of.beside(V.tensor_tensor_scan(rank[:].rearrange(scanned), carry, taken[:].rearrange(scanned), 0.0,
                                                ALU.mult, ALU.add))
            dve.wait_ge(taken_summed, 1)
            step_of(V.tensor_copy(fits[:], ps_earlier[:, 0:HALVES]))
            for h in range(HALVES):
                step_of(V.scalar_tensor_tensor(ties[:, h, :], rank[:, h, :], fits[:, h:h + 1], taken[:, h, :],
                                               ALU.add, ALU.mult))
            V.engine_nop().then_inc(slot_ready, 1)
            step_of(V.tensor_copy(gate_parts[:, 0], key[:]))
            step_of(V.tensor_tensor(gate_rest[:], key[:], gate_parts[:, 0], ALU.subtract))
            step_of(V.tensor_copy(gate_parts[:, 1], gate_rest[:]))
            step_of(V.tensor_tensor(gate_parts[:, 2], gate_rest[:], gate_parts[:, 1], ALU.subtract))
            dve.wait_ge(slot_turned, 1)
            step_of(V.tensor_scalar(slot[:].rearrange(flat), ps_slot[:, 0:E * T], -1.0, None, ALU.add))
            step_of(V.tensor_scalar(row[:], slot[:], float(P), None, ALU.is_ge))
            for k in range(2, CT):
                step_of(V.scalar_tensor_tensor(row[:].rearrange(flat), slot[:].rearrange(flat), float(k * P),
                                               row[:].rearrange(flat), ALU.is_ge, ALU.add))
            V.scalar_tensor_tensor(lane[:].rearrange(flat), row[:].rearrange(flat), -float(P), slot[:].rearrange(flat),
                                   ALU.mult, ALU.add).then_inc(chain, 1)

        @block.tensor
        def _(pe):
            def per_expert(matrix, counts, sums):
                return nc.tensor.matmul(sums[:, 0:HALVES], matrix[:], counts[:], start=True, stop=True)

            pe.wait_ge(key_ready, 1)
            for h in range(HALVES):
                nc.tensor.transpose(ps_key[h][:, 0:P], key[:, EXPERTS * h:EXPERTS * (h + 1), :].rearrange("p e t -> p (e t)"),
                                    ident[:]).then_inc(key_turned, 1)
            pe.wait_ge(consts, 4 + EXPERTS)
            with pe.Fori(0, BITS // UNROLLED) as i:
                for j in range(UNROLLED):
                    pe.wait_ge(search, i * (STEPS * UNROLLED) + (STEPS * j + 3))
                    per_expert(same, count, ps_count).then_inc(counted, 1)
            pe.wait_ge(search, BITS * STEPS)
            pe.wait_ge(ties_ready, 1)
            per_expert(same, count, ps_count)
            per_expert(earlier, tie_count, ps_earlier).then_inc(ties_summed, 1)
            pe.wait_ge(taken_ready, 1)
            per_expert(earlier, count, ps_earlier).then_inc(taken_summed, 1)
            pe.wait_ge(slot_ready, 1)
            for h in range(HALVES):
                mm = nc.tensor.transpose(ps_slot[:, P * h:P * (h + 1)], ties[:, h, :], ident[:])
            mm.then_inc(slot_turned, 1)


def experts(nc, io, x, ident, n_rows, sum_rows, weights_in, E, F, FC, T, N, CT, out, gamma, beta, b1, w1, w2,
            minus_half, key, gate_parts, row, lane, lanes, rows_of, numbers, spare):
    HALF = CAP // 2
    PAYLOADS = 6
    TOTALS = 4
    ctx = ExitStack()
    with ctx:
        def sb(name, shape, dt=F32):
            return ctx.enter_context(nc.sbuf_tensor("e_" + name, shape, dt))

        def ps(name, shape, dt=F32):
            return ctx.enter_context(nc.psum_tensor("e_ps_" + name, shape, dt))

        def sem(name):
            return ctx.enter_context(nc.semaphore("e_" + name))

        b2 = sb("b2", [P, 2, D])
        xe = [sb(f"xe{i}", [P, CT, D]) for i in range(2)]
        xT = [sb(f"xT{i}", [P, KC, CAP]) for i in range(2)]
        hT = sb("hT", [P, FC, CAP])
        y = [sb(f"y{i}", [P, CT, D]) for i in range(2)]
        biased_y = sb("biased_y", [P, 2, D])
        total = [sb(f"total{i}", [P, NT, D]) for i in range(TOTALS)]
        lane_hot = [sb(f"lane_hot{i}", [P, T, P], BF16) for i in range(2)]
        row_hot = [sb(f"row_hot{i}", [P, T, PAYLOADS, CT], BF16) for i in range(2)]
        filled = sb("filled", [P, PAYLOADS, CT])
        index = sb("index", [P, 3, CT])
        place, gate = sb("place", [P, E, CT], I32), sb("gate", [P, E, CT])
        stats, moments = sb("stats", [P, T, 6]), sb("moments", [P, T, 2])
        var_eps, rstd = sb("var_eps", [P, T]), sb("rstd", [P, T])
        ps_t = [ps(f"t{i}", [P, S]) for i in range(2)]
        ps_h = [ps(f"h{i}", [P, 2, S]) for i in range(2)]
        ps_y = [ps(f"y{i}", [P, S]) for i in range(2)]
        ps_slots = ps_t[1]

        added, total_in, stored = sem("added"), [sem(f"total_in{i}") for i in range(TOTALS)], [
            sem(f"stored{i}") for i in range(TOTALS)]
        lane_ready, row_ready, slots_ready, fill, place_ready = (sem("lane_ready"), sem("row_ready"), sem("slots_ready"),
                                                                 sem("fill"), sem("place_ready"))
        gathered = [sem(f"gathered{i}") for i in range(2)]
        turned, xT_ready, h_sum, hT_ready, y_sum, biased, y_ready = (
            sem("turned"), sem("xT_ready"), sem("h_sum"), sem("hT_ready"), sem("y_sum"), sem("biased"), sem("y_ready"))
        stats_ready, moments_ready, var_ready, rstd_ready, done, scaled_by = (
            sem("stats_ready"), sem("moments_ready"), sem("var_ready"), sem("rstd_ready"), sem("done"), sem("scaled_by"))

        block = ctx.enter_context(nc.Block())

        @block.sync
        def _(sp):
            for e in range(E):
                if e >= 2:
                    sp.wait_ge(y_ready, CT * (e - 1))
                    load_expert(sp, io, e, w1[e % 2], w2[e % 2], weights_in[e % 2])
                    sp.wait_ge(biased, CT * (e - 1))
                sp.dma_start(b2[:, e % 2, :], io["mb2"][e:e + 1, :].to_broadcast([P, D])).then_inc(weights_in[e % 2], 16)
            sp.wait_ge(added, 16 * CT * E)
            for b in range(B):
                if b >= TOTALS:
                    sp.wait_ge(stored[b % TOTALS], 16 * (b // TOTALS))
                sp.dma_start(total[b % TOTALS][:], sum_rows[b * S:(b + 1) * S, :].rearrange("(t p) d -> p t d", p=P)
                             ).then_inc(total_in[b % TOTALS], 16)

        @block.gpsimd
        def _(pool):
            def gather(e):
                if e >= 2:
                    pool.wait_ge(turned, 3 * (e - 1))
                for c in range(CT):
                    nc.gpsimd.indirect_dma_start(
                        out=xe[e % 2][:, c, :], out_offset=None, in_=n_rows,
                        in_offset=bass.IndirectOffsetOnAxis(ap=place[:, e, c:c + 1], axis=0)).then_inc(gathered[e % 2], 16)

            pool.wait_ge(place_ready, 1)
            gather(0)
            pool.wait_ge(place_ready, 2)
            gather(1)
            for e in range(E):
                for c in range(CT):
                    pool.wait_ge(y_ready, CT * e + c + 1)
                    if c == 0 and e > 0:
                        pool.wait_ge(added, 16 * CT * e)
                    nc.gpsimd.indirect_dma_start(
                        out=sum_rows, out_offset=bass.IndirectOffsetOnAxis(ap=place[:, e, c:c + 1], axis=0),
                        in_=y[e % 2][:, c, :], in_offset=None, compute_op=ALU.add).then_inc(added, 16)
                if e + 2 < E:
                    pool.wait_ge(place_ready, e + 3)
                    gather(e + 2)

            def add_x(b):
                pool.wait_ge(scaled_by, (NT + 1) * (b + 1))
                nc.gpsimd.tensor_tensor(total[b % TOTALS][:], total[b % TOTALS][:], x[:, b * NT:(b + 1) * NT, :], ALU.add
                                        ).then_inc(done, 1)

            for b in range(B):
                pool.wait_ge(var_ready, b + 1)
                nc.gpsimd.tensor_tensor(rstd[:, b * NT:(b + 1) * NT], var_eps[:, b * NT:(b + 1) * NT],
                                        minus_half[:, 0:NT], ALU.pow).then_inc(rstd_ready, 1)
                if b >= 1:
                    add_x(b - 1)
            add_x(B - 1)

        @block.scalar
        def _(act):
            def turned_in(e):
                for i in range(3):
                    act.wait_ge(turned, 3 * e + i + 1)
                    if i < KC:
                        nc.scalar.copy(xT[e % 2][:, i, 0:S], ps_t[i % 2][:]).then_inc(xT_ready, 1)
                    else:
                        nc.scalar.copy(xT[e % 2][:, :, S:], ps_t[i % 2][:, 0:KC * P].rearrange("p (c n) -> p c n", c=KC)
                                       ).then_inc(xT_ready, 1)

            turned_in(0)
            for e in range(E):
                for f in range(FC):
                    n = FC * e + f
                    act.wait_ge(h_sum, n + 1)
                    if f == 0 and e > 0:
                        act.wait_ge(y_sum, CT * e)
                    nc.scalar.activation(hT[:, f, :].rearrange("p (a n) -> p a n", a=2), ps_h[f % 2][:, :, 0:HALF], ACT.Gelu,
                                         bias=b1[:, e, f:f + 1]).then_inc(hT_ready, 1)
                if e + 1 < E:
                    turned_in(e + 1)
            for b in range(B):
                act.wait_ge(done, b + 1)
                act.dma_start(out[b].rearrange("(t p) d -> p t d", p=P), total[b % TOTALS][:]
                              ).then_inc(stored[b % TOTALS], 16)
            for i in range(TOTALS):
                act.wait_ge(stored[i], 16 * (B // TOTALS))

        @block.vector
        def _(dve):
            V = nc.vector

            def one_hot(e):
                if e >= 2:
                    dve.wait_ge(slots_ready, e - 1)
                lane_e, row_e = lane[:, e, :], row[:, e, :]
                V.tensor_tensor(lane_hot[e % 2][:], repeated(lanes[:], (0, T), (1, P)), repeated(lane_e, (1, T), (0, P)),
                                ALU.is_equal).then_inc(lane_ready, 1)
                hot = row_hot[e % 2]
                V.tensor_tensor(hot[:, :, 0, :], repeated(rows_of[:], (0, T), (1, CT)), repeated(row_e, (1, T), (0, CT)),
                                ALU.is_equal).then_inc(row_ready, 1)
                dve.wait_ge(row_ready, PAYLOADS * e + 1)
                for j in range(1, PAYLOADS):
                    load = numbers[:, j - 1, :] if j < 3 else gate_parts[:, j - 3, e, :]
                    V.tensor_tensor(hot[:, :, j, :], hot[:, :, 0, :], repeated(load, (1, T), (0, CT)), ALU.mult
                                    ).then_inc(row_ready, 1)

            def read_slots(e):
                done = [6 * e]

                def step(ins):
                    done[0] += 1
                    ins.then_inc(fill, 1)
                    dve.wait_ge(fill, done[0])

                dve.wait_ge(slots_ready, e + 1)
                step(V.tensor_copy(filled[:], ps_slots[:, 0:PAYLOADS * CT].rearrange("p (j c) -> p j c", j=PAYLOADS)))
                step(V.tensor_tensor(index[:, 2, :], filled[:, 3, :], filled[:, 4, :], ALU.add))
                step(V.tensor_tensor(gate[:, e, :], index[:, 2, :], filled[:, 5, :], ALU.add))
                step(V.scalar_tensor_tensor(index[:, 0, :], filled[:, 1, :], float(P), filled[:, 2, :], ALU.mult, ALU.add))
                step(V.tensor_tensor(index[:, 1, :], filled[:, 0, :], spare[:], ALU.mult))
                step(V.tensor_tensor(index[:, 1, :], spare[:], index[:, 1, :], ALU.subtract))
                V.tensor_tensor(place[:, e, :], index[:, 0, :], index[:, 1, :], ALU.add).then_inc(place_ready, 1)

            one_hot(0)
            one_hot(1)
            read_slots(0)
            read_slots(1)
            for e in range(E):
                if e + 2 < E:
                    one_hot(e + 2)
                    read_slots(e + 2)
                for c in range(CT):
                    n = CT * e + c
                    dve.wait_ge(y_sum, n + 1)
                    if c == 0:
                        dve.wait_ge(weights_in[e % 2], 48 * (e // 2 + 1))
                        if e >= 2:
                            dve.wait_ge(added, 16 * CT * (e - 1))
                    if n >= 2:
                        dve.wait_ge(y_ready, n - 1)
                    V.tensor_tensor(biased_y[:, n % 2, :], ps_y[n % 2][:, 0:D], b2[:, e % 2, :], ALU.add).then_inc(biased, 1)
                    dve.wait_ge(biased, n + 1)
                    V.tensor_scalar(y[e % 2][:, c, :], biased_y[:, n % 2, :], gate[:, e, c:c + 1], None, ALU.mult
                                    ).then_inc(y_ready, 1)

            def statistics(b):
                tot = total[b % TOTALS]
                of_b = slice(b * NT, (b + 1) * NT)
                dve.wait_ge(total_in[b % TOTALS], 16 * (b // TOTALS + 1))
                for t in range(NT):
                    V.bn_stats(stats[:, b * NT + t, :], tot[:, t, :]).then_inc(stats_ready, 1)
                dve.wait_ge(stats_ready, NT * (b + 1))
                for t in range(NT):
                    V.bn_aggr(moments[:, b * NT + t, :], stats[:, b * NT + t, :]).then_inc(moments_ready, 1)
                dve.wait_ge(moments_ready, NT * (b + 1))
                V.tensor_scalar(var_eps[:, of_b], moments[:, of_b, 1], EPS, None, ALU.add).then_inc(var_ready, 1)

            def normalise(b):
                tot = total[b % TOTALS]
                dve.wait_ge(rstd_ready, b + 1)
                for t in range(NT):
                    V.tensor_scalar(tot[:, t, :], tot[:, t, :], moments[:, b * NT + t, 0:1],
                                    rstd[:, b * NT + t:b * NT + t + 1], ALU.subtract, ALU.mult).then_inc(scaled_by, 1)
                dve.wait_ge(scaled_by, (NT + 1) * b + NT)
                V.tensor_tensor(tot[:], tot[:], repeated(gamma[:], (0, NT), (1, D)), ALU.mult).then_inc(scaled_by, 1)

            for b in range(B):
                statistics(b)
                if b >= 1:
                    normalise(b - 1)
            normalise(B - 1)

        @block.tensor
        def _(pe):
            def transposes(e):
                pe.wait_ge(gathered[e % 2], 16 * CT * (e // 2 + 1))
                for i in range(3):
                    if i == 1:
                        pe.wait_ge(fill, 6 * min(e + 1, E - 1) + 1)
                    elif i == 2 or e > 0:
                        pe.wait_ge(xT_ready, 3 * e + (1 if i == 2 else 0))
                    if i < KC:
                        for c in range(NT):
                            mm = nc.tensor.transpose(ps_t[i % 2][:, c * P:(c + 1) * P], xe[e % 2][:, c, i * P:(i + 1) * P], ident[:])
                    else:
                        for k in range(KC):
                            mm = nc.tensor.transpose(ps_t[i % 2][:, k * P:(k + 1) * P], xe[e % 2][:, NT, k * P:(k + 1) * P], ident[:])
                    mm.then_inc(turned, 1)

            def slots(e):
                pe.wait_ge(lane_ready, e + 1)
                pe.wait_ge(row_ready, PAYLOADS * (e + 1))
                if e == 1:
                    pe.wait_ge(fill, 1)
                if e >= 2:
                    pe.wait_ge(xT_ready, 3 * (e - 2) + 2)
                for t in range(T):
                    mm = nc.tensor.matmul(ps_slots[:, 0:PAYLOADS * CT], lane_hot[e % 2][:, t, :],
                                          row_hot[e % 2][:, t].rearrange("p j c -> p (j c)"), start=(t == 0), stop=(t == T - 1))
                mm.then_inc(slots_ready, 1)

            slots(0)
            slots(1)
            transposes(0)
            for e in range(E):
                pe.wait_ge(xT_ready, 3 * (e + 1))
                pe.wait_ge(weights_in[e % 2], 48 * (e // 2 + 1))
                for f in range(FC):
                    n = FC * e + f
                    if n >= 2:
                        pe.wait_ge(hT_ready, n - 1)
                    for half in range(2):
                        for c in range(KC):
                            mm = nc.tensor.matmul(ps_h[f % 2][:, half, 0:HALF], w1[e % 2][:, c, f * P:(f + 1) * P],
                                                  xT[e % 2][:, c, half * HALF:(half + 1) * HALF], start=(c == 0), stop=(c == KC - 1))
                    mm.then_inc(h_sum, 1)
                if e + 2 < E:
                    slots(e + 2)
                if e + 1 < E:
                    transposes(e + 1)
                pe.wait_ge(hT_ready, FC * (e + 1))
                for c in range(CT):
                    n = CT * e + c
                    if n >= 2:
                        pe.wait_ge(biased, n - 1)
                    for f in range(FC):
                        mm = nc.tensor.matmul(ps_y[n % 2][:, 0:D], hT[:, f, c * P:(c + 1) * P], w2[e % 2][:, f, :],
                                              start=(f == 0), stop=(f == FC - 1))
                    mm.then_inc(y_sum, 1)


def program(nc, io, out):
    ctx = ExitStack()
    with ctx:
        x = ctx.enter_context(nc.sbuf_tensor("x_sb", [P, B * NT, D], F32))
        ident = ctx.enter_context(nc.sbuf_tensor("ident", [P, P], F32))
        identb = ctx.enter_context(nc.sbuf_tensor("identb", [P, P], BF16))
        logits = ctx.enter_context(nc.sbuf_tensor("logits", [P, NE, B * NT], F32))
        n_rows = nc.dram_tensor("n_rows", [B * S + SPARE, D], F32, kind="Internal").ap()
        sum_rows = nc.dram_tensor("sum_rows", [B * S + SPARE, D], F32, kind="Internal").ap()
        ident_set = ctx.enter_context(nc.semaphore("ident_set"))
        with nc.Block() as block:
            @block.gpsimd
            def _(pool):
                nc.gpsimd.memset(ident[:], 0.0).then_inc(ident_set, 1)
                pool.wait_ge(ident_set, 1)
                nc.gpsimd.affine_select(out=ident[:], in_=ident[:], compare_op=ALU.not_equal, fill=1.0, base=0,
                                        pattern=[[-1, P]], channel_multiplier=1).then_inc(ident_set, 1)
                pool.wait_ge(ident_set, 2)
                nc.gpsimd.tensor_copy(identb[:], ident[:]).then_inc(ident_set, 1)
        softmax_attention(nc, io, x, ident, identb)
        expert_per_batch(nc, io, x, ident)
        sigmoid_attention(nc, io, x, ident, logits, n_rows, sum_rows)
        mixture(nc, io, x, ident, logits, n_rows, sum_rows, out)


def laid_out(inputs):
    a = {k: np.asarray(v) for k, v in inputs.items()}
    order = np.arange(D).reshape(KC, HC, HD).transpose(0, 2, 1).reshape(D)
    cols = lambda v: v.reshape(KC, P).T
    m = {
        "x": a["x"],
        "ctxT": a["ctx_1024"].transpose(0, 2, 1),
        "mask": a["mask_BxS2_bf1"].view(np.uint8),
        "wq": a["L0_xattn_Wq"][order].T, "wk": a["L0_xattn_Wk"][order].T,
        "wv": a["L0_xattn_Wv"].T, "wo": a["L0_xattn_Wo"].T,
        "bq": cols(a["L0_xattn_bq"][order]), "bk": cols(a["L0_xattn_bk"][order]), "bv": cols(a["L0_xattn_bv"]),
        "bo": a["L0_xattn_bo"].reshape(1, D),
        "pw1": a["L0_ffn_Wp1"], "pb1": a["L0_ffn_bp1"].reshape(P, 1), "pw2": a["L0_ffn_Wp2"],
        "pb2": a["L0_ffn_bp2"].reshape(1, -1),
        "fw1": a["L0_ffn_W1"], "fb1": a["L0_ffn_b1"].reshape(8, 4, P).transpose(0, 2, 1),
        "fw2": a["L0_ffn_W2"], "fb2": a["L0_ffn_b2"].reshape(8, KC, P).transpose(0, 2, 1),
        "fwo": a["L0_ffn_Wo"], "fbo": a["L0_ffn_bo"].reshape(1, D),
        "swq": a["L1_xattn_Wq"][order].T, "swk": a["L1_xattn_Wk"][order].T, "swv": a["L1_xattn_Wv"].T,
        "swp": a["L1_xattn_Wp"].T,
        "sgq": a["L1_xattn_gq"].repeat(HC).reshape(P, 1), "sbq": a["L1_xattn_bq"].repeat(HC).reshape(P, 1),
        "sgk": a["L1_xattn_gk"].repeat(HC).reshape(P, 1), "sbk": a["L1_xattn_bk"].repeat(HC).reshape(P, 1),
        "sbp": a["L1_xattn_bp"].reshape(1, D),
        "mwr": a["L1_ffn_Wr"], "mbr": a["L1_ffn_br"].reshape(1, -1),
        "mw1": a["L1_ffn_W1"], "mb1": a["L1_ffn_b1"].reshape(8, 8, P).transpose(0, 2, 1),
        "mw2": a["L1_ffn_W2"], "mb2": a["L1_ffn_b2"],
        "mgamma": a["L1_ffn_gamma"].reshape(1, D), "mbeta": a["L1_ffn_beta"].reshape(1, D),
    }
    return {k: np.ascontiguousarray(v) for k, v in m.items()}


def kernel(**inputs):
    import concourse.bacc as bacc
    from concourse.bass_utils import run_bass_kernel_spmd

    arrays = laid_out(inputs)
    nc = bacc.Bacc("TRN2", target_bir_lowering=False, num_devices=1)
    io = {k: nc.dram_tensor(k, v.shape, mybir.dt.from_np(v.dtype), kind="ExternalInput").ap() for k, v in arrays.items()}
    out = nc.dram_tensor("out", (B, S, D), F32, kind="ExternalOutput").ap()
    program(nc, io, out)
    r = run_bass_kernel_spmd(nc, [arrays], core_ids=[0])
    return r.results[0]["out"]
```

```python
from contextlib import ExitStack

import numpy as np

import concourse.bass as bass
from concourse import mybir

F32 = mybir.dt.float32
BF16 = mybir.dt.bfloat16
I32 = mybir.dt.int32
U8 = mybir.dt.uint8
ALU = mybir.AluOpType
ACT = mybir.ActivationFunctionType
AX = mybir.AxisListType

P = 128
B, S, D = 8, 512, 256
NT = S // P
KC = D // P
H, HD = 16, 16
HC = H // KC
HG = 4
NG = H // HG
NE = 8
EPS = 1e-5
PAIRS = 6
K_MASK = PAIRS * HD
K_MAX = K_MASK + 1
K_ALL = K_MASK + 4
Q_PARTS = (0, 0, 0, 1, 1, 2)
K_PARTS = (0, 1, 2, 0, 1, 0)
SCALE = 1.0 / np.sqrt(HD)
MASK_Q, MASK_K = 250.0, -160.0
assert MASK_Q * MASK_K * SCALE == -10000.0

CAP = -(-(B * S // NE * 5) // 4)
SPARE = CAP


def softmax_attention(nc, io, x, ident, identb):
    QUADS = NG * NT
    MX_LEAD = 7
    MX_RING = 3
    PV_LAG = 2
    ctx = ExitStack()
    with ctx:
        def sb(name, shape, dt=F32):
            return ctx.enter_context(nc.sbuf_tensor("a_" + name, shape, dt))

        def ps(name, shape, dt=F32):
            return ctx.enter_context(nc.psum_tensor("a_" + name, shape, dt))

        spent = []

        def sem(name):
            spent.append(ctx.enter_context(nc.semaphore("a_" + name)))
            return spent[-1]

        wq, wk, wv, wo = (sb(n, [P, KC, D]) for n in ("wq", "wk", "wv", "wo"))
        bq, bk, bv = (sb(n, [P, KC]) for n in ("bq", "bk", "bv"))
        bo = sb("bo", [P, D])
        head_rows = sb("head_rows", [H, KC, P])
        ctxT = sb("ctxT", [P, KC, S])
        mask8 = sb("mask8", [P, S], U8)
        maskf = sb("maskf", [P, S])
        mask_row = sb("mask_row", [P, S], BF16)
        q_row, k_rows = sb("q_row", [1, S], BF16), sb("k_rows", [3, S], BF16)
        stats = sb("stats", [P, NT, 6])
        moments = sb("moments", [P, NT, 2])
        var_eps = sb("var_eps", [P, NT])
        rstd = sb("rstd", [P, NT])
        minus_half = sb("minus_half", [P, NT])
        xn = sb("xn", [P, NT, D])
        xT = sb("xT", [P, KC, S])
        proj = sb("proj", [P, 2, S])
        rest = sb("rest", [P, 2, S])
        parts = sb("parts", [P, 2, 3, S], BF16)
        q_stack = [sb(f"q_stack{i}", [P, H, S], BF16) for i in range(2)]
        k_stack = [sb(f"k_stack{i}", [P, H, S], BF16) for i in range(2)]
        v_ones = [sb(f"v_ones{i}", [P, NT, H, 2 * HD]) for i in range(2)]
        probs = sb("probs", [P, NT, HG, S])
        neg_max = sb("neg_max", [P, 2, NT, HG])
        neg_rest = sb("neg_rest", [P, NT, HG])
        neg_parts = sb("neg_parts", [P, NT, 3, HG], BF16)
        neg_rows = sb("neg_rows", [3 * HG, S], BF16)
        sums = sb("sums", [P, 2, S])
        values = sb("values", [P, 2, KC, S])
        den = sb("den", [P, 64])
        rden = sb("rden", [P, 64])
        rden_h = sb("rden_h", [H, S])
        oT = sb("oT", [P, KC, S])

        ps_score = [ps(f"score{i}", [P, S]) for i in range(2)]
        ps_max = [ps(f"max{i}", [P, S]) for i in range(MX_RING)]
        ps_pv = ps("pv", [P, S])
        ps_a = ps("act", [P, S])
        ps_d = ps("dve", [P, S])

        x_first_in, x_second_in, x_rest_in = sem("x_first_in"), sem("x_second_in"), sem("x_rest_in")
        wk_in, w_in, ctx_in, mask_in = sem("wk_in"), sem("w_in"), sem("ctx_in"), sem("mask_in")
        consts, v_consts, rows_set = sem("consts"), sem("v_consts"), sem("rows_set")
        stats_ready, moments_ready, var_ready = sem("stats_ready"), sem("moments_ready"), sem("var_ready")
        rstd_ready, xn_ready = sem("rstd_ready"), sem("xn_ready")
        a_ready, a_empty = sem("a_ready"), sem("a_empty")
        d_ready, d_empty = sem("d_ready"), sem("d_empty")
        maskf_ready, mask_row_ready, mask_landed = sem("maskf_ready"), sem("mask_row_ready"), sem("mask_landed")
        masked, part0, rest_ready, part1, part2 = (
            sem("masked"), sem("part0"), sem("rest_ready"), sem("part1"), sem("part2"))
        stacked = [sem(f"stacked{i}") for i in range(2)]
        score_ready, probs_ready, pv_ready, sums_ready = (
            sem("score_ready"), sem("probs_ready"), sem("pv_ready"), sem("sums_ready"))
        max_ready, max_read, neg_chain, neg_ready, neg_landed = (
            sem("max_ready"), sem("max_read"), sem("neg_chain"), sem("neg_ready"), sem("neg_landed"))
        values_landed = [sem(f"values_landed{i}") for i in range(2)]
        den_landed = [sem(f"den_landed{i}") for i in range(2)]
        rden_ready, rden_landed = sem("rden_ready"), sem("rden_landed")
        weighted, ot_ready, residual = sem("weighted"), sem("ot_ready"), sem("residual")

        def batches(eng, batch):
            batch(0, 0, True, False)
            with eng.Fori(0, (B - 2) // 2) as i:
                batch(i * 2 + 1, 1, False, False)
                batch(i * 2 + 2, 0, False, False)
            batch(B - 1, (B - 1) % 2, False, True)

        KEYS0, KEYS1, XT0, XT1, QUERIES0, QUERIES1, V0, V1 = range(8)
        A_ITEMS = 8
        PROJ = ((KEYS0, False, 0), (KEYS1, False, 1), (QUERIES0, True, 0), (QUERIES1, True, 1))

        D_FIRST = ("neg1", "neg2", "neg3", "neg4")
        D_LATER = ("neg1", "neg2", "rden0", "rden1", "neg3", "out0", "out1", "neg4")
        D_END = 1 + len(D_FIRST) + len(D_LATER) * (B - 1) - 1

        def d_item(b, first, name):
            if first:
                return 1 + D_FIRST.index(name)
            return (b - 1) * len(D_LATER) + (1 + len(D_FIRST) + D_LATER.index(name))

        first_banks = (ps_a, *ps_score)

        def bank_of(bb, item):
            return first_banks[item % len(first_banks)] if isinstance(bb, int) and bb == 0 else ps_a

        block = ctx.enter_context(nc.Block())

        @block.sync
        def _(sp):
            def loads(bb):
                sp.dma_start(ctxT[:], io["ctxT"][bass.ds(bb, 1)].rearrange("a (c p) n -> p (a c) n", p=P)
                             ).then_inc(ctx_in, 16)
                sp.dma_start(mask8[:], io["mask"][bass.ds(bb, 1), :].to_broadcast([P, S])).then_inc(mask_in, 16)

            def mask_to_stack(bb, par, unused=True):
                if not unused:
                    sp.wait_ge(score_ready, (bb - 1) * 64)
                sp.wait_ge(mask_row_ready, bb * 2 + 2)
                row = mask_row[96:97, :]
                sp.dma_start(k_stack[par][K_MASK:K_MASK + 1, :, :],
                             bass.AP(row.tensor, row.offset, [[S, 1], [0, H], [1, S]])).then_inc(mask_landed, 16)

            def stack(bb, par, k):
                _, is_q, c = PROJ[k]
                dst = (q_stack if is_q else k_stack)[par]
                for part, ready in enumerate((part0, part1, part2)):
                    sp.wait_ge(ready, bb * 4 + (k + 1))
                    for j in range(PAIRS):
                        if (Q_PARTS if is_q else K_PARTS)[j] == part:
                            sp.dma_start(dst[HD * j:HD * (j + 1), HC * c:HC * (c + 1), :],
                                         parts[:, k % 2, part, :]).then_inc(stacked[k % 2], 16)

            def sums_out(b, par, g, first):
                if g == 0 and not first:
                    sp.wait_ge(ot_ready, (b - 1) * KC)
                    sp.wait_ge(rden_ready, b)
                sp.wait_ge(sums_ready, b * 4 + (g + 1))
                for hh in range(HG):
                    h = HG * g + hh
                    sp.dma_start(den[8 * h:8 * h + 8, :],
                                 sums[32 * hh + HD:32 * hh + HD + 1, g % 2, :]).then_inc(den_landed[g % 2], 16)
                for hh in range(HG):
                    h = HG * g + hh
                    sp.dma_start(values[HD * (h % HC):HD * (h % HC + 1), par, h // HC, :],
                                 sums[32 * hh:32 * hh + HD, g % 2, :]).then_inc(values_landed[g % 2], 16)

            def rden_out(b, d_prev):
                sp.wait_ge(d_ready, d_prev)
                sp.wait_ge(rden_ready, b + 1)
                sp.dma_start(rden_h[:, :], rden[:, :]).then_inc(rden_landed, 16)

            sp.dma_start(wk[:], io["wk"].rearrange("(c p) n -> p c n", p=P)).then_inc(wk_in, 16)
            loads(0)
            sp.dma_start(bk[:], io["bk"]).then_inc(wk_in, 16)
            for dst, name in ((bq, "bq"), (bv, "bv")):
                sp.dma_start(dst[:], io[name]).then_inc(w_in, 16)
            for dst, name in ((wq, "wq"), (wv, "wv"), (wo, "wo")):
                sp.dma_start(dst[:], io[name].rearrange("(c p) n -> p c n", p=P)).then_inc(w_in, 16)
            sp.dma_start(bo[:], io["bo"].to_broadcast([P, D])).then_inc(w_in, 16)
            sp.dma_start(x[:, NT:2 * NT, :], io["x"][1].rearrange("(t p) d -> p t d", p=P)).then_inc(x_second_in, 16)
            sp.wait_ge(consts, 3)
            for i in range(2):
                for rows, source, n in ((q_stack[i][K_MASK:K_MASK + 1], q_row[:], 1), (k_stack[i][K_MAX:K_ALL], k_rows[:], 3)):
                    sp.dma_start(rows, bass.AP(source.tensor, source.offset, [[S, n], [0, H], [1, S]])).then_inc(rows_set, 16)
            mask_to_stack(0, 0)
            for k in range(4):
                stack(0, 0, k)
            sp.dma_start(x[:, 2 * NT:, :], io["x"][2:].rearrange("b (t p) d -> p (b t) d", p=P)).then_inc(x_rest_in, 16)

            def batch(b, par, first, last):
                if not last:
                    sp.wait_ge(maskf_ready, b + 1)
                    sp.wait_ge(a_ready, b * A_ITEMS + A_ITEMS)
                    loads(b + 1)
                    if not first:
                        sums_out(b - 1, 1 - par, 2, False)
                    mask_to_stack(b + 1, 1 - par, first)
                if not first:
                    if last:
                        sums_out(b - 1, 1 - par, 2, False)
                    sums_out(b - 1, 1 - par, 3, False)
                if not last:
                    stack(b + 1, 1 - par, 0)
                if not first:
                    rden_out(b - 1, (b - 1) * len(D_LATER) + (1 + len(D_FIRST) + D_LATER.index("rden1") + 1 - len(D_LATER)))
                if not last:
                    stack(b + 1, 1 - par, 1)
                if not last:
                    stack(b + 1, 1 - par, 2)
                    stack(b + 1, 1 - par, 3)
                sums_out(b, par, 0, first)
                sums_out(b, par, 1, first)

            batches(sp, batch)
            sums_out(B - 1, (B - 1) % 2, 2, False)
            sums_out(B - 1, (B - 1) % 2, 3, False)
            rden_out(B - 1, d_item(B - 1, False, "rden1") + 1)

        @block.scalar
        def _(act):
            def evacuate(bb, item, out, **kw):
                act.wait_ge(a_ready, bb * A_ITEMS + (item + 1))
                bank = bank_of(bb, item)
                nc.scalar.activation(out, bank[:] if len(out.shape) == 2 else
                                     bank[:].rearrange("p (t h d) -> p t h d", t=2, h=H), ACT.Identity,
                                     **kw).then_inc(a_empty, 1)

            def project(bb, k):
                item, is_q, c = PROJ[k]
                if k >= 2:
                    act.wait_ge(rest_ready, bb * 4 + (k - 1))
                elif not (isinstance(bb, int) and bb == 0):
                    act.wait_ge(rest_ready, (bb - 1) * 4 + (k + 3))
                evacuate(bb, item, proj[:, k % 2, :], bias=(bq if is_q else bk)[:, c:c + 1])

            def transposed(bb, c):
                evacuate(bb, XT0 + c, xT[:, c, :])

            def v_tiles(bb, par, t):
                evacuate(bb, V0 + t, v_ones[par][:, 2 * t:2 * t + 2, :, 0:HD])

            def neg_in(b, par, g, d):
                act.wait_ge(d_empty, d + 1)
                act.dma_start(q_stack[par][K_MAX:K_ALL, HG * g:HG * (g + 1), :], neg_rows[:]).then_inc(neg_landed, 16)

            def sums_of(b, g):
                G = b * 4 + g
                act.wait_ge(pv_ready, G * NT + NT)
                if not (isinstance(b, int) and b * 4 + g < 2):
                    act.wait_ge(values_landed[g % 2], b * 128 + (g // 2) * 64)
                    act.wait_ge(den_landed[g % 2], b * 128 + (g // 2) * 64)
                nc.scalar.copy(sums[:, g % 2, :], ps_pv[:]).then_inc(sums_ready, 1)

            act.dma_start(x[:, 0:NT, :], io["x"][0].rearrange("(t p) d -> p t d", p=P)).then_inc(x_first_in, 16)
            act.wait_ge(wk_in, 32)
            project(0, 0), project(0, 1)
            transposed(0, 0), transposed(0, 1)
            act.wait_ge(w_in, 16 * 6)
            project(0, 2), project(0, 3)
            v_tiles(0, 0, 0), v_tiles(0, 0, 1)
            neg_in(0, 0, 0, 0)

            def batch(b, par, first, last):
                for u in range(QUADS):
                    g, kc = divmod(u, NT)
                    quad = b * QUADS + u
                    for hh in range(HG):
                        act.wait_ge(score_ready, quad * HG + (hh + 1))
                        if hh == 0 and not (first and u < NT):
                            act.wait_ge(pv_ready, quad + (1 - NT))
                        nc.scalar.activation(probs[:, kc, hh, :], ps_score[hh % 2][:], ACT.Exp, scale=SCALE
                                             ).then_inc(probs_ready, 1)
                    if u == 1 and not first:
                        sums_of(b - 1, 3)
                    if u % NT == 1 and u > 1:
                        sums_of(b, g - 1)
                    if not last:
                        {0: lambda: project(b + 1, 0),
                         1: lambda: project(b + 1, 1),
                         2: lambda: (transposed(b + 1, 0), transposed(b + 1, 1)),
                         3: lambda: project(b + 1, 2),
                         4: lambda: project(b + 1, 3),
                         11: lambda: v_tiles(b + 1, 1 - par, 0),
                         12: lambda: v_tiles(b + 1, 1 - par, 1)}.get(u, lambda: None)()
                    if u % NT == 2 and u < 12:
                        neg_in(b, par, g + 1, d_item(b, first, f"neg{g + 1}"))
                    if u == 14 and not last:
                        neg_in(b + 1, 1 - par, 0, d_item(b, first, "neg4"))

            batches(act, batch)
            sums_of(B - 1, 3)

        @block.gpsimd
        def _(pool):
            nc.gpsimd.memset(minus_half[:], -0.5).then_inc(consts, 1)
            nc.gpsimd.memset(q_row[:], MASK_Q).then_inc(consts, 1)
            nc.gpsimd.memset(k_rows[:], 1.0).then_inc(consts, 1)
            pool.wait_ge(consts, 3)
            nc.gpsimd.memset(head_rows[:], 1.0).then_inc(consts, 1)
            pool.wait_ge(consts, 4)
            nc.gpsimd.affine_select(out=head_rows[:], in_=head_rows[:], compare_op=ALU.is_ge, fill=0.0, base=0,
                                    pattern=[[P, KC], [1, P]], channel_multiplier=-HD).then_inc(consts, 1)
            pool.wait_ge(consts, 5)
            nc.gpsimd.affine_select(out=head_rows[:], in_=head_rows[:], compare_op=ALU.is_ge, fill=0.0, base=HD - 1,
                                    pattern=[[-P, KC], [-1, P]], channel_multiplier=HD).then_inc(consts, 1)

            def invert_deviation(bb):
                pool.wait_ge(var_ready, bb + 1)
                nc.gpsimd.tensor_tensor(rstd[:], var_eps[:], minus_half[:], ALU.pow).then_inc(rstd_ready, 1)

            def split(bb, k, step):
                n = bb * 4 + k
                item, is_q, _ = PROJ[k]
                if step == 0:
                    pool.wait_ge(a_empty, bb * A_ITEMS + (item + 1))
                    pool.wait_ge(maskf_ready, bb + 1)
                    nc.gpsimd.tensor_tensor(proj[:, k % 2, :], proj[:, k % 2, :], maskf[:], ALU.mult).then_inc(masked, 1)
                elif step == 1:
                    pool.wait_ge(part0, n + 1)
                    if not (isinstance(n, int) and n < 2):
                        pool.wait_ge(part2, n - 1)
                    nc.gpsimd.tensor_tensor(rest[:, k % 2, :], proj[:, k % 2, :], parts[:, k % 2, 0, :],
                                            ALU.subtract).then_inc(rest_ready, 1)
                else:
                    pool.wait_ge(part1, n + 1)
                    nc.gpsimd.tensor_tensor(parts[:, k % 2, 2, :], rest[:, k % 2, :], parts[:, k % 2, 1, :],
                                            ALU.subtract).then_inc(part2, 1)

            def add_output_bias(b, first):
                for t in range(NT):
                    tile = x[:, bass.ds(b * NT + t, 1), :].rearrange("p a n -> p (a n)")
                    if t == 0:
                        pool.wait_ge(xn_ready, b * NT + NT)
                        pool.wait_ge(w_in, 16 * 6)
                    nc.gpsimd.tensor_tensor(tile, tile, bo[:], ALU.add).then_inc(residual, 1)

            def prepare(bb):
                invert_deviation(bb)
                split(bb, 0, 0)
                split(bb, 0, 1)
                split(bb, 1, 0)
                split(bb, 0, 2)
                split(bb, 1, 1)
                split(bb, 1, 2)
                split(bb, 2, 1)
                split(bb, 2, 2)
                split(bb, 3, 1)
                split(bb, 3, 2)

            pool.wait_ge(consts, 6)
            prepare(0)

            def batch(b, par, first, last):
                if not last:
                    prepare(b + 1)
                add_output_bias(b, first)

            batches(pool, batch)

        @block.vector
        def _(dve):
            def normalise(bb):
                dve.wait_ge({0: x_first_in, 1: x_second_in}.get(bb, x_rest_in) if isinstance(bb, int) else x_rest_in, 16)
                for t in range(NT):
                    nc.vector.bn_stats(stats[:, t, :], x[:, bass.ds(bb * NT + t, 1), :].rearrange("p a n -> p (a n)")
                                       ).then_inc(stats_ready, 1)
                dve.wait_ge(stats_ready, bb * NT + NT)
                nc.vector.memset(var_eps[:], EPS).then_inc(moments_ready, 1)
                for t in range(NT):
                    nc.vector.bn_aggr(moments[:, t, :], stats[:, t, :]).then_inc(moments_ready, 1)
                dve.wait_ge(moments_ready, bb * (NT + 1) + (NT + 1))
                nc.vector.tensor_tensor(var_eps[:], moments[:, :, 1], var_eps[:], ALU.add).then_inc(var_ready, 1)

            def centre(bb):
                dve.wait_ge(rstd_ready, bb + 1)
                if not (isinstance(bb, int) and bb == 0):
                    dve.wait_ge(a_ready, (bb - 1) * A_ITEMS + (XT1 + 1))
                for t in range(NT):
                    nc.vector.tensor_scalar(xn[:, t, :], x[:, bass.ds(bb * NT + t, 1), :].rearrange("p a n -> p (a n)"),
                                            moments[:, t, 0:1], rstd[:, t:t + 1], ALU.subtract, ALU.mult
                                            ).then_inc(xn_ready, 1)

            def read_mask(bb):
                dve.wait_ge(mask_in, (bb + 1) * 16)
                if not (isinstance(bb, int) and bb == 0):
                    dve.wait_ge(masked, bb * 2)
                    dve.wait_ge(mask_landed, bb * 16)
                nc.vector.tensor_copy(maskf[:], mask8[:]).then_inc(maskf_ready, 1)
                dve.wait_ge(maskf_ready, bb + 1)
                nc.vector.tensor_scalar(mask_row[96:97, :], maskf[96:97, :], -MASK_K, MASK_K, ALU.mult, ALU.add
                                        ).then_inc(mask_row_ready, 2)

            def part(bb, k, step):
                n = bb * 4 + k
                item, is_q, _ = PROJ[k]
                if step == 0:
                    dve.wait_ge(a_empty, bb * A_ITEMS + (item + 1))
                    if not is_q:
                        dve.wait_ge(masked, bb * 2 + (k + 1))
                    if not (isinstance(n, int) and n < 2):
                        dve.wait_ge(stacked[k % 2], bb * (2 * 96) + 96 * (k // 2))
                    nc.vector.tensor_copy(parts[:, k % 2, 0, :], proj[:, k % 2, :]).then_inc(part0, 1)
                else:
                    dve.wait_ge(rest_ready, n + 1)
                    nc.vector.tensor_copy(parts[:, k % 2, 1, :], rest[:, k % 2, :]).then_inc(part1, 1)

            def maxima(b, v):
                for s in range(NT):
                    n = b * 64 + (4 * v + s)
                    dve.wait_ge(max_ready, n + 1)
                    nc.vector.tensor_reduce(neg_max[:, (v // HG) % 2, s, v % HG:v % HG + 1], ps_max[(4 * v + s) % MX_RING][:], AX.X,
                                            ALU.max, negate=True).then_inc(max_read, 1)

            def split_maxima(b, g):
                G = b * 4 + g
                dve.wait_ge(max_read, G * 16 + 16)
                nm = neg_max[:, g % 2, :, :]
                nc.vector.tensor_copy(neg_parts[:, :, 0, :], nm).then_inc(neg_chain, 1)
                dve.wait_ge(neg_chain, G * 3 + 1)
                nc.vector.tensor_tensor(neg_rest[:], nm, neg_parts[:, :, 0, :], ALU.subtract).then_inc(neg_chain, 1)
                dve.wait_ge(neg_chain, G * 3 + 2)
                nc.vector.tensor_copy(neg_parts[:, :, 1, :], neg_rest[:]).then_inc(neg_chain, 1)
                dve.wait_ge(neg_chain, G * 3 + 3)
                nc.vector.tensor_tensor(neg_parts[:, :, 2, :], neg_rest[:], neg_parts[:, :, 1, :], ALU.subtract
                                        ).then_inc(neg_ready, 1)

            def rows_of_maxima(b, g, d):
                dve.wait_ge(d_ready, d + 1)
                if not (isinstance(b, int) and b * 4 + g == 0):
                    dve.wait_ge(neg_landed, (b * 4 + g) * 16)
                nc.vector.tensor_copy(neg_rows[:], ps_d[:].bitcast(BF16)[0:3 * HG, 0:S]).then_inc(d_empty, 1)

            def invert_denominators(b):
                for i in range(2):
                    dve.wait_ge(den_landed[i], b * 128 + 128)
                if not (isinstance(b, int) and b == 0):
                    dve.wait_ge(rden_landed, b * 16)
                nc.vector.reciprocal(rden[:], den[:]).then_inc(rden_ready, 1)

            def weigh(b, par, c, d):
                dve.wait_ge(d_ready, d + 1)
                if c == 0:
                    for i in range(2):
                        dve.wait_ge(values_landed[i], b * 128 + 128)
                nc.vector.tensor_tensor(oT[:, c, :], values[:, par, c, :], ps_d[:], ALU.mult).then_inc(d_empty, 1)
                dve.wait_ge(d_empty, d + 1)
                nc.vector.tensor_scalar(oT[:, c, :], oT[:, c, :], bv[:, c:c + 1], None, ALU.add).then_inc(ot_ready, 1)

            def output(b, t, d):
                dve.wait_ge(d_ready, d + 1)
                dve.wait_ge(residual, b * NT + NT)
                tiles = x[:, bass.ds(b * NT + 2 * t, 2), :]
                nc.vector.tensor_tensor(tiles, ps_d[:].rearrange("p (t n) -> p t n", t=2), tiles, ALU.add
                                        ).then_inc(d_empty, 1)

            for i in range(2):
                nc.vector.memset(v_ones[i][:, :, :, HD:], 1.0).then_inc(v_consts, 1)
            read_mask(0)
            normalise(0)
            centre(0)
            for k in range(4):
                part(0, k, 0)
                part(0, k, 1)
            for v in range(MX_LEAD):
                maxima(0, v)
                if v == HG - 1:
                    split_maxima(0, 0)
                if v == HG:
                    rows_of_maxima(0, 0, 0)

            def batch(b, par, first, last):
                for u in range(QUADS):
                    v = u + MX_LEAD
                    if v < H:
                        maxima(b, v)
                    elif not last:
                        maxima(b + 1, v - H)
                    if u % 4 == 0 and u < 12:
                        split_maxima(b, u // 4 + 1)
                    if u == 12 and not last:
                        split_maxima(b + 1, 0)
                    if not last:
                        if u == 0:
                            read_mask(b + 1)
                            normalise(b + 1)
                        elif u == 1:
                            centre(b + 1)
                        for k, at in ((0, 1), (1, 2), (2, 4), (3, 5)):
                            if u == at + 1:
                                part(b + 1, k, 1)
                            if u == at:
                                part(b + 1, k, 0)
                    if u == 3 and not first:
                        invert_denominators(b - 1)
                    if u % 4 == 1 and u < 12:
                        rows_of_maxima(b, u // 4 + 1, d_item(b, first, f"neg{u // 4 + 1}"))
                    if u == 13 and not last:
                        rows_of_maxima(b + 1, 0, d_item(b, first, "neg4"))
                    if not first:
                        if u in (7, 8):
                            weigh(b - 1, 1 - par, u - 7, d_item(b, first, f"rden{u - 7}"))
                        if u in (10, 11):
                            output(b - 1, u - 10, d_item(b, first, f"out{u - 10}"))

            batches(dve, batch)
            invert_denominators(B - 1)
            for c in range(KC):
                weigh(B - 1, (B - 1) % 2, c, D_END + c)
            for t in range(2):
                output(B - 1, t, D_END + 2 + t)

        @block.tensor
        def _(pe):
            def take_act(bb, item):
                if not (isinstance(bb, int) and bb == 0):
                    pe.wait_ge(a_empty, bb * A_ITEMS + item)
                elif item >= len(first_banks):
                    pe.wait_ge(a_empty, item + 1 - len(first_banks))
                return bank_of(bb, item)

            def project(bb, k):
                item, is_q, c = PROJ[k]
                bank = take_act(bb, item)
                if is_q:
                    pe.wait_ge(a_empty, bb * A_ITEMS + (XT1 + 1))
                else:
                    pe.wait_ge(ctx_in, (bb + 1) * 16)
                for kk in range(KC):
                    mm = nc.tensor.matmul(bank[:], (wq if is_q else wk)[:, kk, c * P:(c + 1) * P],
                                          (xT if is_q else ctxT)[:, kk, :], start=(kk == 0), stop=(kk == KC - 1))
                mm.then_inc(a_ready, 1)

            def transpose_x(bb, c):
                bank = take_act(bb, XT0 + c)
                pe.wait_ge(xn_ready, bb * NT + NT)
                for t in range(NT):
                    mm = nc.tensor.transpose(bank[:, t * P:(t + 1) * P], xn[:, t, c * P:(c + 1) * P], ident[:])
                mm.then_inc(a_ready, 1)

            def v_tiles(bb, t):
                bank = take_act(bb, V0 + t)
                for tt in range(2):
                    for kk in range(KC):
                        mm = nc.tensor.matmul(bank[:, tt * D:(tt + 1) * D],
                                              ctxT[:, kk, (2 * t + tt) * P:(2 * t + tt + 1) * P], wv[:, kk, :],
                                              start=(kk == 0), stop=(kk == KC - 1))
                mm.then_inc(a_ready, 1)

            def head_scores_max(b, par, v, s):
                n = b * 64 + (4 * v + s)
                if v % HC == 0 and s == 0:
                    pe.wait_ge(stacked[v // HC], b * 192 + 192)
                if v == 0 and s == 0:
                    pe.wait_ge(mask_landed, b * 16 + 16)
                if 4 * v + s >= MX_RING:
                    pe.wait_ge(max_read, n + (1 - MX_RING))
                elif v == 0 and s == 0 and not (isinstance(b, int) and b == 0):
                    pe.wait_ge(max_read, n)
                nc.tensor.matmul(ps_max[(4 * v + s) % MX_RING][:], q_stack[par][0:K_MAX, v, s * P:(s + 1) * P],
                                 k_stack[par][0:K_MAX, v, :], start=True, stop=True).then_inc(max_ready, 1)

            def rows_of_maxima(b, g, d):
                pe.wait_ge(neg_ready, b * 4 + (g + 1))
                if not (isinstance(d, int) and d == 0):
                    pe.wait_ge(d_empty, d)
                for t in range(NT):
                    mm = nc.tensor.transpose(ps_d[:].bitcast(BF16)[0:3 * HG, t * P:(t + 1) * P],
                                             neg_parts[:, t, :, :].rearrange("p j h -> p (j h)"), identb[:])
                mm.then_inc(d_ready, 1)

            def scores(b, par, u, hh):
                g, kc = divmod(u, NT)
                n = b * 64 + (4 * u + hh)
                if kc == 0 and hh == 0:
                    pe.wait_ge(neg_landed, (b * 4 + g) * 16 + 16)
                if not (isinstance(n, int) and n < 2):
                    pe.wait_ge(probs_ready, n - 1)
                elif n == 0:
                    pe.wait_ge(a_empty, A_ITEMS)
                nc.tensor.matmul(ps_score[hh % 2][:], k_stack[par][0:K_ALL, HG * g + hh, kc * P:(kc + 1) * P],
                                 q_stack[par][0:K_ALL, HG * g + hh, :], start=True, stop=True).then_inc(score_ready, 1)

            def weighted_values(b, par, w):
                g, kc = divmod(w, NT)
                G = b * 4 + g
                pe.wait_ge(probs_ready, b * 64 + (4 * w + 4))
                if w == 0:
                    pe.wait_ge(a_empty, b * A_ITEMS + A_ITEMS)
                    pe.wait_ge(v_consts, 2)
                if kc == 0 and not (isinstance(G, int) and G == 0):
                    pe.wait_ge(sums_ready, G)
                for hh in range(HG):
                    mm = nc.tensor.matmul(ps_pv[32 * hh:32 * hh + 32, :], v_ones[par][:, kc, HG * g + hh, :],
                                          probs[:, kc, hh, :], start=(kc == 0), stop=(kc == NT - 1),
                                          tile_position=(0, 32 * hh))
                mm.then_inc(pv_ready, 1)

            def spread_denominators(b, c, d):
                pe.wait_ge(rden_landed, b * 16 + 16)
                pe.wait_ge(d_empty, d)
                nc.tensor.matmul(ps_d[:], head_rows[:, c, :], rden_h[:, :], start=True, stop=True).then_inc(d_ready, 1)

            def output(b, t, d):
                pe.wait_ge(ot_ready, b * KC + KC)
                pe.wait_ge(d_empty, d)
                for tt in range(2):
                    for c in range(KC):
                        mm = nc.tensor.matmul(ps_d[:, tt * D:(tt + 1) * D], oT[:, c, (2 * t + tt) * P:(2 * t + tt + 1) * P],
                                              wo[:, c, :], start=(c == 0), stop=(c == KC - 1))
                mm.then_inc(d_ready, 1)

            pe.wait_ge(wk_in, 32)
            project(0, 0), project(0, 1)
            transpose_x(0, 0), transpose_x(0, 1)
            pe.wait_ge(w_in, 16 * 6)
            project(0, 2), project(0, 3)
            v_tiles(0, 0), v_tiles(0, 1)
            pe.wait_ge(consts, 6)
            pe.wait_ge(rows_set, 16 * 4)
            for v in range(MX_LEAD):
                for s in range(NT):
                    head_scores_max(0, 0, v, s)
                if v == HG:
                    rows_of_maxima(0, 0, 0)

            def batch(b, par, first, last):
                for u in range(QUADS):
                    v = u + MX_LEAD
                    for half in range(2):
                        for s in (2 * half, 2 * half + 1):
                            scores(b, par, u, s)
                            if v < H:
                                head_scores_max(b, par, v, s)
                            elif not last:
                                head_scores_max(b + 1, 1 - par, v - H, s)
                        if half == 0 and u >= PV_LAG:
                            weighted_values(b, par, u - PV_LAG)
                        elif half == 0 and not first:
                            weighted_values(b - 1, 1 - par, QUADS + u - PV_LAG)
                    if not last:
                        if u in (0, 1):
                            project(b + 1, u)
                        if u == 2:
                            transpose_x(b + 1, 0)
                            transpose_x(b + 1, 1)
                        if u in (3, 4):
                            project(b + 1, u - 1)
                        if u in (11, 12):
                            v_tiles(b + 1, u - 11)
                    if u % 4 == 1 and u < 12:
                        rows_of_maxima(b, u // 4 + 1, d_item(b, first, f"neg{u // 4 + 1}"))
                    if u == 13 and not last:
                        rows_of_maxima(b + 1, 0, d_item(b, first, "neg4"))
                    if not first:
                        if u in (7, 8):
                            spread_denominators(b - 1, u - 7, d_item(b, first, f"rden{u - 7}"))
                        if u in (10, 11):
                            output(b - 1, u - 10, d_item(b, first, f"out{u - 10}"))

            batches(pe, batch)
            for w in range(QUADS - PV_LAG, QUADS):
                weighted_values(B - 1, (B - 1) % 2, w)
            for c in range(KC):
                spread_denominators(B - 1, c, D_END + c)
            for t in range(2):
                output(B - 1, t, D_END + 2 + t)
    return spent


def expert_per_batch(nc, io, x, ident, spent, later):
    E, F = 8, 2 * D
    FC = F // P
    OUT_SCALE = 0.3
    ctx = ExitStack()
    with ctx:
        def sb(name, shape, dt=F32):
            return ctx.enter_context(nc.sbuf_tensor("b_" + name, shape, dt))

        def ps(name, shape, dt=F32):
            return ctx.enter_context(nc.psum_tensor("b_" + name, shape, dt))

        def sem(name):
            return ctx.enter_context(nc.semaphore("b_" + name))

        pw1, pb1, pw2, pb2 = sb("pw1", [P, KC, P]), sb("pb1", [P, 1]), sb("pw2", [P, E]), sb("pb2", [B, E])
        last = sb("last", [B, D])
        last_stats, last_moments = sb("last_stats", [B, 6]), sb("last_moments", [B, 2])
        last_var, last_rstd = sb("last_var", [B, 1]), sb("last_rstd", [B, 1])
        lastT, hiddenT = sb("lastT", [P, KC, B]), sb("hiddenT", [P, B])
        logits, neg_top, exps, total = sb("logits", [B, E]), sb("neg_top", [B, 1]), sb("exps", [B, E]), sb("total", [B, 1])
        inv_total, policy, top = sb("inv_total", [B, 1]), sb("policy", [B, E]), sb("top", [B, 1])
        countdown, winner = sb("countdown", [B, E]), sb("winner", [B, E])
        choice = sb("choice", [B, 1])
        choices = sb("choices", [1, B], I32)
        minus_half = sb("minus_half", [P, NT])
        w1 = [sb(f"w1_{i}", [P, KC, F]) for i in range(2)]
        w2 = [sb(f"w2_{i}", [P, FC, D]) for i in range(2)]
        b1 = [sb(f"b1_{i}", [P, FC]) for i in range(2)]
        b2 = [sb(f"b2_{i}", [P, KC]) for i in range(2)]
        wo, bo = sb("wo", [P, KC, D]), sb("bo", [P, D])
        stats, moments = sb("stats", [P, NT, 6]), sb("moments", [P, NT, 2])
        var_eps, rstd = sb("var_eps", [P, NT]), sb("rstd", [P, NT])
        xn = [sb(f"xn{i}", [P, NT, D]) for i in range(2)]
        xT = [sb(f"xT{i}", [P, KC, S]) for i in range(2)]
        hT = sb("hT", [P, FC, S])
        rT = [sb(f"rT{i}", [P, KC, S]) for i in range(2)]

        ps_t = [ps(f"t{i}", [P, S]) for i in range(2)]
        ps_h = [ps(f"h{i}", [P, S]) for i in range(2)]
        ps_r = [ps(f"r{i}", [P, S]) for i in range(2)]
        ps_o = [ps(f"o{i}", [P, S]) for i in range(2)]

        policy_in, wo_in, bo_in, last_in = sem("policy_in"), sem("wo_in"), sem("bo_in"), sem("last_in")
        up_in, down_in = [sem(f"up_in{i}") for i in range(2)], [sem(f"down_in{i}") for i in range(2)]
        consts, policy_dve, last_rstd_ready = sem("consts"), sem("policy_dve"), sem("last_rstd_ready")
        policy_pe, policy_act, bo_scaled = sem("policy_pe"), sem("policy_act"), sem("bo_scaled")
        stats_ready, moments_ready, var_ready, rstd_ready, xn_ready = (
            sem("stats_ready"), sem("moments_ready"), sem("var_ready"), sem("rstd_ready"), sem("xn_ready"))
        turned, xT_ready, h_sum, hT_ready, r_sum, rT_ready, o_sum, x_done, residual = (
            sem("turned"), sem("xT_ready"), sem("h_sum"), sem("hT_ready"), sem("r_sum"), sem("rT_ready"),
            sem("o_sum"), sem("x_done"), sem("residual"))

        def batches(eng, batch):
            batch(0, 0, True, False)
            with eng.Fori(0, (B - 2) // 2) as i:
                batch(i * 2 + 1, 1, False, False)
                batch(i * 2 + 2, 0, False, False)
            batch(B - 1, (B - 1) % 2, False, True)

        def tiles(b, t, n):
            return x[:, bass.ds(b * NT + t, n), :]

        block = ctx.enter_context(nc.Block())

        @block.sync
        def _(sp):
            sp.dma_start(last[:], x[P - 1:P, NT - 1:B * NT:NT, :]).then_inc(last_in, 16)
            sp.dma_start(pw1[:], io["pw1"].rearrange("(c p) n -> p c n", p=P)).then_inc(policy_in, 16)
            sp.dma_start(pb1[:], io["pb1"]).then_inc(policy_in, 16)
            sp.dma_start(pw2[:], io["pw2"]).then_inc(policy_in, 16)
            sp.dma_start(pb2[:], io["pb2"].to_broadcast([B, E])).then_inc(policy_in, 16)
            sp.dma_start(bo[:], io["fbo"].to_broadcast([P, D])).then_inc(bo_in, 16)
            sp.dma_start(wo[:], io["fwo"].rearrange("(c p) n -> p c n", p=P)).then_inc(wo_in, 16)
            numbers = [s.num for s in spent]
            sp.sem_clear(range(min(numbers), max(numbers) + 1))
            sp.wait_ge(policy_dve, 13)

            def load(bb, par):
                e = sp.value_load(choices[0:1, bass.ds(bb, 1)], min_val=0, max_val=E - 1)
                sp.dma_start(w1[par][:], io["fw1"][bass.ds(e, 1)].rearrange("a (c p) f -> p (a c) f", p=P)
                             ).then_inc(up_in[par], 16)
                sp.dma_start(b1[par][:], io["fb1"][bass.ds(e, 1)].rearrange("a p c -> p (a c)")
                             ).then_inc(up_in[par], 16)
                sp.dma_start(w2[par][:], io["fw2"][bass.ds(e, 1)].rearrange("a (c p) f -> p (a c) f", p=P)
                             ).then_inc(down_in[par], 16)
                sp.dma_start(b2[par][:], io["fb2"][bass.ds(e, 1)].rearrange("a p c -> p (a c)")
                             ).then_inc(down_in[par], 16)

            load(0, 0)

            def batch(b, par, first, last):
                if not last:
                    if not first:
                        sp.wait_ge(rT_ready, b * KC)
                    load(b + 1, 1 - par)
                else:
                    later.fetch(sp, io)

            batches(sp, batch)

        @block.gpsimd
        def _(pool):
            nc.gpsimd.memset(minus_half[:], -0.5).then_inc(consts, 1)
            nc.gpsimd.iota(countdown[:], pattern=[[-1, E]], base=E, channel_multiplier=0,
                           allow_small_or_imprecise_dtypes=True).then_inc(consts, 1)
            pool.wait_ge(consts, 2)
            pool.wait_ge(policy_dve, 3)
            nc.gpsimd.tensor_tensor(last_rstd[:], last_var[:], minus_half[0:B, 0:1], ALU.pow).then_inc(last_rstd_ready, 1)

            def invert_deviation(bb):
                pool.wait_ge(var_ready, bb + 1)
                nc.gpsimd.tensor_tensor(rstd[:], var_eps[:], minus_half[:], ALU.pow).then_inc(rstd_ready, 1)

            pool.wait_ge(last_rstd_ready, 1)
            invert_deviation(0)
            pool.wait_ge(bo_scaled, 1)

            def batch(b, par, first, last):
                if not last:
                    invert_deviation(b + 1)
                else:
                    later.set_constants(nc)
                pool.wait_ge(xn_ready, b * NT + NT)
                nc.gpsimd.tensor_tensor(tiles(b, 0, NT), tiles(b, 0, NT), xn[par][:], ALU.add).then_inc(residual, 1)
                for t in reversed(range(NT)):
                    tile = tiles(b, t, 1).rearrange("p a n -> p (a n)")
                    if t == NT - 1:
                        pool.wait_ge(residual, b * (NT + 1) + 1)
                    nc.gpsimd.tensor_tensor(tile, tile, bo[:], ALU.add).then_inc(residual, 1)

            batches(pool, batch)

        @block.vector
        def _(dve):
            step = [0]

            def chained(ins):
                step[0] += 1
                ins.then_inc(policy_dve, 1)
                dve.wait_ge(policy_dve, step[0])

            dve.wait_ge(last_in, 16)
            chained(nc.vector.bn_stats(last_stats[:], last[:]))
            chained(nc.vector.bn_aggr(last_moments[:], last_stats[:]))
            chained(nc.vector.tensor_scalar(last_var[:], last_moments[:, 1:2], EPS, None, ALU.add))
            dve.wait_ge(last_rstd_ready, 1)
            chained(nc.vector.tensor_scalar(last[:], last[:], last_moments[:, 0:1], last_rstd[:], ALU.subtract, ALU.mult))
            dve.wait_ge(policy_pe, 1)
            chained(nc.vector.tensor_copy(lastT[:], ps_t[0][:, 0:KC * B].rearrange("p (c b) -> p c b", c=KC)))

            def statistics(bb):
                for t in range(NT):
                    nc.vector.bn_stats(stats[:, t, :], tiles(bb, t, 1).rearrange("p a n -> p (a n)")
                                       ).then_inc(stats_ready, 1)
                dve.wait_ge(stats_ready, bb * NT + NT)
                nc.vector.memset(var_eps[:], EPS).then_inc(moments_ready, 1)
                for t in range(NT):
                    nc.vector.bn_aggr(moments[:, t, :], stats[:, t, :]).then_inc(moments_ready, 1)
                dve.wait_ge(moments_ready, bb * (NT + 1) + (NT + 1))
                nc.vector.tensor_tensor(var_eps[:], moments[:, :, 1], var_eps[:], ALU.add).then_inc(var_ready, 1)

            def centre(bb, par):
                dve.wait_ge(rstd_ready, bb + 1)
                for t in range(NT):
                    nc.vector.tensor_scalar(xn[par][:, t, :], tiles(bb, t, 1).rearrange("p a n -> p (a n)"),
                                            moments[:, t, 0:1], rstd[:, t:t + 1], ALU.subtract, ALU.mult
                                            ).then_inc(xn_ready, 1)

            statistics(0)
            dve.wait_ge(policy_pe, 3)
            dve.wait_ge(policy_in, 64)
            chained(nc.vector.tensor_tensor(logits[:], ps_t[0][0:B, 32:32 + E], pb2[:], ALU.add))
            chained(nc.vector.tensor_reduce(neg_top[:], logits[:], AX.X, ALU.max, negate=True))
            centre(0, 0)
            dve.wait_ge(policy_act, 2)
            chained(nc.vector.reciprocal(inv_total[:], total[:]))
            chained(nc.vector.tensor_scalar(policy[:], exps[:], inv_total[:], None, ALU.mult))
            chained(nc.vector.tensor_reduce(top[:], policy[:], AX.X, ALU.max))
            dve.wait_ge(consts, 2)
            chained(nc.vector.scalar_tensor_tensor(winner[:], policy[:], top[:], countdown[:], ALU.is_equal, ALU.mult))
            chained(nc.vector.tensor_reduce(choice[:], winner[:], AX.X, ALU.max))
            dve.wait_ge(policy_pe, 4)
            nc.vector.tensor_scalar(choices[:], ps_h[0][0:1, 0:B], -1.0, float(E), ALU.mult, ALU.add).then_inc(policy_dve, 1)
            dve.wait_ge(bo_in, 16)
            nc.vector.tensor_scalar(bo[:], bo[:], OUT_SCALE, None, ALU.mult).then_inc(bo_scaled, 1)

            for t in range(2):
                nc.vector.engine_nop().then_inc(x_done, 1)

            def output(b, t):
                dve.wait_ge(o_sum, b * 2 + (t + 1))
                if t == 0:
                    dve.wait_ge(residual, b * (NT + 1) + (NT + 1))
                nc.vector.scalar_tensor_tensor(tiles(b, 2 * t, 2).rearrange("p t n -> p (t n)"), ps_o[t][:], OUT_SCALE,
                                               tiles(b, 2 * t, 2).rearrange("p t n -> p (t n)"), ALU.mult, ALU.add
                                               ).then_inc(x_done, 1)

            def batch(b, par, first, last):
                if not last:
                    statistics(b + 1)
                    if not first:
                        dve.wait_ge(turned, b * KC)
                        dve.wait_ge(residual, b * (NT + 1))
                    centre(b + 1, 1 - par)
                if not first:
                    output(b - 1, 0)
                    output(b - 1, 1)
                if last:
                    later.centre_weights(nc, dve)

            batches(dve, batch)
            output(B - 1, 0)
            output(B - 1, 1)

        @block.scalar
        def _(act):
            act.wait_ge(policy_in, 64)
            act.wait_ge(policy_pe, 2)
            nc.scalar.activation(hiddenT[:], ps_t[0][:, 64:64 + B], ACT.Gelu, bias=pb1[:, 0:1]).then_inc(policy_act, 1)
            act.wait_ge(policy_dve, 7)
            nc.scalar.activation(exps[:], logits[:], ACT.Exp, bias=neg_top[:], accum_out=total[:]).then_inc(policy_act, 1)

            def transposed(bb, par):
                for c in range(KC):
                    act.wait_ge(turned, bb * KC + (c + 1))
                    nc.scalar.copy(xT[par][:, c, :], ps_t[c][:]).then_inc(xT_ready, 1)

            transposed(0, 0)

            def batch(b, par, first, last):
                for f in range(FC):
                    act.wait_ge(h_sum, b * FC + (f + 1))
                    if f == 0:
                        act.wait_ge(up_in[par], (b - par) * 16 + 32)
                        if not first:
                            act.wait_ge(r_sum, b * KC)
                    nc.scalar.activation(hT[:, f, :], ps_h[f % 2][:], ACT.Gelu, bias=b1[par][:, f:f + 1]
                                         ).then_inc(hT_ready, 1)
                act.wait_ge(down_in[par], (b - par) * 16 + 32)
                for c in range(KC):
                    act.wait_ge(r_sum, b * KC + (c + 1))
                    nc.scalar.activation(rT[par][:, c, :], ps_r[c][:], ACT.Identity, bias=b2[par][:, c:c + 1]
                                         ).then_inc(rT_ready, 1)
                if not last:
                    transposed(b + 1, 1 - par)

            batches(act, batch)

        @block.tensor
        def _(pe):
            pe.wait_ge(policy_dve, 4)
            for c in range(KC):
                mm = nc.tensor.transpose(ps_t[0][:, c * B:(c + 1) * B], last[:, c * P:(c + 1) * P], ident[0:B, 0:B])
            mm.then_inc(policy_pe, 1)
            pe.wait_ge(policy_dve, 5)
            pe.wait_ge(policy_in, 64)
            for c in range(KC):
                mm = nc.tensor.matmul(ps_t[0][:, 64:64 + B], pw1[:, c, :], lastT[:, c, :], start=(c == 0), stop=(c == KC - 1))
            mm.then_inc(policy_pe, 1)
            pe.wait_ge(policy_act, 1)
            nc.tensor.matmul(ps_t[0][0:B, 32:32 + E], hiddenT[:], pw2[:], start=True, stop=True).then_inc(policy_pe, 1)
            pe.wait_ge(policy_dve, 6)

            def transpose_x(bb, par):
                pe.wait_ge(xn_ready, bb * NT + NT)
                for c in range(KC):
                    if not (isinstance(bb, int) and bb == 0):
                        pe.wait_ge(xT_ready, (bb - 1) * KC + (c + 1))
                    for t in range(NT):
                        mm = nc.tensor.transpose(ps_t[c][:, t * P:(t + 1) * P], xn[par][:, t, c * P:(c + 1) * P], ident[:])
                    mm.then_inc(turned, 1)

            def up(b, par, first):
                pe.wait_ge(xT_ready, b * KC + KC)
                pe.wait_ge(up_in[par], (b - par) * 16 + 32)
                for f in range(FC):
                    if not (first and f < 2):
                        pe.wait_ge(hT_ready, b * FC + (f - 1))
                    for c in range(KC):
                        mm = nc.tensor.matmul(ps_h[f % 2][:], w1[par][:, c, f * P:(f + 1) * P], xT[par][:, c, :],
                                              start=(c == 0), stop=(c == KC - 1))
                    mm.then_inc(h_sum, 1)

            def down(b, par, first):
                pe.wait_ge(hT_ready, b * FC + FC)
                pe.wait_ge(down_in[par], (b - par) * 16 + 32)
                for c in range(KC):
                    if not first:
                        pe.wait_ge(rT_ready, (b - 1) * KC + (c + 1))
                    for f in range(FC):
                        mm = nc.tensor.matmul(ps_r[c][:], w2[par][:, f, c * P:(c + 1) * P], hT[:, f, :],
                                              start=(f == 0), stop=(f == FC - 1))
                    mm.then_inc(r_sum, 1)

            def output(b, par):
                pe.wait_ge(rT_ready, b * KC + KC)
                for t in range(2):
                    pe.wait_ge(x_done, b * 2 + (t + 1))
                    for tt in range(2):
                        for c in range(KC):
                            mm = nc.tensor.matmul(ps_o[t][:, tt * D:(tt + 1) * D],
                                                  rT[par][:, c, (2 * t + tt) * P:(2 * t + tt + 1) * P], wo[:, c, :],
                                                  start=(c == 0), stop=(c == KC - 1))
                    mm.then_inc(o_sum, 1)

            transpose_x(0, 0)
            pe.wait_ge(policy_dve, 12)
            nc.tensor.transpose(ps_h[0][0:1, 0:B], choice[:], ident[0:B, 0:B]).then_inc(policy_pe, 1)
            pe.wait_ge(policy_dve, 13)
            pe.wait_ge(wo_in, 16)

            def batch(b, par, first, last):
                up(b, par, first)
                if not first:
                    output(b - 1, 1 - par)
                down(b, par, first)
                if not last:
                    transpose_x(b + 1, 1 - par)

            batches(pe, batch)
            output(B - 1, (B - 1) % 2)


class SigmoidOperands:

    def __init__(self, nc, ctx):
        def sb(name, shape, dt=F32):
            return ctx.enter_context(nc.sbuf_tensor("c_" + name, shape, dt))

        def sem(name):
            return ctx.enter_context(nc.semaphore("c_" + name))

        self.wq, self.wk, self.wv, self.wo = (sb(n, [P, KC, D]) for n in ("wq", "wk", "wv", "wo"))
        self.w_mean = sb("w_mean", [P, 2, KC * KC, HC])
        self.gq, self.bq, self.gk, self.bk, self.eps = (sb(n, [P, 1]) for n in ("gq", "bq", "gk", "bk", "eps"))
        self.bo = sb("bo", [P, D])
        self.average = sb("average", [P, 4, HC])
        self.spread = sb("spread", [P, HD, HC])
        self.as_int = sb("as_int", [P, 2, P], I32)
        self.ctxT = sb("ctxT", [P, KC, S])
        self.wr, self.br = sb("wr", [P, KC, NE]), sb("br", [P, NE])
        self.v_pad = [sb(f"v_pad{i}", [P, NT, HC, 2, 2 * HD]) for i in range(2)]
        self.w_in, self.ctx_in, self.router_in = sem("w_in"), sem("ctx_in"), sem("router_in")
        self.consts, self.v_consts, self.means, self.centred = (sem("consts"), sem("v_consts"), sem("means"),
                                                                sem("centred"))

    def fetch(self, sp, io):
        for w, name in ((self.wk, "swk"), (self.wq, "swq"), (self.wv, "swv"), (self.wo, "swp")):
            sp.dma_start(w[:], io[name].rearrange("(c p) n -> p c n", p=P)).then_inc(self.w_in, 16)
        for dst, name in ((self.gq, "sgq"), (self.bq, "sbq"), (self.gk, "sgk"), (self.bk, "sbk")):
            sp.dma_start(dst[:], io[name]).then_inc(self.w_in, 16)
        sp.dma_start(self.bo[:], io["sbp"].to_broadcast([P, D])).then_inc(self.w_in, 16)
        self.fetch_context(sp, io, 0)
        sp.dma_start(self.wr[:], io["mwr"].rearrange("(c p) n -> p c n", p=P)).then_inc(self.router_in, 16)
        sp.dma_start(self.br[:], io["mbr"].to_broadcast([P, NE])).then_inc(self.router_in, 16)

    def fetch_context(self, sp, io, bb):
        sp.dma_start(self.ctxT[:], io["ctxT"][bass.ds(bb, 1)].rearrange("a (c p) n -> p (a c) n", p=P)
                     ).then_inc(self.ctx_in, 16)

    def set_constants(self, nc):
        for m in (self.average, self.spread):
            nc.gpsimd.iota(m[:], pattern=[[0, m.shape[1]], [-1, HC]], base=P, channel_multiplier=1,
                           allow_small_or_imprecise_dtypes=True).then_inc(self.consts, 1)
        nc.gpsimd.memset(self.eps[:], EPS).then_inc(self.consts, 1)
        for v in self.v_pad:
            for odd in range(2):
                nc.gpsimd.memset(v[:, :, :, odd, HD * (1 - odd):HD * (2 - odd)], 0.0).then_inc(self.v_consts, 1)

    def centre_weights(self, nc, dve):
        dve.wait_ge(self.w_in, 16 * 9)
        for i, w in enumerate((self.wk, self.wq)):
            by_head = w[:].rearrange("p c (k d h) -> p (c k) h d", d=HD, h=HC)
            nc.vector.tensor_reduce(self.w_mean[:, i], by_head, AX.X, ALU.add).then_inc(self.means, 1)
            dve.wait_ge(self.means, 2 * i + 1)
            nc.vector.tensor_scalar(self.w_mean[:, i], self.w_mean[:, i], 1.0 / HD, None, ALU.mult).then_inc(self.means, 1)
            dve.wait_ge(self.means, 2 * i + 2)
            for ck in range(KC * KC):
                part = w[:, ck // KC, P * (ck % KC):P * (ck % KC + 1)].rearrange("p (d h) -> p d h", d=HD)
                mean = self.w_mean[:, i, ck:ck + 1, :]
                mean = bass.AP(mean.tensor, mean.offset, [mean.ap[0], [0, HD], [1, HC]])
                nc.vector.tensor_tensor(part, part, mean, ALU.subtract).then_inc(self.centred, 1)
        dve.wait_ge(self.consts, 2)
        for i, (m, value) in enumerate(((self.average, 1.0 / HD), (self.spread, 1.0))):
            m32 = m[:].rearrange("p a h -> p (a h)")
            as_int = self.as_int[:, i, 0:m32.shape[1]]
            nc.vector.tensor_copy(as_int, m32).then_inc(self.means, 1)
            dve.wait_ge(self.means, 5 + 3 * i)
            nc.vector.tensor_scalar(as_int, as_int, HC - 1, None, ALU.bitwise_and).then_inc(self.means, 1)
            dve.wait_ge(self.means, 6 + 3 * i)
            nc.vector.tensor_scalar(m32, as_int, 0.0, value, ALU.is_equal, ALU.mult).then_inc(self.means, 1)


def sigmoid_attention(nc, io, x, ident, operands, logits, n_rows, sum_rows):
    QUADS = NG * NT
    PV_LAG = 2
    ctx = ExitStack()
    with ctx:
        def sb(name, shape, dt=F32):
            return ctx.enter_context(nc.sbuf_tensor("c_" + name, shape, dt))

        def ps(name, shape, dt=F32):
            return ctx.enter_context(nc.psum_tensor("c_" + name, shape, dt))

        def sem(name):
            return ctx.enter_context(nc.semaphore("c_" + name))

        wq, wk, wv, wo, bo, wr, br = (operands.wq, operands.wk, operands.wv, operands.wo, operands.bo, operands.wr,
                                      operands.br)
        gq, bq, gk, bk, eps = operands.gq, operands.bq, operands.gk, operands.bk, operands.eps
        average, spread, ctxT, v_pad = operands.average, operands.spread, operands.ctxT, operands.v_pad
        ctx_in, router_in = operands.ctx_in, operands.router_in
        stats, moments = sb("stats", [P, NT, 6]), sb("moments", [P, NT, 2])
        var_eps, rstd, minus_half = sb("var_eps", [P, NT]), sb("rstd", [P, NT]), sb("minus_half", [P, NT])
        xn, xT = sb("xn", [P, NT, D]), sb("xT", [P, KC, S])
        proj, square = sb("proj", [P, 4, S]), sb("square", [P, 4, S])
        head_std, head_rstd = sb("head_std", [P, S]), sb("head_rstd", [P, S])
        rest = sb("rest", [P, 2, S])
        parts = sb("parts", [P, 2, 3, S], BF16)
        q_stack = [sb(f"q_stack{i}", [K_MASK, H, S], BF16) for i in range(2)]
        k_stack = [sb(f"k_stack{i}", [K_MASK, H, S], BF16) for i in range(2)]
        probs = sb("probs", [P, NT, HG, S])
        oT = sb("oT", [P, KC, S])

        ps_score = [ps(f"score{i}", [P, S]) for i in range(HG)]
        ps_pv = [ps(f"pv{i}", [P, S]) for i in range(KC)]
        ps_a = ps("act", [P, S])
        ps_d = ps("dve", [P, S])

        minus_half_set = sem("minus_half_set")
        stats_ready, moments_ready, var_ready, rstd_ready, xn_ready = (
            sem("stats_ready"), sem("moments_ready"), sem("var_ready"), sem("rstd_ready"), sem("xn_ready"))
        a_ready, a_empty, d_ready, d_empty = sem("a_ready"), sem("a_empty"), sem("d_ready"), sem("d_empty")
        squared, head_rstd_ready, scaled = sem("squared"), sem("head_rstd_ready"), sem("scaled")
        part0, rest_ready, part1, part2 = sem("part0"), sem("rest_ready"), sem("part1"), sem("part2")
        stacked = [sem(f"stacked{i}") for i in range(2)]
        score_ready, probs_ready, pv_ready, ot_ready = (sem("score_ready"), sem("probs_ready"), sem("pv_ready"),
                                                        sem("ot_ready"))
        residual = sem("residual")
        row_stats, row_moments, row_var, row_rstd, rows_ready = (
            sem("row_stats"), sem("row_moments"), sem("row_var"), sem("row_rstd"), sem("rows_ready"))
        rows_out = sem("rows_out")

        def batches(eng, batch):
            batch(0, 0, True, False)
            with eng.Fori(0, (B - 2) // 2) as i:
                batch(i * 2 + 1, 1, False, False)
                batch(i * 2 + 2, 0, False, False)
            batch(B - 1, (B - 1) % 2, False, True)

        first_banks = (ps_a, *ps_score)

        def bank_of(bb, item):
            return first_banks[item % len(first_banks)] if isinstance(bb, int) and bb == 0 else ps_a

        spread_banks = (ps_d, *ps_pv)

        def spread_bank(bb, k):
            return spread_banks[k % len(spread_banks)] if isinstance(bb, int) and bb == 0 else ps_d

        KEYS0, KEYS1, XT0, XT1, QUERIES0, QUERIES1, VARIANCES, V0, V1 = range(9)
        A_ITEMS = 9
        PROJ = ((KEYS0, False, 0), (QUERIES0, True, 0), (KEYS1, False, 1), (QUERIES1, True, 1))
        D_FIRST = ("std0", "std1", "std2", "std3")
        D_ROWS = ("turn0", "turn1", "route")
        D_LATER = ("out0", "out1") + D_FIRST + D_ROWS
        D_LAST = ("out0", "out1") + D_ROWS
        D_END = 2 * len(D_FIRST) + (B - 2) * len(D_LATER) + len(D_LAST)

        def d_before(b):
            return (b - 1) * len(D_LATER) + 2 * len(D_FIRST)

        def d_item(b, first, last, name):
            if first:
                return len(D_FIRST) + D_FIRST.index(name)
            return d_before(b) + (D_LAST if last else D_LATER).index(name)

        def head_of(g, hh):
            return HC * (g // 2) + 2 * hh + g % 2

        AT = {KEYS0: 0, KEYS1: 1, XT0: 2, XT1: 3, QUERIES0: 4, QUERIES1: 5, VARIANCES: 7, V0: 8, V1: 13}
        STD_AT = (9, 10, 11, 12)
        OUT_AT = (3, 5)
        ROW_STATS_AT, ROWS_AT, TURN_AT, ROUTE_AT = 7, 10, (13, 14), 15

        block = ctx.enter_context(nc.Block())

        @block.sync
        def _(sp):
            def stack(bb, par, k):
                _, is_q, c = PROJ[k]
                dst = (q_stack if is_q else k_stack)[par]
                for part, ready in enumerate((part0, part1, part2)):
                    sp.wait_ge(ready, bb * 4 + (k + 1))
                    for j in range(PAIRS):
                        if (Q_PARTS if is_q else K_PARTS)[j] == part:
                            sp.dma_start(dst[HD * j:HD * (j + 1), HC * c:HC * (c + 1), :],
                                         parts[:, k % 2, part, :]).then_inc(stacked[k % 2], 16)

            for k in range(4):
                stack(0, 0, k)
                if k == 0:
                    sp.wait_ge(a_ready, A_ITEMS)
                    operands.fetch_context(sp, io, 1)

            def rows_to_dram(r):
                sp.wait_ge(rows_ready, r * NT + NT)
                for rows in (n_rows, sum_rows):
                    sp.dma_start(rows[bass.ds(r * S, S), :].rearrange("(t p) d -> p t d", p=P), xn[:]).then_inc(rows_out, 16)

            def batch(b, par, first, last):
                if not last:
                    if not first:
                        sp.wait_ge(a_ready, b * A_ITEMS + A_ITEMS)
                        operands.fetch_context(sp, io, b + 1)
                        sp.wait_ge(score_ready, b * 64)
                    for k in range(4):
                        stack(b + 1, 1 - par, k)
                        if k == 1 and not first:
                            rows_to_dram(b - 1)
                else:
                    rows_to_dram(b - 1)

            batches(sp, batch)
            rows_to_dram(B - 1)
            sp.wait_ge(rows_out, 32 * B + 1)

        @block.scalar
        def _(act):
            def evacuate(bb, item):
                bank = bank_of(bb, item)
                act.wait_ge(a_ready, bb * A_ITEMS + (item + 1))
                if item in (XT0, XT1):
                    if item == XT0 and not (isinstance(bb, int) and bb < 2):
                        act.wait_ge(d_ready, d_before(bb - 1))
                    nc.scalar.copy(xT[:, item - XT0, :], bank[:]).then_inc(a_empty, 1)
                elif item == VARIANCES:
                    nc.scalar.activation(head_std[:], bank[:], ACT.Sqrt, bias=eps[:, 0:1]).then_inc(a_empty, 1)
                else:
                    k = [i[0] for i in PROJ].index(item)
                    if not (isinstance(bb, int) and bb == 0):
                        act.wait_ge(rest_ready, (bb - 1) * 4 + (k + 1))
                    nc.scalar.copy(proj[:, k, :], bank[:]).then_inc(squared, 1)
                    nc.scalar.activation(square[:, k, :], bank[:], ACT.Square).then_inc(a_empty, 1)

            def v_tiles(bb, par, t):
                bank = bank_of(bb, V0 + t)
                act.wait_ge(a_ready, bb * A_ITEMS + (V0 + t + 1))
                for odd in range(2):
                    ins = nc.scalar.copy(
                        v_pad[par][:, 2 * t:2 * t + 2, :, odd, HD * odd:HD * (odd + 1)],
                        bank[:].rearrange("p (t h o d) -> p t h o d", t=2, h=HC, o=2)[:, :, :, odd, :])
                    ins.then_inc(squared if odd == 0 else a_empty, 1)

            for item in range(V0):
                evacuate(0, item)
            v_tiles(0, 0, 0), v_tiles(0, 0, 1)

            def batch(b, par, first, last):
                for u in range(QUADS):
                    kc = u % NT
                    quad = b * QUADS + u
                    for hh in range(HG):
                        act.wait_ge(score_ready, quad * HG + (hh + 1))
                        if hh == 0 and not (first and u < NT):
                            act.wait_ge(pv_ready, quad + (1 - NT))
                        nc.scalar.activation(probs[:, kc, hh, :], ps_score[hh][:], ACT.Sigmoid, scale=SCALE
                                             ).then_inc(probs_ready, 1)
                    if not last:
                        for item in range(V0):
                            if AT[item] == u:
                                evacuate(b + 1, item)
                        for t in range(2):
                            if AT[V0 + t] == u:
                                v_tiles(b + 1, 1 - par, t)

            batches(act, batch)

        @block.gpsimd
        def _(pool):
            nc.gpsimd.memset(minus_half[:], -0.5).then_inc(minus_half_set, 1)

            def invert_deviation(bb):
                pool.wait_ge(var_ready, bb + 1)
                nc.gpsimd.tensor_tensor(rstd[:], var_eps[:], minus_half[:], ALU.pow).then_inc(rstd_ready, 1)

            def remainder(bb, k):
                pool.wait_ge(part0, bb * 4 + (k + 1))
                if k >= 2:
                    pool.wait_ge(part2, bb * 4 + (k - 1))
                nc.gpsimd.tensor_tensor(rest[:, k % 2, :], proj[:, k, :], parts[:, k % 2, 0, :], ALU.subtract
                                        ).then_inc(rest_ready, 1)

            def third(bb, k):
                pool.wait_ge(part1, bb * 4 + (k + 1))
                nc.gpsimd.tensor_tensor(parts[:, k % 2, 2, :], rest[:, k % 2, :], parts[:, k % 2, 1, :], ALU.subtract
                                        ).then_inc(part2, 1)

            def invert_row_deviation(r):
                pool.wait_ge(row_var, r + 1)
                nc.gpsimd.tensor_tensor(rstd[:], var_eps[:], minus_half[:], ALU.pow).then_inc(row_rstd, 1)

            def prepare(bb, row):
                invert_deviation(bb)
                if row is not None:
                    invert_row_deviation(row)
                for k in range(4):
                    remainder(bb, k)
                    third(bb, k)

            pool.wait_ge(minus_half_set, 1)
            prepare(0, None)

            def batch(b, par, first, last):
                for t in range(NT):
                    tile = x[:, bass.ds(b * NT + t, 1), :].rearrange("p a n -> p (a n)")
                    if t == 0:
                        pool.wait_ge(xn_ready, b * NT + NT)
                    nc.gpsimd.tensor_tensor(tile, tile, bo[:], ALU.add).then_inc(residual, 1)
                if not last:
                    prepare(b + 1, None if first else b - 1)
                else:
                    invert_row_deviation(b - 1)

            batches(pool, batch)
            invert_row_deviation(B - 1)

        @block.vector
        def _(dve):
            def statistics(bb):
                for t in range(NT):
                    nc.vector.bn_stats(stats[:, t, :], x[:, bass.ds(bb * NT + t, 1), :].rearrange("p a n -> p (a n)")
                                       ).then_inc(stats_ready, 1)
                dve.wait_ge(stats_ready, bb * NT + NT)
                nc.vector.memset(var_eps[:], EPS).then_inc(moments_ready, 1)
                for t in range(NT):
                    nc.vector.bn_aggr(moments[:, t, :], stats[:, t, :]).then_inc(moments_ready, 1)
                dve.wait_ge(moments_ready, bb * (NT + 1) + (NT + 1))
                nc.vector.tensor_tensor(var_eps[:], moments[:, :, 1], var_eps[:], ALU.add).then_inc(var_ready, 1)

            def centre(bb):
                dve.wait_ge(rstd_ready, bb + 1)
                if not (isinstance(bb, int) and bb == 0):
                    dve.wait_ge(a_ready, (bb - 1) * A_ITEMS + (XT1 + 1))
                if not (isinstance(bb, int) and bb < 2):
                    dve.wait_ge(rows_out, (bb - 2) * 32 + 1)
                    dve.wait_ge(d_ready, d_before(bb - 1))
                for t in range(NT):
                    nc.vector.tensor_scalar(xn[:, t, :], x[:, bass.ds(bb * NT + t, 1), :].rearrange("p a n -> p (a n)"),
                                            moments[:, t, 0:1], rstd[:, t:t + 1], ALU.subtract, ALU.mult
                                            ).then_inc(xn_ready, 1)

            def invert_std(bb):
                dve.wait_ge(a_empty, bb * A_ITEMS + (VARIANCES + 1))
                if not (isinstance(bb, int) and bb == 0):
                    spread_before = len(D_FIRST) if isinstance(bb, int) and bb == 1 else d_before(bb - 1)
                    dve.wait_ge(d_ready, spread_before)
                nc.vector.reciprocal(head_rstd[:], head_std[:]).then_inc(head_rstd_ready, 1)

            def scale(bb, k, d):
                _, is_q, _ = PROJ[k]
                n = bb * 4 + k
                dve.wait_ge(d_ready, d + 1)
                nc.vector.tensor_tensor(proj[:, k, :], proj[:, k, :], spread_bank(bb, k)[:], ALU.mult).then_inc(d_empty, 1)
                dve.wait_ge(d_empty, d + 1)
                nc.vector.tensor_scalar(proj[:, k, :], proj[:, k, :], (gq if is_q else gk)[:, 0:1],
                                        (bq if is_q else bk)[:, 0:1], ALU.mult, ALU.add).then_inc(scaled, 1)
                dve.wait_ge(scaled, n + 1)
                dve.wait_ge(stacked[k % 2], bb * 192 + 96 * (k // 2))
                nc.vector.tensor_copy(parts[:, k % 2, 0, :], proj[:, k, :]).then_inc(part0, 1)

            def second(bb, k):
                dve.wait_ge(rest_ready, bb * 4 + (k + 1))
                nc.vector.tensor_copy(parts[:, k % 2, 1, :], rest[:, k % 2, :]).then_inc(part1, 1)

            def heads_out(b, c):
                dve.wait_ge(pv_ready, b * QUADS + 8 * (c + 1))
                if not (isinstance(b, int) and b == 0) and c == 0:
                    dve.wait_ge(d_ready, d_before(b) + 2)
                nc.vector.tensor_copy(oT[:, c, :], ps_pv[c][:]).then_inc(ot_ready, 1)

            def output(b, t, d):
                dve.wait_ge(d_ready, d + 1)
                dve.wait_ge(residual, b * NT + NT)
                two = x[:, bass.ds(b * NT + 2 * t, 2), :]
                nc.vector.tensor_tensor(two, ps_d[:].rearrange("p (t n) -> p t n", t=2), two, ALU.add).then_inc(d_empty, 1)

            def row_statistics(r, out_item):
                dve.wait_ge(d_empty, out_item + 1)
                nc.vector.memset(var_eps[:, 0:2], EPS).then_inc(row_moments, 1)
                for t in range(NT):
                    nc.vector.bn_stats(stats[:, t, :], x[:, bass.ds(r * NT + t, 1), :].rearrange("p a n -> p (a n)")
                                       ).then_inc(row_stats, 1)
                dve.wait_ge(row_stats, r * NT + NT)
                nc.vector.memset(var_eps[:, 2:NT], EPS).then_inc(row_moments, 1)
                for t in range(NT):
                    nc.vector.bn_aggr(moments[:, t, :], stats[:, t, :]).then_inc(row_moments, 1)
                dve.wait_ge(row_moments, r * (NT + 2) + (NT + 2))
                nc.vector.tensor_tensor(var_eps[:], moments[:, :, 1], var_eps[:], ALU.add).then_inc(row_var, 1)

            def normalised_rows(r):
                dve.wait_ge(row_rstd, r + 1)
                for t in range(NT):
                    nc.vector.tensor_scalar(xn[:, t, :], x[:, bass.ds(r * NT + t, 1), :].rearrange("p a n -> p (a n)"),
                                            moments[:, t, 0:1], rstd[:, t:t + 1], ALU.subtract, ALU.mult
                                            ).then_inc(rows_ready, 1)

            def turned_rows(c, d):
                dve.wait_ge(d_ready, d + 1)
                nc.vector.tensor_copy(xT[:, c, :], ps_d[:]).then_inc(d_empty, 1)

            def routed(r, d):
                dve.wait_ge(d_ready, d + 1)
                nc.vector.tensor_tensor(logits[:, :, bass.ds(r * NT, NT)].rearrange("p e t -> p t e"),
                                        ps_d[:, 0:NT * NE].rearrange("p (t e) -> p t e", t=NT),
                                        bass.AP(br[:].tensor, br[:].offset, [br[:].ap[0], [0, NT], [1, NE]]), ALU.add
                                        ).then_inc(d_empty, 1)

            nc.vector.engine_nop().then_inc(rows_out, 1)
            statistics(0)
            centre(0)
            invert_std(0)
            for k in range(4):
                scale(0, k, k)
                if k >= 1:
                    second(0, k - 1)
            second(0, 3)

            def batch(b, par, first, last):
                for u in range(QUADS):
                    if not last:
                        for k in range(4):
                            if u == STD_AT[k] + 1:
                                second(b + 1, k)
                        if u == 0:
                            statistics(b + 1)
                        if u == 1:
                            centre(b + 1)
                    if u == 2 and not first:
                        heads_out(b - 1, 1)
                    if u == 10:
                        heads_out(b, 0)
                    if not last and u == AT[VARIANCES] + 1:
                        invert_std(b + 1)
                    for t in range(2):
                        if not first and u == OUT_AT[t]:
                            output(b - 1, t, d_item(b, first, last, f"out{t}"))
                    for k in range(4):
                        if not last and u == STD_AT[k]:
                            scale(b + 1, k, d_item(b, first, last, f"std{k}"))
                    if not first:
                        if u == ROW_STATS_AT:
                            row_statistics(b - 1, d_item(b, first, last, "out1"))
                        if u == ROWS_AT:
                            if last:
                                dve.wait_ge(rows_out, (b - 1) * 32 + 1)
                                dve.wait_ge(d_ready, d_before(b))
                            else:
                                dve.wait_ge(a_ready, b * A_ITEMS + (A_ITEMS + QUERIES1 + 1))
                            normalised_rows(b - 1)
                        for c in range(KC):
                            if u == TURN_AT[c]:
                                turned_rows(c, d_item(b, first, last, f"turn{c}"))
                        if u == ROUTE_AT:
                            dve.wait_ge(router_in, 32)
                            routed(b - 1, d_item(b, first, last, "route"))

            batches(dve, batch)
            heads_out(B - 1, 1)
            for t in range(2):
                output(B - 1, t, D_END + t)
            row_statistics(B - 1, D_END + 1)
            dve.wait_ge(rows_out, (B - 1) * 32 + 1)
            dve.wait_ge(d_ready, D_END)
            normalised_rows(B - 1)
            for c in range(KC):
                turned_rows(c, D_END + 2 + c)
            routed(B - 1, D_END + 2 + KC)

        @block.tensor
        def _(pe):
            def take_act(bb, item):
                if not (isinstance(bb, int) and bb == 0):
                    pe.wait_ge(a_empty, bb * A_ITEMS + item)
                    return
                read = {QUERIES0: XT1 + 1, QUERIES1: XT1 + 1, VARIANCES: VARIANCES}.get(item, 0)
                done = max(read, item + 1 - len(first_banks))
                if done > 0:
                    pe.wait_ge(a_empty, done)

            def prepare(bb, item):
                take_act(bb, item)
                bank = bank_of(bb, item)
                if item in (XT0, XT1):
                    c = item - XT0
                    pe.wait_ge(xn_ready, bb * NT + NT)
                    for t in range(NT):
                        mm = nc.tensor.transpose(bank[:, t * P:(t + 1) * P], xn[:, t, c * P:(c + 1) * P], ident[:])
                elif item == VARIANCES:
                    for k in range(4):
                        mm = nc.tensor.matmul(bank[32 * k:32 * k + 32, :], average[:].rearrange("p a h -> p (a h)"),
                                              square[:, k, :], start=True, stop=True, tile_position=(0, 32 * k))
                elif item in (V0, V1):
                    for tt in range(2):
                        for kk in range(KC):
                            at = 2 * (item - V0) + tt
                            mm = nc.tensor.matmul(bank[:, tt * D:(tt + 1) * D], ctxT[:, kk, at * P:(at + 1) * P],
                                                  wv[:, kk, :], start=(kk == 0), stop=(kk == KC - 1))
                else:
                    _, is_q, c = PROJ[[i[0] for i in PROJ].index(item)]
                    if not is_q:
                        pe.wait_ge(ctx_in, (bb + 1) * 16)
                    for kk in range(KC):
                        mm = nc.tensor.matmul(bank[:], (wq if is_q else wk)[:, kk, c * P:(c + 1) * P],
                                              (xT if is_q else ctxT)[:, kk, :], start=(kk == 0), stop=(kk == KC - 1))
                mm.then_inc(a_ready, 1)

            def spread_deviations(bb, k, d):
                pe.wait_ge(head_rstd_ready, bb + 1)
                if not (isinstance(bb, int) and bb == 0):
                    pe.wait_ge(d_empty, d)
                elif k >= len(spread_banks):
                    pe.wait_ge(d_empty, k + 1 - len(spread_banks))
                nc.tensor.matmul(spread_bank(bb, k)[:], spread[32 * k:32 * k + HC].rearrange("p a h -> p (a h)"),
                                 head_rstd[32 * k:32 * k + HC, :], start=True, stop=True,
                                 tile_position=(32 * k, 0)).then_inc(d_ready, 1)

            def scores(b, par, u, hh):
                g, kc = divmod(u, NT)
                n = b * 64 + (4 * u + hh)
                h = head_of(g, hh)
                if u % (QUADS // KC) == 0 and hh == 0:
                    for i in range(2):
                        pe.wait_ge(stacked[i], b * 192 + 96 * (u // (QUADS // KC) + 1))
                if not (isinstance(n, int) and n < HG):
                    pe.wait_ge(probs_ready, n + (1 - HG))
                elif n == 0:
                    pe.wait_ge(a_empty, A_ITEMS)
                nc.tensor.matmul(ps_score[hh][:], k_stack[par][:, h, kc * P:(kc + 1) * P], q_stack[par][:, h, :],
                                 start=True, stop=True).then_inc(score_ready, 1)

            def weighted_values(b, par, w):
                g, kc = divmod(w, NT)
                c, odd = divmod(g, 2)
                pe.wait_ge(probs_ready, b * 64 + (4 * w + 4))
                if w == 0:
                    pe.wait_ge(a_empty, b * A_ITEMS + A_ITEMS)
                if w == 0 and isinstance(b, int) and b == 0:
                    pe.wait_ge(d_empty, len(D_FIRST))
                if kc == 0 and odd == 0 and not (isinstance(b, int) and b == 0):
                    pe.wait_ge(ot_ready, b * KC + (c - 1))
                for hh in range(HG):
                    mm = nc.tensor.matmul(ps_pv[c][32 * hh:32 * hh + 32, :], v_pad[par][:, kc, HG * c + hh, odd, :],
                                          probs[:, kc, hh, :], start=(kc == 0 and odd == 0),
                                          stop=(kc == NT - 1 and odd == 1), tile_position=(0, 32 * hh))
                mm.then_inc(pv_ready, 1)

            def output(b, t, d):
                pe.wait_ge(ot_ready, b * KC + KC)
                pe.wait_ge(d_empty, d)
                for tt in range(2):
                    for c in range(KC):
                        mm = nc.tensor.matmul(ps_d[:, tt * D:(tt + 1) * D], oT[:, c, (2 * t + tt) * P:(2 * t + tt + 1) * P],
                                              wo[:, c, :], start=(c == 0), stop=(c == KC - 1))
                mm.then_inc(d_ready, 1)

            def turn_rows(r, c, d):
                pe.wait_ge(rows_ready, r * NT + NT)
                pe.wait_ge(d_empty, d)
                for t in range(NT):
                    mm = nc.tensor.transpose(ps_d[:, t * P:(t + 1) * P], xn[:, t, c * P:(c + 1) * P], ident[:])
                mm.then_inc(d_ready, 1)

            def route(d):
                pe.wait_ge(d_empty, d)
                for t in range(NT):
                    for c in range(KC):
                        mm = nc.tensor.matmul(ps_d[:, t * NE:(t + 1) * NE], xT[:, c, t * P:(t + 1) * P], wr[:, c, :],
                                              start=(c == 0), stop=(c == KC - 1))
                mm.then_inc(d_ready, 1)

            for item in range(A_ITEMS):
                prepare(0, item)
            for k in range(4):
                spread_deviations(0, k, k)

            def batch(b, par, first, last):
                for u in range(QUADS):
                    for half in range(2):
                        for hh in (2 * half, 2 * half + 1):
                            scores(b, par, u, hh)
                        if half == 0 and u >= PV_LAG:
                            weighted_values(b, par, u - PV_LAG)
                        elif half == 0 and not first:
                            weighted_values(b - 1, 1 - par, QUADS + u - PV_LAG)
                    for t in range(2):
                        if not first and u == OUT_AT[t]:
                            output(b - 1, t, d_item(b, first, last, f"out{t}"))
                    if not first:
                        for c in range(KC):
                            if u == TURN_AT[c]:
                                turn_rows(b - 1, c, d_item(b, first, last, f"turn{c}"))
                        if u == ROUTE_AT:
                            pe.wait_ge(router_in, 32)
                            route(d_item(b, first, last, "route"))
                    if not last:
                        for item in range(A_ITEMS):
                            if AT[item] == u:
                                prepare(b + 1, item)
                        for k in range(4):
                            if STD_AT[k] == u:
                                spread_deviations(b + 1, k, d_item(b, first, last, f"std{k}"))

            batches(pe, batch)
            for w in range(QUADS - PV_LAG, QUADS):
                weighted_values(B - 1, (B - 1) % 2, w)
            for t in range(2):
                output(B - 1, t, D_END + t)
            for c in range(KC):
                turn_rows(B - 1, c, D_END + 2 + c)
            route(D_END + 2 + KC)


def mixture(nc, io, x, ident, logits, n_rows, sum_rows, out):
    E, F = NE, 4 * D
    FC = F // P
    T = B * NT
    N = T * P
    CT = CAP // P
    assert CT * P == CAP
    outer = ExitStack()
    with outer:
        def sb(name, shape, dt=F32):
            return outer.enter_context(nc.sbuf_tensor("d_" + name, shape, dt))

        t = dict(
            gamma=sb("gamma", [P, D]), beta=sb("beta", [P, D]), b1=sb("b1", [P, E, FC]),
            w1=[sb(f"w1_{i}", [P, KC, F]) for i in range(2)], w2=[sb(f"w2_{i}", [P, FC, D]) for i in range(2)],
            minus_half=sb("minus_half", [P, T]),
            key=sb("key", [P, E, T]),
            gate_parts=sb("gate_parts", [P, 3, E, T], BF16),
            row=sb("row", [P, E, T], BF16), lane=sb("lane", [P, E, T], BF16),
            lanes=sb("lanes", [P, P], BF16),
            rows_of=sb("rows_of", [P, CT], BF16),
            numbers=sb("numbers", [P, 2, T], BF16),
            spare=sb("spare", [P, CT]))
        weights_in = [outer.enter_context(nc.semaphore(f"d_weights_in{i}")) for i in range(2)]
        route(nc, io, x, ident, logits, n_rows, sum_rows, weights_in, E, F, FC, T, N, CT, **t)
        experts(nc, io, x, ident, n_rows, sum_rows, weights_in, E, F, FC, T, N, CT, out, **t)


def load_expert(sp, io, e, w1, w2, weights_in):
    sp.dma_start(w1[:], io["mw1"][bass.ds(e, 1)].rearrange("a (c p) f -> p (a c) f", p=P)).then_inc(weights_in, 16)
    sp.dma_start(w2[:], io["mw2"][bass.ds(e, 1)].rearrange("a (c p) f -> p (a c) f", p=P)).then_inc(weights_in, 16)


def repeated(ap, *pattern):
    return bass.AP(ap.tensor, ap.offset, [ap.ap[0], *[list(p) for p in pattern]])


def route(nc, io, x, ident, logits, n_rows, sum_rows, weights_in, E, F, FC, T, N, CT, gamma, beta, b1, w1, w2,
          minus_half, key, gate_parts, row, lane, lanes, rows_of, numbers, spare):
    LOW = -3.0e38
    BITS = 30
    DIGIT = 2
    TRIED = (1 << DIGIT) - 1
    ROUNDS, UNROLLED = BITS // DIGIT, 5
    STEPS = 4 + 2 * TRIED
    HALVES = 2
    EXPERTS = E // HALVES
    assert EXPERTS * T == P
    ctx = ExitStack()
    with ctx:
        def sb(name, shape, dt=F32):
            return ctx.enter_context(nc.sbuf_tensor("r_" + name, shape, dt))

        def ps(name, shape, dt=F32):
            return ctx.enter_context(nc.psum_tensor("r_ps_" + name, shape, dt))

        def sem(name):
            return ctx.enter_context(nc.semaphore("r_" + name))

        zeros = sb("zeros", [P, CT, D])
        work, work2, first, second = (sb(n, [P, E, T]) for n in ("work", "work2", "first", "second"))
        countdown = sb("countdown", [P, E])
        v1, v2, w_first, w_second = (sb(n, [P, T]) for n in ("v1", "v2", "w_first", "w_second"))
        gate_rest = sb("gate_rest", [P, E, T])
        keyT, above, ties, rank, taken = (sb(n, [P, HALVES, P]) for n in ("keyT", "above", "ties", "rank", "taken"))
        no_carry = sb("no_carry", [P, HALVES, P])
        threshold = sb("threshold", [P, HALVES])
        digit, candidate = (sb(n, [P, HALVES, TRIED + 1], I32) for n in ("digit", "candidate"))
        reached = sb("reached", [P, HALVES, TRIED + 1])
        counts = sb("counts", [P, HALVES, TRIED + 1], BF16)
        count, tie_count, fits = sb("count", [P, HALVES], BF16), sb("tie_count", [P, HALVES], BF16), sb("fits", [P, HALVES])
        same, earlier = sb("same", [P, P], BF16), sb("earlier", [P, P], BF16)
        slot, slot_row = sb("slot", [P, E, T]), sb("slot_row", [P, E, T])

        ps_key = [ps(f"key{h}", [P, S]) for h in range(HALVES)]
        ps_count, ps_earlier = ps("count", [P, S]), ps("earlier", [P, S])
        ps_slot = ps("slot", [P, S])

        consts, small_in, spare_out = sem("consts"), sem("small_in"), sem("spare_out")
        chain, exp_ready, search, counted = sem("chain"), sem("exp_ready"), sem("search"), sem("counted")
        key_ready, key_turned, ties_ready, ties_summed = sem("key_ready"), sem("key_turned"), sem("ties_ready"), sem("ties_summed")
        taken_ready, taken_summed, slot_ready, slot_turned = (sem("taken_ready"), sem("taken_summed"), sem("slot_ready"),
                                                              sem("slot_turned"))
        beta_added, gate_split = sem("beta_added"), sem("gate_split")

        def over_experts(ap):
            return repeated(ap, (0, E), (1, T))

        block = ctx.enter_context(nc.Block())

        @block.sync
        def _(sp):
            sp.dma_start(gamma[:], io["mgamma"].to_broadcast([P, D])).then_inc(small_in, 16)
            sp.dma_start(beta[:], io["mbeta"].to_broadcast([P, D])).then_inc(small_in, 16)
            sp.dma_start(b1[:], io["mb1"].rearrange("e p c -> p e c")).then_inc(small_in, 16)
            for e in range(2):
                load_expert(sp, io, e, w1[e], w2[e], weights_in[e])
            sp.wait_ge(consts, 1)
            for rows in (n_rows, sum_rows):
                sp.dma_start(rows[N:N + CAP, :].rearrange("(t p) d -> p t d", p=P), zeros[:]).then_inc(spare_out, 16)
            sp.wait_ge(small_in, 48)
            sp.wait_ge(spare_out, 32)

        @block.gpsimd
        def _(pool):
            def const(ins):
                const.n += 1
                ins.then_inc(consts, 1)
                pool.wait_ge(consts, const.n)
            const.n = 0
            fine = dict(allow_small_or_imprecise_dtypes=True)
            const(nc.gpsimd.memset(zeros[:], 0.0))
            const(nc.gpsimd.iota(countdown[:], pattern=[[-1, E]], base=E, channel_multiplier=0, **fine))
            const(nc.gpsimd.memset(same[:], 0.0))
            for k in range(EXPERTS):
                const(nc.gpsimd.memset(same[T * k:T * (k + 1), T * k:T * (k + 1)], 1.0))
            const(nc.gpsimd.affine_select(out=earlier[:], in_=same[:], compare_op=ALU.is_ge, fill=0.0, base=-1,
                                          pattern=[[1, P]], channel_multiplier=-1))
            const(nc.gpsimd.memset(no_carry[:], 1.0))
            const(nc.gpsimd.memset(no_carry[:, :, 0], 0.0))
            const(nc.gpsimd.memset(minus_half[:], -0.5))
            const(nc.gpsimd.iota(lanes[:], pattern=[[1, P]], base=0, channel_multiplier=0, **fine))
            const(nc.gpsimd.iota(rows_of[:], pattern=[[1, CT]], base=0, channel_multiplier=0, **fine))
            const(nc.gpsimd.iota(numbers[:, 0, :], pattern=[[1, T]], base=0, channel_multiplier=0, **fine))
            const(nc.gpsimd.iota(numbers[:, 1, :], pattern=[[0, T]], base=0, channel_multiplier=1, **fine))
            const(nc.gpsimd.iota(spare[:], pattern=[[P, CT]], base=N, channel_multiplier=1, **fine))
            pool.wait_ge(small_in, 48)
            with pool.Fori(0, T) as t:
                tile = x[:, bass.ds(t, 1), :].rearrange("p a n -> p (a n)")
                nc.gpsimd.tensor_tensor(tile, tile, beta[:], ALU.add).then_inc(beta_added, 1)
            pool.wait_ge(key_ready, 1)
            nc.gpsimd.tensor_copy(gate_parts[:, 0], key[:]).then_inc(gate_split, 1)
            pool.wait_ge(gate_split, 1)
            nc.gpsimd.tensor_tensor(gate_rest[:], key[:], gate_parts[:, 0], ALU.subtract).then_inc(gate_split, 1)
            pool.wait_ge(gate_split, 2)
            nc.gpsimd.tensor_copy(gate_parts[:, 1], gate_rest[:]).then_inc(gate_split, 1)
            pool.wait_ge(gate_split, 3)
            nc.gpsimd.tensor_tensor(gate_parts[:, 2], gate_rest[:], gate_parts[:, 1], ALU.subtract).then_inc(gate_split, 1)

        @block.scalar
        def _(act):
            act.wait_ge(chain, 12)
            nc.scalar.activation(v2[:], v2[:], ACT.Exp).then_inc(exp_ready, 1)

        @block.vector
        def _(dve):
            class Chain:
                def __init__(self, sem, base=0):
                    self.sem, self.base, self.n = sem, base, 0

                def __call__(self, ins):
                    self.beside(ins)
                    dve.wait_ge(self.sem, self.base + self.n)

                def beside(self, ins):
                    self.n += 1
                    ins.then_inc(self.sem, 1)

            V = nc.vector
            flat = "p e t -> p (e t)"
            by_token = "p e t -> p t e"
            step_of = Chain(chain)
            preference = repeated(countdown[:], (1, E), (0, T))
            dve.wait_ge(consts, 2)

            def best(values, value, hot):
                step_of(V.tensor_tensor(work[:], values[:], over_experts(value[:]), ALU.is_equal))
                step_of(V.tensor_tensor(work[:], work[:], preference, ALU.mult))
                step_of(V.tensor_reduce(w_first[:], work[:].rearrange(by_token), AX.X, ALU.max))
                step_of(V.tensor_tensor(hot[:], work[:], over_experts(w_first[:]), ALU.is_equal))

            step_of(V.tensor_reduce(v1[:], logits[:].rearrange(by_token), AX.X, ALU.max))
            best(logits, v1, first)
            step_of(V.tensor_scalar(work[:], first[:], -1.0, 1.0, ALU.mult, ALU.add))
            step_of(V.tensor_tensor(work2[:], logits[:], work[:], ALU.mult))
            step_of(V.scalar_tensor_tensor(work2[:].rearrange(flat), first[:].rearrange(flat),
                                           LOW, work2[:].rearrange(flat), ALU.mult, ALU.add))
            step_of(V.tensor_reduce(v2[:], work2[:].rearrange(by_token), AX.X, ALU.max))
            step_of(V.tensor_tensor(work[:], work2[:], over_experts(v2[:]), ALU.is_equal))
            step_of(V.tensor_tensor(work[:], work[:], preference, ALU.mult))
            step_of(V.tensor_tensor(v2[:], v2[:], v1[:], ALU.subtract))
            step_of(V.tensor_reduce(w_first[:], work[:].rearrange(by_token), AX.X, ALU.max))
            step_of(V.tensor_tensor(second[:], work[:], over_experts(w_first[:]), ALU.is_equal))
            dve.wait_ge(exp_ready, 1)
            step_of(V.tensor_scalar(v1[:], v2[:], 1.0, None, ALU.add))
            step_of(V.reciprocal(w_first[:], v1[:]))
            step_of(V.tensor_tensor(w_second[:], v2[:], w_first[:], ALU.mult))
            step_of(V.tensor_tensor(key[:], first[:], over_experts(w_first[:]), ALU.mult))
            step_of(V.tensor_tensor(work[:], second[:], over_experts(w_second[:]), ALU.mult))
            step_of(V.tensor_tensor(key[:], key[:], work[:], ALU.add))
            step_of(V.tensor_tensor(work[:], first[:], second[:], ALU.add))
            step_of(V.tensor_scalar(work[:], work[:], -1.0, None, ALU.add))
            step_of(V.tensor_tensor(key[:], key[:], work[:], ALU.add))
            V.engine_nop().then_inc(key_ready, 1)
            step_of.beside(V.memset(threshold[:], 0.0))
            for m in range(TRIED):
                step_of.beside(V.memset(digit[:, :, m:m + 1], (m + 1) << (BITS - DIGIT)))
            step_of.beside(V.memset(digit[:, :, TRIED:], 0))
            step_of(V.memset(counts[:, :, TRIED:], float(CAP)))
            for h in range(HALVES):
                dve.wait_ge(key_turned, h + 1)
                step_of(V.tensor_copy(keyT[:, h, :], ps_key[h][:, 0:P]))

            ctx.enter_context(nc.allow_low_precision(reason="counts of at most 128 columns are whole in bf16"))
            with dve.Fori(0, ROUNDS // UNROLLED) as i:
                for j in range(UNROLLED):
                    step_in = Chain(search, i * (STEPS * UNROLLED) + STEPS * j)
                    step_in(V.tensor_tensor(candidate[:], repeated(threshold[:].bitcast(I32), (1, HALVES), (0, TRIED + 1)),
                                           digit[:], ALU.bitwise_or))
                    for m in range(TRIED):
                        for h in range(HALVES):
                            step_in.beside(V.tensor_scalar(
                                (taken, above, ties)[m][:, h, :], keyT[:, h, :], candidate[:, h, m:m + 1].bitcast(F32), 0.0,
                                ALU.is_ge, ALU.add, accum_out=counts[:, h, m:m + 1]))
                    dve.wait_ge(counted, i * UNROLLED + (j + 1))
                    step_in(V.scalar_tensor_tensor(
                        reached[:].rearrange("p h m -> p (h m)"), ps_count[:, 0:HALVES * (TRIED + 1)], float(CAP),
                        candidate[:].bitcast(F32).rearrange("p h m -> p (h m)"), ALU.is_ge, ALU.mult))
                    step_in.beside(V.tensor_scalar(digit[:], digit[:], DIGIT, None, ALU.logical_shift_right))
                    step_in(V.tensor_reduce(threshold[:], reached[:], AX.X, ALU.max))

            for h in range(HALVES):
                limit = threshold[:, h:h + 1]
                step_of.beside(V.tensor_scalar(above[:, h, :], keyT[:, h, :], limit, 0.0, ALU.is_gt, ALU.add,
                                               accum_out=count[:, h:h + 1]))
                step_of.beside(V.tensor_scalar(ties[:, h, :], keyT[:, h, :], limit, 0.0, ALU.is_equal, ALU.add,
                                               accum_out=tie_count[:, h:h + 1]))
            dve.wait_ge(chain, step_of.n)
            V.engine_nop().then_inc(ties_ready, 1)
            dve.wait_ge(consts, 6 + EXPERTS)
            scanned, carry = "p h n -> p (h n)", no_carry[:].rearrange("p h n -> p (h n)")
            step_of.beside(V.tensor_tensor_scan(rank[:].rearrange(scanned), carry, ties[:].rearrange(scanned), 0.0,
                                                ALU.mult, ALU.add))
            dve.wait_ge(ties_summed, 1)
            step_of(V.tensor_scalar(fits[:], ps_count[:, 0:HALVES], -1.0, float(CAP), ALU.mult, ALU.add))
            step_of(V.tensor_tensor(fits[:], fits[:], ps_earlier[:, 0:HALVES], ALU.subtract))
            for h in range(HALVES):
                step_of.beside(V.scalar_tensor_tensor(taken[:, h, :], rank[:, h, :], fits[:, h:h + 1], ties[:, h, :],
                                                      ALU.is_le, ALU.mult))
            dve.wait_ge(chain, step_of.n)
            step_of(V.tensor_tensor(taken[:], taken[:], above[:], ALU.add))
            step_of(V.tensor_reduce(count[:], taken[:], AX.X, ALU.add))
            V.engine_nop().then_inc(taken_ready, 1)
            step_of.beside(V.tensor_tensor_scan(rank[:].rearrange(scanned), carry, taken[:].rearrange(scanned), 0.0,
                                                ALU.mult, ALU.add))
            dve.wait_ge(taken_summed, 1)
            step_of(V.tensor_copy(fits[:], ps_earlier[:, 0:HALVES]))
            for h in range(HALVES):
                step_of(V.scalar_tensor_tensor(ties[:, h, :], rank[:, h, :], fits[:, h:h + 1], taken[:, h, :],
                                               ALU.add, ALU.mult))
            V.engine_nop().then_inc(slot_ready, 1)
            dve.wait_ge(slot_turned, 1)
            step_of(V.tensor_scalar(slot[:].rearrange(flat), ps_slot[:, 0:E * T], -1.0, None, ALU.add))
            step_of(V.tensor_scalar(slot_row[:], slot[:], float(P), None, ALU.is_ge))
            for k in range(2, CT):
                step_of(V.scalar_tensor_tensor(slot_row[:].rearrange(flat), slot[:].rearrange(flat), float(k * P),
                                               slot_row[:].rearrange(flat), ALU.is_ge, ALU.add))
            step_of.beside(V.tensor_copy(row[:], slot_row[:]))
            step_of.beside(V.scalar_tensor_tensor(lane[:].rearrange(flat), slot_row[:].rearrange(flat), -float(P),
                                                  slot[:].rearrange(flat), ALU.mult, ALU.add))

        @block.tensor
        def _(pe):
            def per_expert(matrix, numbers, sums):
                return nc.tensor.matmul(sums[:, 0:numbers.shape[1]], matrix[:], numbers, start=True, stop=True)

            pe.wait_ge(key_ready, 1)
            for h in range(HALVES):
                nc.tensor.transpose(ps_key[h][:, 0:P], key[:, EXPERTS * h:EXPERTS * (h + 1), :].rearrange("p e t -> p (e t)"),
                                    ident[:]).then_inc(key_turned, 1)
            pe.wait_ge(consts, 4 + EXPERTS)
            with pe.Fori(0, ROUNDS // UNROLLED) as i:
                for j in range(UNROLLED):
                    pe.wait_ge(search, i * (STEPS * UNROLLED) + (STEPS * j + 1 + HALVES * TRIED))
                    per_expert(same, counts[:].rearrange("p h m -> p (h m)"), ps_count).then_inc(counted, 1)
            pe.wait_ge(search, ROUNDS * STEPS)
            pe.wait_ge(ties_ready, 1)
            per_expert(same, count[:], ps_count)
            per_expert(earlier, tie_count[:], ps_earlier).then_inc(ties_summed, 1)
            pe.wait_ge(taken_ready, 1)
            per_expert(earlier, count[:], ps_earlier).then_inc(taken_summed, 1)
            pe.wait_ge(slot_ready, 1)
            for h in range(HALVES):
                mm = nc.tensor.transpose(ps_slot[:, P * h:P * (h + 1)], ties[:, h, :], ident[:])
            mm.then_inc(slot_turned, 1)


def experts(nc, io, x, ident, n_rows, sum_rows, weights_in, E, F, FC, T, N, CT, out, gamma, beta, b1, w1, w2,
            minus_half, key, gate_parts, row, lane, lanes, rows_of, numbers, spare):
    HALF = CAP // 2
    PAYLOADS = 6
    ctx = ExitStack()
    with ctx:
        def sb(name, shape, dt=F32):
            return ctx.enter_context(nc.sbuf_tensor("e_" + name, shape, dt))

        def ps(name, shape, dt=F32):
            return ctx.enter_context(nc.psum_tensor("e_ps_" + name, shape, dt))

        def sem(name):
            return ctx.enter_context(nc.semaphore("e_" + name))

        b2 = sb("b2", [P, 2, D])
        xe = [sb(f"xe{i}", [P, CT, D]) for i in range(2)]
        xT = [sb(f"xT{i}", [P, KC, CAP]) for i in range(2)]
        hT = sb("hT", [P, FC, CAP])
        y = [sb(f"y{i}", [P, CT, D]) for i in range(2)]
        biased_y = sb("biased_y", [P, 2, D])
        total = [sb(f"total{i}", [P, NT, D]) for i in range(B)]
        lane_hot = [sb(f"lane_hot{i}", [P, T, P], BF16) for i in range(2)]
        row_hot = [sb(f"row_hot{i}", [P, T, PAYLOADS, CT], BF16) for i in range(2)]
        filled = sb("filled", [P, PAYLOADS, CT])
        index = sb("index", [P, 3, CT])
        place, gate = sb("place", [P, E, CT], I32), sb("gate", [P, E, CT])
        stats, moments = sb("stats", [P, T, 6]), sb("moments", [P, T, 2])
        var_eps, rstd, shift = (sb(n, [P, T]) for n in ("var_eps", "rstd", "shift"))
        ps_t = [ps(f"t{i}", [P, S]) for i in range(2)]
        ps_h = [ps(f"h{i}", [P, 2, S]) for i in range(2)]
        ps_y = [ps(f"y{i}", [P, S]) for i in range(2)]
        ps_slots = ps_t[1]

        added, total_in, stored = sem("added"), [sem(f"total_in{i}") for i in range(B)], [
            sem(f"stored{i}") for i in range(B)]
        lane_ready, row_ready, slots_ready, fill, place_ready = (sem("lane_ready"), sem("row_ready"), sem("slots_ready"),
                                                                 sem("fill"), sem("place_ready"))
        bias_in = [sem(f"bias_in{i}") for i in range(2)]
        gathered = [sem(f"gathered{i}") for i in range(2)]
        turned, xT_ready, h_sum, hT_ready, y_sum, biased, y_ready = (
            sem("turned"), sem("xT_ready"), sem("h_sum"), sem("hT_ready"), sem("y_sum"), sem("biased"), sem("y_ready"))
        stats_ready, moments_ready, var_ready, rstd_ready, done, scaled_by = (
            sem("stats_ready"), sem("moments_ready"), sem("var_ready"), sem("rstd_ready"), sem("done"), sem("scaled_by"))
        weighted, last_done = sem("weighted"), sem("last_done")

        block = ctx.enter_context(nc.Block())

        @block.sync
        def _(sp):
            for e in range(E):
                if e >= 2:
                    sp.wait_ge(y_ready, CT * (e - 1))
                    load_expert(sp, io, e, w1[e % 2], w2[e % 2], weights_in[e % 2])
                    sp.wait_ge(biased, CT * (e - 1))
                sp.dma_start(b2[:, e % 2, :], io["mb2"][e:e + 1, :].to_broadcast([P, D])).then_inc(bias_in[e % 2], 16)
            sp.wait_ge(added, 16 * CT * E)
            for b in range(B):
                sp.dma_start(total[b][:], sum_rows[b * S:(b + 1) * S, :].rearrange("(t p) d -> p t d", p=P)
                             ).then_inc(total_in[b], 16)

        @block.gpsimd
        def _(pool):
            def gather(e):
                if e >= 2:
                    pool.wait_ge(turned, 3 * (e - 1))
                for c in range(CT):
                    nc.gpsimd.indirect_dma_start(
                        out=xe[e % 2][:, c, :], out_offset=None, in_=n_rows,
                        in_offset=bass.IndirectOffsetOnAxis(ap=place[:, e, c:c + 1], axis=0)).then_inc(gathered[e % 2], 16)

            pool.wait_ge(place_ready, 1)
            gather(0)
            pool.wait_ge(place_ready, 2)
            gather(1)
            for e in range(E):
                for c in range(CT):
                    pool.wait_ge(y_ready, CT * e + c + 1)
                    if c == 0 and e > 0:
                        pool.wait_ge(added, 16 * CT * e)
                    nc.gpsimd.indirect_dma_start(
                        out=sum_rows, out_offset=bass.IndirectOffsetOnAxis(ap=place[:, e, c:c + 1], axis=0),
                        in_=y[e % 2][:, c, :], in_offset=None, compute_op=ALU.add).then_inc(added, 16)
                if e + 2 < E:
                    pool.wait_ge(place_ready, e + 3)
                    gather(e + 2)

            def add_x(b):
                pool.wait_ge(weighted, b + 1)
                nc.gpsimd.tensor_tensor(total[b][:], total[b][:], x[:, b * NT:(b + 1) * NT, :], ALU.add
                                        ).then_inc(done, 1)

            for b in range(B):
                of_b = slice(b * NT, (b + 1) * NT)
                pool.wait_ge(var_ready, 2 * (b + 1))
                nc.gpsimd.tensor_tensor(rstd[:, of_b], var_eps[:, of_b], minus_half[:, 0:NT], ALU.pow).then_inc(rstd_ready, 1)
                pool.wait_ge(rstd_ready, 2 * b + 1)
                nc.gpsimd.tensor_tensor(shift[:, of_b], shift[:, of_b], rstd[:, of_b], ALU.mult).then_inc(rstd_ready, 1)
                if b >= 1:
                    add_x(b - 1)

        @block.scalar
        def _(act):
            def turned_in(e):
                for i in range(3):
                    act.wait_ge(turned, 3 * e + i + 1)
                    if i < KC:
                        nc.scalar.copy(xT[e % 2][:, i, 0:S], ps_t[i % 2][:]).then_inc(xT_ready, 1)
                    else:
                        nc.scalar.copy(xT[e % 2][:, :, S:], ps_t[i % 2][:, 0:KC * P].rearrange("p (c n) -> p c n", c=KC)
                                       ).then_inc(xT_ready, 1)

            turned_in(0)
            for e in range(E):
                for f in range(FC):
                    n = FC * e + f
                    act.wait_ge(h_sum, n + 1)
                    if f == 0 and e > 0:
                        act.wait_ge(y_sum, CT * e)
                    nc.scalar.activation(hT[:, f, :].rearrange("p (a n) -> p a n", a=2), ps_h[f % 2][:, :, 0:HALF], ACT.Gelu,
                                         bias=b1[:, e, f:f + 1]).then_inc(hT_ready, 1)
                if e + 1 < E:
                    turned_in(e + 1)

            def store(b):
                act.wait_ge(last_done if b == B - 1 else done, 1 if b == B - 1 else b + 1)
                act.dma_start(out[b].rearrange("(t p) d -> p t d", p=P), total[b][:]
                              ).then_inc(stored[b], 16)

            for b in range(B):
                act.wait_ge(rstd_ready, 2 * (b + 1))
                for t in range(NT):
                    tile = total[b][:, t, :]
                    nc.scalar.activation(tile, tile, ACT.Identity, bias=shift[:, b * NT + t:b * NT + t + 1],
                                         scale=rstd[:, b * NT + t:b * NT + t + 1]).then_inc(scaled_by, 1)
                if b >= 2:
                    store(b - 2)
            store(B - 2)
            store(B - 1)
            for i in range(B):
                act.wait_ge(stored[i], 16)

        @block.vector
        def _(dve):
            V = nc.vector

            def one_hot(e):
                if e >= 2:
                    dve.wait_ge(slots_ready, e - 1)
                lane_e, row_e = lane[:, e, :], row[:, e, :]
                V.tensor_tensor(lane_hot[e % 2][:], repeated(lanes[:], (0, T), (1, P)), repeated(lane_e, (1, T), (0, P)),
                                ALU.is_equal).then_inc(lane_ready, 1)
                hot = row_hot[e % 2]
                V.tensor_tensor(hot[:, :, 0, :], repeated(rows_of[:], (0, T), (1, CT)), repeated(row_e, (1, T), (0, CT)),
                                ALU.is_equal).then_inc(row_ready, 1)
                dve.wait_ge(row_ready, PAYLOADS * e + 1)
                for j in range(1, PAYLOADS):
                    load = numbers[:, j - 1, :] if j < 3 else gate_parts[:, j - 3, e, :]
                    V.tensor_tensor(hot[:, :, j, :], hot[:, :, 0, :], repeated(load, (1, T), (0, CT)), ALU.mult
                                    ).then_inc(row_ready, 1)

            def read_slots(e):
                done = [6 * e]

                def step(ins):
                    done[0] += 1
                    ins.then_inc(fill, 1)
                    dve.wait_ge(fill, done[0])

                dve.wait_ge(slots_ready, e + 1)
                step(V.tensor_copy(filled[:], ps_slots[:, 0:PAYLOADS * CT].rearrange("p (j c) -> p j c", j=PAYLOADS)))
                step(V.tensor_tensor(index[:, 2, :], filled[:, 3, :], filled[:, 4, :], ALU.add))
                step(V.tensor_tensor(gate[:, e, :], index[:, 2, :], filled[:, 5, :], ALU.add))
                step(V.scalar_tensor_tensor(index[:, 0, :], filled[:, 1, :], float(P), filled[:, 2, :], ALU.mult, ALU.add))
                step(V.tensor_tensor(index[:, 1, :], filled[:, 0, :], spare[:], ALU.mult))
                step(V.tensor_tensor(index[:, 1, :], spare[:], index[:, 1, :], ALU.subtract))
                V.tensor_tensor(place[:, e, :], index[:, 0, :], index[:, 1, :], ALU.add).then_inc(place_ready, 1)

            one_hot(0)
            read_slots(0)
            one_hot(1)
            one_hot(2)
            read_slots(1)
            read_slots(2)
            for e in range(E):
                if 1 <= e < E - 2:
                    one_hot(e + 2)
                    read_slots(e + 2)
                for c in range(CT):
                    n = CT * e + c
                    dve.wait_ge(y_sum, n + 1)
                    if c == 0:
                        dve.wait_ge(bias_in[e % 2], 16 * (e // 2 + 1))
                        if e >= 2:
                            dve.wait_ge(added, 16 * CT * (e - 1))
                    if n >= 2:
                        dve.wait_ge(y_ready, n - 1)
                    V.tensor_tensor(biased_y[:, n % 2, :], ps_y[n % 2][:, 0:D], b2[:, e % 2, :], ALU.add).then_inc(biased, 1)
                    dve.wait_ge(biased, n + 1)
                    V.tensor_scalar(y[e % 2][:, c, :], biased_y[:, n % 2, :], gate[:, e, c:c + 1], None, ALU.mult
                                    ).then_inc(y_ready, 1)

            def statistics(b):
                tot = total[b]
                of_b = slice(b * NT, (b + 1) * NT)
                dve.wait_ge(total_in[b], 16)
                for t in range(NT):
                    V.bn_stats(stats[:, b * NT + t, :], tot[:, t, :]).then_inc(stats_ready, 1)
                dve.wait_ge(stats_ready, NT * (b + 1))
                for t in range(NT):
                    V.bn_aggr(moments[:, b * NT + t, :], stats[:, b * NT + t, :]).then_inc(moments_ready, 1)
                dve.wait_ge(moments_ready, NT * (b + 1))
                V.tensor_scalar(var_eps[:, of_b], moments[:, of_b, 1], EPS, None, ALU.add).then_inc(var_ready, 1)
                V.tensor_scalar(shift[:, of_b], moments[:, of_b, 0], -1.0, None, ALU.mult).then_inc(var_ready, 1)

            def times_gamma(b):
                tot = total[b]
                dve.wait_ge(scaled_by, NT * (b + 1))
                V.tensor_tensor(tot[:], tot[:], repeated(gamma[:], (0, NT), (1, D)), ALU.mult).then_inc(weighted, 1)

            for b in range(B):
                statistics(b)
                if b >= 1:
                    times_gamma(b - 1)
            times_gamma(B - 1)
            dve.wait_ge(weighted, B)
            V.tensor_tensor(total[B - 1][:], total[B - 1][:], x[:, (B - 1) * NT:, :], ALU.add).then_inc(last_done, 1)

        @block.tensor
        def _(pe):
            def transposes(e):
                pe.wait_ge(gathered[e % 2], 16 * CT * (e // 2 + 1))
                for i in range(3):
                    if i == 1:
                        pe.wait_ge(fill, 6 * (min(e + 1, E - 1) if e > 0 else 0) + 1)
                    elif i == 2 or e > 0:
                        pe.wait_ge(xT_ready, 3 * e + (1 if i == 2 else 0))
                    if i < KC:
                        for c in range(NT):
                            mm = nc.tensor.transpose(ps_t[i % 2][:, c * P:(c + 1) * P], xe[e % 2][:, c, i * P:(i + 1) * P], ident[:])
                    else:
                        for k in range(KC):
                            mm = nc.tensor.transpose(ps_t[i % 2][:, k * P:(k + 1) * P], xe[e % 2][:, NT, k * P:(k + 1) * P], ident[:])
                    mm.then_inc(turned, 1)

            def slots(e):
                pe.wait_ge(lane_ready, e + 1)
                pe.wait_ge(row_ready, PAYLOADS * (e + 1))
                if e >= 1:
                    pe.wait_ge(fill, 6 * (e - 1) + 1)
                    pe.wait_ge(xT_ready, 3 * max(e - 2, 0) + 2)
                for t in range(T):
                    mm = nc.tensor.matmul(ps_slots[:, 0:PAYLOADS * CT], lane_hot[e % 2][:, t, :],
                                          row_hot[e % 2][:, t].rearrange("p j c -> p (j c)"), start=(t == 0), stop=(t == T - 1))
                mm.then_inc(slots_ready, 1)

            slots(0)
            transposes(0)
            for e in range(E):
                pe.wait_ge(xT_ready, 3 * (e + 1))
                pe.wait_ge(weights_in[e % 2], 32 * (e // 2 + 1))
                for f in range(FC):
                    n = FC * e + f
                    if n >= 2:
                        pe.wait_ge(hT_ready, n - 1)
                    for half in range(2):
                        for c in range(KC):
                            mm = nc.tensor.matmul(ps_h[f % 2][:, half, 0:HALF], w1[e % 2][:, c, f * P:(f + 1) * P],
                                                  xT[e % 2][:, c, half * HALF:(half + 1) * HALF], start=(c == 0), stop=(c == KC - 1))
                    mm.then_inc(h_sum, 1)
                    if e == 0 and f == FC // 2:
                        slots(1)
                if e + 2 < E:
                    slots(e + 2)
                if e + 1 < E:
                    transposes(e + 1)
                pe.wait_ge(hT_ready, FC * (e + 1))
                for c in range(CT):
                    n = CT * e + c
                    if n >= 2:
                        pe.wait_ge(biased, n - 1)
                    for f in range(FC):
                        mm = nc.tensor.matmul(ps_y[n % 2][:, 0:D], hT[:, f, c * P:(c + 1) * P], w2[e % 2][:, f, :],
                                              start=(f == 0), stop=(f == FC - 1))
                    mm.then_inc(y_sum, 1)


def program(nc, io, out):
    ctx = ExitStack()
    with ctx:
        x = ctx.enter_context(nc.sbuf_tensor("x_sb", [P, B * NT, D], F32))
        ident = ctx.enter_context(nc.sbuf_tensor("ident", [P, P], F32))
        identb = ctx.enter_context(nc.sbuf_tensor("identb", [P, P], BF16))
        logits = ctx.enter_context(nc.sbuf_tensor("logits", [P, NE, B * NT], F32))
        n_rows = nc.dram_tensor("n_rows", [B * S + SPARE, D], F32, kind="Internal").ap()
        sum_rows = nc.dram_tensor("sum_rows", [B * S + SPARE, D], F32, kind="Internal").ap()
        ident_set = ctx.enter_context(nc.semaphore("ident_set"))
        with nc.Block() as block:
            @block.gpsimd
            def _(pool):
                nc.gpsimd.memset(ident[:], 0.0).then_inc(ident_set, 1)
                pool.wait_ge(ident_set, 1)
                nc.gpsimd.affine_select(out=ident[:], in_=ident[:], compare_op=ALU.not_equal, fill=1.0, base=0,
                                        pattern=[[-1, P]], channel_multiplier=1).then_inc(ident_set, 1)
                pool.wait_ge(ident_set, 2)
                nc.gpsimd.tensor_copy(identb[:], ident[:]).then_inc(ident_set, 1)
        spent = softmax_attention(nc, io, x, ident, identb)
        with ExitStack() as until_attention:
            operands = SigmoidOperands(nc, until_attention)
            expert_per_batch(nc, io, x, ident, spent, operands)
            sigmoid_attention(nc, io, x, ident, operands, logits, n_rows, sum_rows)
        mixture(nc, io, x, ident, logits, n_rows, sum_rows, out)


def laid_out(inputs):
    a = {k: np.asarray(v) for k, v in inputs.items()}
    order = np.arange(D).reshape(KC, HC, HD).transpose(0, 2, 1).reshape(D)
    cols = lambda v: v.reshape(KC, P).T
    m = {
        "x": a["x"],
        "ctxT": a["ctx_1024"].transpose(0, 2, 1),
        "mask": a["mask_BxS2_bf1"].view(np.uint8),
        "wq": a["L0_xattn_Wq"][order].T, "wk": a["L0_xattn_Wk"][order].T,
        "wv": a["L0_xattn_Wv"].T, "wo": a["L0_xattn_Wo"].T,
        "bq": cols(a["L0_xattn_bq"][order]), "bk": cols(a["L0_xattn_bk"][order]), "bv": cols(a["L0_xattn_bv"]),
        "bo": a["L0_xattn_bo"].reshape(1, D),
        "pw1": a["L0_ffn_Wp1"], "pb1": a["L0_ffn_bp1"].reshape(P, 1), "pw2": a["L0_ffn_Wp2"],
        "pb2": a["L0_ffn_bp2"].reshape(1, -1),
        "fw1": a["L0_ffn_W1"], "fb1": a["L0_ffn_b1"].reshape(8, 4, P).transpose(0, 2, 1),
        "fw2": a["L0_ffn_W2"], "fb2": a["L0_ffn_b2"].reshape(8, KC, P).transpose(0, 2, 1),
        "fwo": a["L0_ffn_Wo"], "fbo": a["L0_ffn_bo"].reshape(1, D),
        "swq": a["L1_xattn_Wq"][order].T, "swk": a["L1_xattn_Wk"][order].T, "swv": a["L1_xattn_Wv"].T,
        "swp": a["L1_xattn_Wp"].T,
        "sgq": a["L1_xattn_gq"].repeat(HC).reshape(P, 1), "sbq": a["L1_xattn_bq"].repeat(HC).reshape(P, 1),
        "sgk": a["L1_xattn_gk"].repeat(HC).reshape(P, 1), "sbk": a["L1_xattn_bk"].repeat(HC).reshape(P, 1),
        "sbp": a["L1_xattn_bp"].reshape(1, D),
        "mwr": a["L1_ffn_Wr"], "mbr": a["L1_ffn_br"].reshape(1, -1),
        "mw1": a["L1_ffn_W1"], "mb1": a["L1_ffn_b1"].reshape(8, 8, P).transpose(0, 2, 1),
        "mw2": a["L1_ffn_W2"], "mb2": a["L1_ffn_b2"],
        "mgamma": a["L1_ffn_gamma"].reshape(1, D), "mbeta": a["L1_ffn_beta"].reshape(1, D),
    }
    return {k: np.ascontiguousarray(v) for k, v in m.items()}


def kernel(**inputs):
    import concourse.bacc as bacc
    from concourse.bass_utils import run_bass_kernel_spmd

    arrays = laid_out(inputs)
    nc = bacc.Bacc("TRN2", target_bir_lowering=False, num_devices=1)
    io = {k: nc.dram_tensor(k, v.shape, mybir.dt.from_np(v.dtype), kind="ExternalInput").ap() for k, v in arrays.items()}
    out = nc.dram_tensor("out", (B, S, D), F32, kind="ExternalOutput").ap()
    program(nc, io, out)
    r = run_bass_kernel_spmd(nc, [arrays], core_ids=[0])
    return r.results[0]["out"]
```
